# Optimizing a Trainium2 kernel written in Bass

```python
import numpy as np
import jax
import jax.numpy as jnp

def _softmax(x, axis=-1):
    return jax.nn.softmax(x, axis=axis)

def _gelu(x):
    return jax.nn.gelu(x, approximate=True)

def _silu(x):
    return jax.nn.silu(x)

def _sigmoid(x):
    return jax.nn.sigmoid(x)

def _layernorm(x, axis=-1, eps=1e-05):
    m = jnp.mean(x, axis=axis, keepdims=True)
    v = jnp.var(x, axis=axis, keepdims=True)
    return (x - m) / jnp.sqrt(v + eps)

def _scatter_add(tgt, idx, src, axis=0):
    return tgt.at[idx].add(src)

def _segment_sum(src, seg, n):
    return jax.ops.segment_sum(src, seg, n)
kernel_name = 'mk_decoder_postln_d1_seqx_r8_aaf5fc'

def setup_inputs(seed: int=0):
    np.random.seed(seed)
    _w = jnp.asarray

    def _rec_inputs():
        import jax
        import jax.numpy as jnp
        _rk = jax.random.key(seed)
        x = 7.22e-05 + 1 * jax.random.normal(jax.random.fold_in(_rk, 1), (8, 128, 256), jnp.float32)
        _lenS = 128 - jax.random.randint(jax.random.fold_in(_rk, 7), (8,), 0, max(1, 128 // 4) + 1, jnp.int32)
        _lenS2 = 128 - jax.random.randint(jax.random.fold_in(_rk, 8), (8,), 0, max(1, 128 // 4) + 1, jnp.int32)
        _ctx_2048P = jax.random.normal(jax.random.fold_in(_rk, 11), (8, 16, 256), jnp.float32)
        _ctx_2048c = jax.random.dirichlet(jax.random.fold_in(_rk, 511), 0.3 * jnp.ones((16,), jnp.float32), (8, 128))
        _ctx_2048t = jnp.einsum('bsk,bkd->bsd', _ctx_2048c, _ctx_2048P)
        _ctx_2048t = _ctx_2048t * jax.lax.rsqrt(jnp.mean(jnp.square(_ctx_2048t)) + 1e-12) * 0.953939
        ctx_2048 = -0.000514642 + 1.00011 * (_ctx_2048t + 0.3 * jax.random.normal(jax.random.fold_in(_rk, 611), (8, 128, 256), jnp.float32))
        return (x, ctx_2048)
    x, ctx_2048 = _rec_inputs()

    def _L0_attn_setup():
        import jax, jax.numpy as jnp
        import numpy as np
        from functools import partial
        BATCH, SEQ = (2, 256)
        D_MODEL, D_INNER, D_XB = (256, 512, 128)
        HEADDIM, D_STATE = (64, 64)
        NHEADS = D_INNER // HEADDIM
        NKV = D_XB // HEADDIM
        REP = NHEADS // NKV
        INTER = 1024
        EPS = 1e-05
        D_IN_PROJ = D_INNER + D_XB + D_XB + D_INNER + NHEADS

        def _layernorm(x, w, b):
            mu = x.mean(-1, keepdims=True)
            var = ((x - mu) ** 2).mean(-1, keepdims=True)
            return (x - mu) * jax.lax.rsqrt(var + EPS) * w + b

        def _ssd_scan(xh, dt, A, Bh, Ch):
            dA = jnp.exp(dt * A)
            to_l = lambda t: jnp.moveaxis(t, 1, 0)

            def step(state, inp):
                dA_t, dt_t, x_t, B_t, C_t = inp
                state = state * dA_t[:, :, None, None] + jnp.einsum('bh,bhp,bhn->bhpn', dt_t, x_t, B_t)
                y = jnp.einsum('bhpn,bhn->bhp', state, C_t)
                return (state, y)
            state0 = jnp.zeros((xh.shape[0], NHEADS, HEADDIM, D_STATE), xh.dtype)
            _, ys = jax.lax.scan(step, state0, (to_l(dA), to_l(dt), to_l(xh), to_l(Bh), to_l(Ch)))
            return jnp.moveaxis(ys, 0, 1)
        key = jax.random.key(seed)
        ks = jax.random.split(key, 8)
        g = lambda k, shape, s: jax.random.normal(k, shape, jnp.float32) * s
        return {'hidden_states': g(ks[0], (BATCH, SEQ, D_MODEL), 1.0), 'ln_w': jnp.ones((D_MODEL,), jnp.float32), 'ln_b': jnp.zeros((D_MODEL,), jnp.float32), 'in_proj_w': g(ks[1], (D_IN_PROJ, D_MODEL), 0.02), 'dt_bias': jax.random.uniform(ks[2], (NHEADS,), jnp.float32, -4.0, 0.0), 'A_log': jnp.log(jnp.arange(1, NHEADS + 1, dtype=jnp.float32)), 'Dp': jnp.ones((NHEADS,), jnp.float32), 'norm_w': jnp.ones((D_INNER,), jnp.float32), 'out_proj_w': g(ks[3], (D_MODEL, D_INNER), 0.02), 'fc1_w': g(ks[4], (INTER, D_MODEL), 0.02), 'fc1_b': jnp.zeros((INTER,), jnp.float32), 'fc2_w': g(ks[5], (D_MODEL, INTER), 0.02), 'fc2_b': jnp.zeros((D_MODEL,), jnp.float32)}
    _L0_attn_all = _L0_attn_setup()
    _L0_attn_in = {k: v for k, v in _L0_attn_all.items() if k in ('ln_w', 'ln_b', 'in_proj_w', 'dt_bias', 'A_log', 'Dp', 'norm_w', 'out_proj_w', 'fc1_w', 'fc1_b', 'fc2_w', 'fc2_b')}
    del _L0_attn_all

    def _L0_xattn_setup():
        import jax, jax.numpy as jnp
        import numpy as np
        HIDDEN = 256
        NUM_HEADS = 16
        NUM_KV_HEADS = 4
        HEAD_DIM = 128
        ROPE_THETA = 10000.0
        EPS = 1e-06

        def rms_norm(x, w, eps=EPS):
            var = jnp.mean(jnp.square(x), axis=-1, keepdims=True)
            return x * jax.lax.rsqrt(var + eps) * w

        def rope_cache(L, head_dim, theta, dtype):
            inv_freq = 1.0 / theta ** (jnp.arange(0, head_dim, 2, dtype=jnp.float32) / head_dim)
            t = jnp.arange(L, dtype=jnp.float32)
            freqs = jnp.outer(t, inv_freq)
            emb = jnp.concatenate([freqs, freqs], -1)
            cos = jnp.cos(emb).astype(dtype)[None, :, None, :]
            sin = jnp.sin(emb).astype(dtype)[None, :, None, :]
            return (cos, sin)

        def rotate_half(x):
            x1, x2 = jnp.split(x, 2, axis=-1)
            return jnp.concatenate([-x2, x1], axis=-1)
        key = jax.random.key(seed)
        ks = jax.random.split(key, 10)
        B, L, T = (2, 256, 64)
        q_out = NUM_HEADS * HEAD_DIM
        kv_out = NUM_KV_HEADS * HEAD_DIM
        s = lambda fan_in: 1.0 / np.sqrt(fan_in)
        return {'x': jax.random.normal(ks[0], (B, L, HIDDEN), jnp.float32), 'h_ctx_kv': jax.random.normal(ks[1], (B, T, HIDDEN), jnp.float32), 'wq': jax.random.normal(ks[2], (HIDDEN, q_out), jnp.float32) * s(HIDDEN), 'wk': jax.random.normal(ks[3], (HIDDEN, kv_out), jnp.float32) * s(HIDDEN), 'wv': jax.random.normal(ks[4], (HIDDEN, kv_out), jnp.float32) * s(HIDDEN), 'wo': jax.random.normal(ks[5], (q_out, HIDDEN), jnp.float32) * s(q_out), 'wk_ctx': jax.random.normal(ks[6], (HIDDEN, kv_out), jnp.float32) * s(HIDDEN), 'wv_ctx': jax.random.normal(ks[7], (HIDDEN, kv_out), jnp.float32) * s(HIDDEN), 'q_norm_w': jnp.ones((HEAD_DIM,), jnp.float32), 'k_norm_w': jnp.ones((HEAD_DIM,), jnp.float32)}
    _L0_xattn_all = _L0_xattn_setup()
    _L0_xattn_in = {k: v for k, v in _L0_xattn_all.items() if k in ('wq', 'wk', 'wv', 'wo', 'wk_ctx', 'wv_ctx', 'q_norm_w', 'k_norm_w')}
    del _L0_xattn_all

    def _L0_ffn_setup():
        import jax, jax.numpy as jnp
        import numpy as np
        E, TOPK, H, I, NSH = (8, 2, 256, 640, 2)
        B, S = (2, 128)
        key = jax.random.key(seed)
        ks = jax.random.split(key, 8)
        sc = 0.02
        return {'x': jax.random.normal(ks[0], (B, S, H), dtype=jnp.float32), 'w_router': jax.random.normal(ks[1], (E, H), dtype=jnp.float32), 'wg': jax.random.normal(ks[2], (E, I, H), dtype=jnp.float32) * sc, 'wu': jax.random.normal(ks[3], (E, I, H), dtype=jnp.float32) * sc, 'wd': jax.random.normal(ks[4], (E, H, I), dtype=jnp.float32) * sc, 'sg': jax.random.normal(ks[5], (NSH, I, H), dtype=jnp.float32) * sc, 'su': jax.random.normal(ks[6], (NSH, I, H), dtype=jnp.float32) * sc, 'sd': jax.random.normal(ks[7], (NSH, H, I), dtype=jnp.float32) * sc}
    _L0_ffn_all = _L0_ffn_setup()
    _L0_ffn_in = {k: v for k, v in _L0_ffn_all.items() if k in ('w_router', 'wg', 'wu', 'wd', 'sg', 'su', 'sd')}
    del _L0_ffn_all
    return {'x': x, 'ctx_2048': ctx_2048, 'L0_attn_ln_w': _L0_attn_in['ln_w'], 'L0_attn_ln_b': _L0_attn_in['ln_b'], 'L0_attn_in_proj_w': _L0_attn_in['in_proj_w'], 'L0_attn_dt_bias': _L0_attn_in['dt_bias'], 'L0_attn_A_log': _L0_attn_in['A_log'], 'L0_attn_Dp': _L0_attn_in['Dp'], 'L0_attn_norm_w': _L0_attn_in['norm_w'], 'L0_attn_out_proj_w': _L0_attn_in['out_proj_w'], 'L0_attn_fc1_w': _L0_attn_in['fc1_w'], 'L0_attn_fc1_b': _L0_attn_in['fc1_b'], 'L0_attn_fc2_w': _L0_attn_in['fc2_w'], 'L0_attn_fc2_b': _L0_attn_in['fc2_b'], 'L0_xattn_wq': _L0_xattn_in['wq'], 'L0_xattn_wk': _L0_xattn_in['wk'], 'L0_xattn_wv': _L0_xattn_in['wv'], 'L0_xattn_wo': _L0_xattn_in['wo'], 'L0_xattn_wk_ctx': _L0_xattn_in['wk_ctx'], 'L0_xattn_wv_ctx': _L0_xattn_in['wv_ctx'], 'L0_xattn_q_norm_w': _L0_xattn_in['q_norm_w'], 'L0_xattn_k_norm_w': _L0_xattn_in['k_norm_w'], 'L0_ffn_w_router': _L0_ffn_in['w_router'], 'L0_ffn_wg': _L0_ffn_in['wg'], 'L0_ffn_wu': _L0_ffn_in['wu'], 'L0_ffn_wd': _L0_ffn_in['wd'], 'L0_ffn_sg': _L0_ffn_in['sg'], 'L0_ffn_su': _L0_ffn_in['su'], 'L0_ffn_sd': _L0_ffn_in['sd']}

def reference(x, ctx_2048, L0_attn_ln_w, L0_attn_ln_b, L0_attn_in_proj_w, L0_attn_dt_bias, L0_attn_A_log, L0_attn_Dp, L0_attn_norm_w, L0_attn_out_proj_w, L0_attn_fc1_w, L0_attn_fc1_b, L0_attn_fc2_w, L0_attn_fc2_b, L0_xattn_wq, L0_xattn_wk, L0_xattn_wv, L0_xattn_wo, L0_xattn_wk_ctx, L0_xattn_wv_ctx, L0_xattn_q_norm_w, L0_xattn_k_norm_w, L0_ffn_w_router, L0_ffn_wg, L0_ffn_wu, L0_ffn_wd, L0_ffn_sg, L0_ffn_su, L0_ffn_sd):
    import jax
    import jax.numpy as jnp

    def _L0_attn_ref(hidden_states, ln_w, ln_b, in_proj_w, dt_bias, A_log, Dp, norm_w, out_proj_w, fc1_w, fc1_b, fc2_w, fc2_b):
        import jax, jax.numpy as jnp
        import numpy as np
        from functools import partial
        BATCH, SEQ = (2, 256)
        D_MODEL, D_INNER, D_XB = (256, 512, 128)
        HEADDIM, D_STATE = (64, 64)
        NHEADS = D_INNER // HEADDIM
        NKV = D_XB // HEADDIM
        REP = NHEADS // NKV
        INTER = 1024
        EPS = 1e-05
        D_IN_PROJ = D_INNER + D_XB + D_XB + D_INNER + NHEADS

        def _layernorm(x, w, b):
            mu = x.mean(-1, keepdims=True)
            var = ((x - mu) ** 2).mean(-1, keepdims=True)
            return (x - mu) * jax.lax.rsqrt(var + EPS) * w + b

        def _ssd_scan(xh, dt, A, Bh, Ch):
            dA = jnp.exp(dt * A)
            to_l = lambda t: jnp.moveaxis(t, 1, 0)

            def step(state, inp):
                dA_t, dt_t, x_t, B_t, C_t = inp
                state = state * dA_t[:, :, None, None] + jnp.einsum('bh,bhp,bhn->bhpn', dt_t, x_t, B_t)
                y = jnp.einsum('bhpn,bhn->bhp', state, C_t)
                return (state, y)
            state0 = jnp.zeros((xh.shape[0], NHEADS, HEADDIM, D_STATE), xh.dtype)
            _, ys = jax.lax.scan(step, state0, (to_l(dA), to_l(dt), to_l(xh), to_l(Bh), to_l(Ch)))
            return jnp.moveaxis(ys, 0, 1)
        residual = hidden_states
        h = _layernorm(hidden_states, ln_w, ln_b)
        zxbcdt = h @ in_proj_w.T
        z, x, Bm, Cm, dt = jnp.split(zxbcdt, np.cumsum([D_INNER, D_XB, D_XB, D_INNER]).tolist(), axis=-1)
        b, l = (h.shape[0], h.shape[1])
        dt = jax.nn.softplus(dt + dt_bias)
        A = -jnp.exp(A_log)
        xh = jnp.repeat(x.reshape(b, l, NKV, HEADDIM), REP, axis=2)
        Bh = jnp.repeat(Bm.reshape(b, l, NKV, D_STATE), REP, axis=2)
        Ch = Cm.reshape(b, l, NHEADS, D_STATE)
        y = _ssd_scan(xh, dt, A, Bh, Ch) + Dp[None, None, :, None] * xh
        yf = y.reshape(b, l, D_INNER)
        yf = yf * jax.nn.silu(z)
        yf = yf * jax.lax.rsqrt((yf * yf).mean(-1, keepdims=True) + EPS) * norm_w
        mamba_out = yf @ out_proj_w.T
        mlp = jax.nn.gelu(h @ fc1_w.T + fc1_b, approximate=True) @ fc2_w.T + fc2_b
        return mamba_out + mlp + residual

    def _L0_xattn_ref(x, h_ctx_kv, wq, wk, wv, wo, wk_ctx, wv_ctx, q_norm_w, k_norm_w):
        import jax, jax.numpy as jnp
        import numpy as np
        HIDDEN = 256
        NUM_HEADS = 16
        NUM_KV_HEADS = 4
        HEAD_DIM = 128
        ROPE_THETA = 10000.0
        EPS = 1e-06

        def rms_norm(x, w, eps=EPS):
            var = jnp.mean(jnp.square(x), axis=-1, keepdims=True)
            return x * jax.lax.rsqrt(var + eps) * w

        def rope_cache(L, head_dim, theta, dtype):
            inv_freq = 1.0 / theta ** (jnp.arange(0, head_dim, 2, dtype=jnp.float32) / head_dim)
            t = jnp.arange(L, dtype=jnp.float32)
            freqs = jnp.outer(t, inv_freq)
            emb = jnp.concatenate([freqs, freqs], -1)
            cos = jnp.cos(emb).astype(dtype)[None, :, None, :]
            sin = jnp.sin(emb).astype(dtype)[None, :, None, :]
            return (cos, sin)

        def rotate_half(x):
            x1, x2 = jnp.split(x, 2, axis=-1)
            return jnp.concatenate([-x2, x1], axis=-1)
        B, L, _ = x.shape
        T = h_ctx_kv.shape[1]
        rep = NUM_HEADS // NUM_KV_HEADS
        q = (x @ wq).reshape(B, L, NUM_HEADS, HEAD_DIM)
        k = (x @ wk).reshape(B, L, NUM_KV_HEADS, HEAD_DIM)
        v = (x @ wv).reshape(B, L, NUM_KV_HEADS, HEAD_DIM)
        q = rms_norm(q, q_norm_w)
        k = rms_norm(k, k_norm_w)
        k_ctx = (h_ctx_kv @ wk_ctx).reshape(B, T, NUM_KV_HEADS, HEAD_DIM)
        v_ctx = (h_ctx_kv @ wv_ctx).reshape(B, T, NUM_KV_HEADS, HEAD_DIM)
        k_ctx = rms_norm(k_ctx, k_norm_w)
        cos, sin = rope_cache(L, HEAD_DIM, ROPE_THETA, x.dtype)
        q = q * cos + rotate_half(q) * sin
        k = k * cos + rotate_half(k) * sin
        k_full = jnp.concatenate([k_ctx, k], axis=1)
        v_full = jnp.concatenate([v_ctx, v], axis=1)
        k_full = jnp.repeat(k_full, rep, axis=2)
        v_full = jnpp_repeat = jnp.repeat(v_full, rep, axis=2)
        i = jnp.arange(L)[:, None]
        j = jnp.arange(L)[None, :]
        causal = jnp.where(j > i, -jnp.inf, 0.0).astype(x.dtype)
        mask = jnp.concatenate([jnp.zeros((L, T), x.dtype), causal], axis=1)
        scale = 1.0 / np.sqrt(HEAD_DIM)
        scores = jnp.einsum('blhd,bmhd->bhlm', q, k_full) * scale + mask
        probs = jax.nn.softmax(scores, axis=-1)
        out = jnp.einsum('bhlm,bmhd->blhd', probs, v_full)
        out = out.reshape(B, L, NUM_HEADS * HEAD_DIM)
        return out @ wo

    def _L0_ffn_ref(x, w_router, wg, wu, wd, sg, su, sd):
        import jax, jax.numpy as jnp
        import numpy as np
        E, TOPK, H, I, NSH = (8, 2, 256, 640, 2)
        B, S = (2, 128)
        b, s, h = x.shape
        xt = x.reshape(-1, h)
        T = xt.shape[0]
        logits = jnp.einsum('th,eh->te', xt.astype(jnp.float32), w_router.astype(jnp.float32))
        scores = jax.nn.sigmoid(logits)
        topk_w, topk_i = jax.lax.top_k(scores, TOPK)
        topk_w = topk_w / jnp.sum(topk_w, axis=-1, keepdims=True)
        comb = jnp.zeros((T, E), dtype=xt.dtype)
        comb = comb.at[jnp.arange(T)[:, None], topk_i].add(topk_w.astype(xt.dtype))
        gate = jax.nn.silu(jnp.einsum('th,eih->tei', xt, wg))
        up = jnp.einsum('th,eih->tei', xt, wu)
        expert_out = jnp.einsum('tei,ehi->teh', gate * up, wd)
        out = jnp.einsum('te,teh->th', comb, expert_out)
        sgate = jax.nn.silu(jnp.einsum('th,jih->tji', xt, sg))
        sup = jnp.einsum('th,jih->tji', xt, su)
        out = out + jnp.einsum('tji,jhi->th', sgate * sup, sd)
        return out.reshape(b, s, h)
    x = _layernorm(x + _L0_attn_ref(x, L0_attn_ln_w, L0_attn_ln_b, L0_attn_in_proj_w, L0_attn_dt_bias, L0_attn_A_log, L0_attn_Dp, L0_attn_norm_w, L0_attn_out_proj_w, L0_attn_fc1_w, L0_attn_fc1_b, L0_attn_fc2_w, L0_attn_fc2_b), axis=-1)
    x = _layernorm(x + _L0_xattn_ref(x, ctx_2048, L0_xattn_wq, L0_xattn_wk, L0_xattn_wv, L0_xattn_wo, L0_xattn_wk_ctx, L0_xattn_wv_ctx, L0_xattn_q_norm_w, L0_xattn_k_norm_w), axis=-1)
    x = _layernorm(x + _L0_ffn_ref(x, L0_ffn_w_router, L0_ffn_wg, L0_ffn_wu, L0_ffn_wd, L0_ffn_sg, L0_ffn_su, L0_ffn_sd), axis=-1)
    return x

_drawn_inputs = setup_inputs


def setup_inputs(seed=0):
    import zlib

    import numpy as np

    out = dict(_drawn_inputs(seed))
    spreads = {'L0_attn_ln_w': (1.0, 0.2),
     'L0_attn_ln_b': (0.0, 0.1),
     'L0_attn_Dp': (1.0, 0.2),
     'L0_attn_norm_w': (1.0, 0.2),
     'L0_attn_fc1_b': (0.0, 0.485),
     'L0_attn_fc2_b': (0.0, 0.1),
     'L0_xattn_q_norm_w': (1.0, 0.2),
     'L0_xattn_k_norm_w': (1.0, 0.2)}
    factors = {'L0_ffn_w_router': 3.427, 'L0_ffn_wg': 3.011, 'L0_ffn_wu': 2.976, 'L0_ffn_wd': 2.974}
    for name, (base, spread) in spreads.items():
        noise = np.random.default_rng([zlib.crc32(name.encode()), seed]).standard_normal(out[name].shape)
        drawn = base * np.exp(spread * noise) if base else spread * noise
        out[name] = jnp.asarray(drawn.astype(out[name].dtype))
    for name, factor in factors.items():
        out[name] = (out[name] * factor).astype(out[name].dtype)
    return out
```

```python
from contextlib import ExitStack

import numpy as np

import concourse.bass as bass
from concourse import mybir

ALU = mybir.AluOpType
ACT = mybir.ActivationFunctionType
AX_X = mybir.AxisListType.X
F32 = mybir.dt.float32
F32R = mybir.dt.float32r

P = 128
BATCH, SEQ, DM = 8, 128, 256
TOK = BATCH * SEQ
KT = DM // P
HALF = 512

D_IN, HD, NH, NG = 512, 64, 8, 2
REP = NH // NG
PAIRS = NH // 2
INTER = 1024
IT1 = INTER // P
LN_EPS = 1e-5

AH, KVH, AD = 16, 4, 128
AREP = AH // KVH
MT = 2
RMS_EPS = 1e-6

E, NSH, FI = 8, 2, 640
NE = E + NSH
IT = FI // P

Z0, C0, B0, X0, DT0 = 0, 512, 1024, 1280, 1536
WIN = 1664
Z_T, C_T, B_T, X_T = 4, 4, 2, 2


def products(pe, out, lhs, rhs, first, last):
    (lh, ll), (rh, rl) = lhs, rhs
    pe.matmul(out, lh, rh, start=first, stop=False)
    pe.matmul(out, lh, rl, start=False, stop=False)
    return pe.matmul(out, ll, rh, start=False, stop=last)


def met(eng, sem):
    eng.wait_ge(sem, 1)


def counter(eng, name, first):
    turn = eng.alloc_register(name)
    eng.reg_mov(turn, first)
    return turn


def wait_turn(eng, sem, turn, step=1):
    eng.wait_ge(sem, turn)
    eng.reg_add(turn, turn, step)


def decoder_layer(nc, a, out):
    with ExitStack() as whole:
        dram = lambda name: a[name]

        def scope(ctx):
            sb = lambda name, shape, dt=F32: ctx.enter_context(nc.sbuf_tensor(name, shape, dt))
            ps = lambda name, shape: ctx.enter_context(nc.psum_tensor(name, shape, F32))
            given = []

            def sem(name):
                given.append(nc.alloc_semaphore(name=name))
                return given[-1]

            def give_back():
                if given:
                    nc.clear_and_free_semaphores(given)
                    nc.all_engine_barrier()

            ctx.callback(give_back)
            return sb, ps, sem

        sb, ps, sem = scope(whole)
        ident = sb("ident", [P, P])
        x_tok = sb("x_tok", [P, BATCH, DM])
        acc = sb("acc", [P, BATCH, DM])
        s_const = sem("s_const")
        s_x = sem("s_x")

        state_space_layer(nc, a, scope, ident, x_tok, acc, s_const, s_x)
        cross_attention(nc, a, scope, ident, x_tok)
        experts(nc, a, scope, ident, x_tok, out)


def state_space_layer(nc, a, scope, ident, x_tok, acc, s_const, s_x):
    with ExitStack() as layer:
        sb, ps, sem = scope(layer)
        h_hi = sb("h_hi", [P, KT, TOK], F32R)
        h_lo = sb("h_lo", [P, KT, TOK], F32R)
        win_hi = sb("win_hi", [P, KT, WIN], F32R)
        win_lo = sb("win_lo", [P, KT, WIN], F32R)
        dt = sb("dt", [P, BATCH, NH])
        dta = sb("dta", [P, BATCH, NH])
        wout = sb("wout", [P, PAIRS, DM])
        d_col = sb("d_col", [P, PAIRS])
        nw_col = sb("nw_col", [P, PAIRS])
        upper = sb("upper", [P, P])
        lower = sb("lower", [P, P])
        s_wout = sem("s_wout")

        with ExitStack() as part:
            sb, ps, sem = scope(part)
            win_raw = sb("win_raw", [P, KT, WIN])
            fc1_raw = sb("fc1_raw", [P, KT, INTER])
            fc2_raw = sb("fc2_raw", [P, IT1, DM])
            fc1_hi = sb("fc1_hi", [P, KT, INTER], F32R)
            fc1_lo = sb("fc1_lo", [P, KT, INTER], F32R)
            fc2_hi = sb("fc2_hi", [P, IT1, DM], F32R)
            fc2_lo = sb("fc2_lo", [P, IT1, DM], F32R)
            g_f = sb("g_f", [P, 2, HALF])
            g_hi = sb("g_hi", [P, IT1, HALF], F32R)
            g_lo = sb("g_lo", [P, IT1, HALF], F32R)
            stats = sb("stats", [P, BATCH, 6])
            mv = sb("mv", [P, BATCH, 2])
            veps = sb("veps", [P, BATCH])
            rstd = sb("rstd", [P, BATCH])
            mhalf = sb("mhalf", [P, BATCH])
            xhat = sb("xhat", [P, BATCH, DM])
            h_f = sb("h_f", [P, KT, TOK])
            x2b = sb("x2b", [P, BATCH, DM])
            fc2_bias = sb("fc2_bias", [P, DM])
            lnw = sb("lnw", [P, KT])
            lnb = sb("lnb", [P, KT])
            fc1b = sb("fc1b", [P, IT1])
            dtb = sb("dtb", [NH, 1])
            alog = sb("alog", [P, BATCH, NH])
            dt_row = sb("dt_row", [NH, TOK])
            sp_x = sb("sp_x", [P, BATCH, NH])
            sp_abs = sb("sp_abs", [P, BATCH, NH])
            sp_e = sb("sp_e", [P, BATCH, NH])
            sp_u = sb("sp_u", [P, BATCH, NH])
            sp_ln = sb("sp_ln", [P, BATCH, NH])
            sp_d = sb("sp_d", [P, BATCH, NH])
            sp_r = sb("sp_r", [P, BATCH, NH])
            sp_t = sb("sp_t", [P, BATCH, NH])
            sp_s = sb("sp_s", [P, BATCH, NH])
            ea = sb("ea", [P, BATCH, NH])
            bank = [ps(f"bank{i}", [P, 512]) for i in range(8)]

            s_small = sem("s_small")
            s_fc1 = sem("s_fc1")
            s_fc2 = sem("s_fc2")
            s_win = sem("s_win")
            s_fc2b = sem("s_fc2b")
            stats_ready = sem("stats_ready")
            mv_ready = sem("mv_ready")
            veps_ready = sem("veps_ready")
            mhalf_ready = sem("mhalf_ready")
            rstd_ready = sem("rstd_ready")
            xhat_ready = sem("xhat_ready")
            hT_ready = sem("hT_ready")
            hf_ready = sem("hf_ready")
            hhi_ready = sem("hhi_ready")
            hlo_ready = sem("hlo_ready")
            fc1hi_ready = sem("fc1hi_ready")
            fc1lo_ready = sem("fc1lo_ready")
            fc2hi_ready = sem("fc2hi_ready")
            fc2lo_ready = sem("fc2lo_ready")
            winhi_ready = sem("winhi_ready")
            winlo_ready = sem("winlo_ready")
            dtp_ready = sem("dtp_ready")
            dtrow_ready = sem("dtrow_ready")
            dtT_ready = sem("dtT_ready")
            sp = sem("sp")
            spa = sem("spa")
            dta_ready = sem("dta_ready")
            x2b_ready = sem("x2b_ready")
            x2_ready = sem("x2_ready")
            fc1_done = sem("fc1_done")
            gf_ready = sem("gf_ready")
            ghi_ready = sem("ghi_ready")
            glo_ready = sem("glo_ready")
            fc2_done = sem("fc2_done")
            acc_ready = sem("acc_ready")
            wout_ready = sem("wout_ready")

            SMALL = 6
            with nc.Block() as block:
                @block.sync
                def _(sp_):
                    xv = a["x"].rearrange("b s d -> s b d")
                    for q in range(4):
                        sp_.dma_start(x_tok[:, 2 * q:2 * q + 2, :], xv[:, 2 * q:2 * q + 2, :]).then_inc(s_x, 16)
                    sp_.dma_start(fc1_raw[:, :, :], a["fc1T"].rearrange("(k p) n -> p k n", p=P)).then_inc(s_fc1, 16)
                    sp_.dma_start(win_raw[:, :, :], a["winT"].rearrange("(k p) n -> p k n", p=P)).then_inc(s_win, 16)
                    sp_.dma_start(fc2_raw[:, :, :], a["fc2T"].rearrange("(k p) n -> p k n", p=P)).then_inc(s_fc2, 16)

                @block.scalar
                def _(act):
                    act.dma_start(ident[:, :], a["ident"]).then_inc(s_const, 16)
                    act.dma_start(lnw[:, :], a["ln_w"]).then_inc(s_small, 16)
                    act.dma_start(lnb[:, :], a["ln_b"]).then_inc(s_small, 16)
                    act.dma_start(fc1b[:, :], a["fc1_b"]).then_inc(s_small, 16)
                    act.dma_start(dtb[:, :], a["dt_bias"]).then_inc(s_small, 16)
                    act.dma_start(alog[:, :, :], a["A_log"]).then_inc(s_small, 16)
                    act.dma_start(nw_col[:, :], a["norm_w"]).then_inc(s_small, 16)
                    act.dma_start(fc2_bias[:, :], a["fc2_b"]).then_inc(s_fc2b, 16)
                    act.dma_start(d_col[:, :], a["Dp"]).then_inc(s_const, 16)
                    act.dma_start(upper[:, :], a["upper"]).then_inc(s_const, 16)
                    act.dma_start(lower[:, :], a["lower"]).then_inc(s_const, 16)
                    act.dma_start(wout[:, :, :], a["woutT"].rearrange("(k p) n -> p k n", p=P)).then_inc(s_wout, 16)
                    act.wait_ge(s_small, 16 * SMALL)
                    for g in range(BATCH // 2):
                        for k in range(KT):
                            act.wait_ge(hT_ready, 2 * g + k + 1)
                            act.activation(h_f[:, k, g * 256:(g + 1) * 256], bank[(2 * g + k) % 4][:, 0:256],
                                           ACT.Identity, bias=lnb[:, k:k + 1],
                                           scale=lnw[:, k:k + 1]).then_inc(hf_ready, 1)
                    for th in range(2):
                        act.wait_ge(dtp_ready, th + 1)
                        act.activation(dt_row[:, th * HALF:(th + 1) * HALF], bank[4 + th][0:NH, :], ACT.Identity,
                                       bias=dtb[:, 0:1]).then_inc(dtrow_ready, 1)
                    act.activation(ea[:, :, :], alog[:, :, :], ACT.Exp).then_inc(spa, 1)
                    act.wait_ge(sp, 2)
                    act.activation(sp_e[:, :, :], sp_abs[:, :, :], ACT.Exp, scale=-1.0).then_inc(spa, 1)
                    act.wait_ge(sp, 3)
                    act.activation(sp_ln[:, :, :], sp_u[:, :, :], ACT.Ln).then_inc(spa, 1)
                    with act.Fori(0, 2) as th:
                        for i in range(IT1):
                            act.wait_ge(fc1_done, th * IT1 + (i + 1))
                            if i < 2:
                                act.wait_ge(glo_ready, th * IT1)
                            else:
                                act.wait_ge(glo_ready, th * IT1 + (i - 1))
                            act.activation(g_f[:, i % 2, :], bank[i % 4][:, :], ACT.Gelu_apprx_tanh,
                                           bias=fc1b[:, i:i + 1]).then_inc(gf_ready, 1)

                @block.gpsimd
                def _(pool):
                    pool.memset(mhalf[:, :], -0.5).then_inc(mhalf_ready, 1)
                    pool.wait_ge(mhalf_ready, 1)
                    pool.wait_ge(mv_ready, BATCH)
                    pool.tensor_scalar(veps[:, :], mv[:, :, 1], 1.0, LN_EPS, ALU.mult,
                                       ALU.add).then_inc(veps_ready, 1)
                    pool.wait_ge(veps_ready, 1)
                    pool.tensor_tensor(rstd[:, :], veps[:, :], mhalf[:, :], ALU.pow).then_inc(rstd_ready, 1)
                    pool.wait_ge(s_win, 16)
                    for k in range(KT):
                        pool.tensor_scalar(win_hi[:, k, :], win_raw[:, k, :], 1.0, 0.0, ALU.mult,
                                           ALU.add).then_inc(winhi_ready, 1)
                        pool.wait_ge(winhi_ready, k + 1)
                        pool.tensor_tensor(win_lo[:, k, :], win_raw[:, k, :], win_hi[:, k, :].bitcast(F32),
                                           ALU.subtract).then_inc(winlo_ready, 1)
                    pool.wait_ge(s_fc2, 16)
                    for k in range(2):
                        s = slice(4 * k, 4 * k + 4)
                        pool.tensor_scalar(fc2_hi[:, s, :], fc2_raw[:, s, :], 1.0, 0.0, ALU.mult,
                                           ALU.add).then_inc(fc2hi_ready, 1)
                        pool.wait_ge(fc2hi_ready, k + 1)
                        pool.tensor_tensor(fc2_lo[:, s, :], fc2_raw[:, s, :], fc2_hi[:, s, :].bitcast(F32),
                                           ALU.subtract).then_inc(fc2lo_ready, 1)

                @block.vector
                def _(dve):
                    for b in range(BATCH):
                        dve.wait_ge(s_x, 16 * 4 if b >= 6 else 16 * 4)
                        dve.bn_stats(stats[:, b, :], x_tok[:, b, :]).then_inc(stats_ready, 1)
                    for b in range(BATCH):
                        dve.wait_ge(stats_ready, b + 1)
                        dve.bn_aggr(mv[:, b, :], stats[:, b, :]).then_inc(mv_ready, 1)
                    dve.wait_ge(rstd_ready, 1)
                    for b in range(BATCH):
                        dve.tensor_scalar(xhat[:, b, :], x_tok[:, b, :], mv[:, b, 0:1], rstd[:, b:b + 1],
                                          ALU.subtract, ALU.mult).then_inc(xhat_ready, 1)
                    dve.wait_ge(s_fc1, 16)
                    for k in range(KT):
                        dve.tensor_copy(fc1_hi[:, k, :], fc1_raw[:, k, :]).then_inc(fc1hi_ready, 1)
                        dve.wait_ge(fc1hi_ready, k + 1)
                        dve.tensor_tensor(fc1_lo[:, k, :], fc1_raw[:, k, :], fc1_hi[:, k, :].bitcast(F32),
                                          ALU.subtract).then_inc(fc1lo_ready, 1)
                    for g in range(BATCH // 2):
                        s = slice(g * 256, (g + 1) * 256)
                        dve.wait_ge(hf_ready, 2 * g + 2)
                        dve.tensor_copy(h_hi[:, :, s], h_f[:, :, s]).then_inc(hhi_ready, 1)
                        dve.wait_ge(hhi_ready, g + 1)
                        dve.tensor_tensor(h_lo[:, :, s], h_f[:, :, s], h_hi[:, :, s].bitcast(F32),
                                          ALU.subtract).then_inc(hlo_ready, 1)
                    dve.wait_ge(s_fc2b, 16)
                    dve.scalar_tensor_tensor(x2b[:, :, :], x_tok[:, :, :], 2.0,
                                             fc2_bias[:, None, :].broadcast_to([P, BATCH, DM]),
                                             ALU.mult, ALU.add).then_inc(x2b_ready, 1)
                    dve.wait_ge(s_wout, 16)
                    dve.wait_ge(s_small, 16 * SMALL)
                    for j in range(PAIRS):
                        dve.tensor_scalar(wout[:, j, :], wout[:, j, :], nw_col[:, j:j + 1], None,
                                          ALU.mult).then_inc(wout_ready, 1)
                    dve.wait_ge(dtT_ready, BATCH)
                    dve.tensor_copy(sp_x[:, :, :],
                                    bank[6][:, 0:BATCH * NH].rearrange("p (b h) -> p b h", b=BATCH)).then_inc(sp, 1)
                    dve.wait_ge(sp, 1)
                    dve.scalar_tensor_tensor(sp_abs[:, :, :], sp_x[:, :, :], -1.0, sp_x[:, :, :], ALU.mult,
                                             ALU.max).then_inc(sp, 1)
                    dve.wait_ge(spa, 2)
                    dve.tensor_scalar(sp_u[:, :, :], sp_e[:, :, :], 1.0, None, ALU.add).then_inc(sp, 1)
                    dve.wait_ge(sp, 3)
                    dve.scalar_tensor_tensor(sp_d[:, :, :], sp_u[:, :, :], -1.0, sp_e[:, :, :], ALU.add,
                                             ALU.subtract).then_inc(sp, 1)
                    dve.reciprocal(sp_r[:, :, :], sp_u[:, :, :]).then_inc(sp, 1)
                    dve.wait_ge(sp, 5)
                    dve.tensor_tensor(sp_t[:, :, :], sp_d[:, :, :], sp_r[:, :, :], ALU.mult).then_inc(sp, 1)
                    dve.wait_ge(spa, 3)
                    dve.wait_ge(sp, 6)
                    dve.tensor_tensor(sp_s[:, :, :], sp_ln[:, :, :], sp_t[:, :, :], ALU.subtract).then_inc(sp, 1)
                    dve.wait_ge(sp, 7)
                    dve.scalar_tensor_tensor(dt[:, :, :], sp_x[:, :, :], 0.0, sp_s[:, :, :], ALU.max,
                                             ALU.add).then_inc(sp, 1)
                    dve.wait_ge(sp, 8)
                    dve.scalar_tensor_tensor(dta[:, :, :], dt[:, :, :], -1.0, ea[:, :, :], ALU.mult,
                                             ALU.mult).then_inc(dta_ready, 1)
                    dve.wait_ge(x2b_ready, 1)
                    with dve.Fori(0, 2) as th:
                        for i in range(IT1):
                            dve.wait_ge(gf_ready, th * IT1 + (i + 1))
                            dve.wait_ge(fc2_done, th * 4)
                            dve.tensor_copy(g_hi[:, i, :], g_f[:, i % 2, :]).then_inc(ghi_ready, 1)
                            dve.wait_ge(ghi_ready, th * IT1 + (i + 1))
                            dve.tensor_tensor(g_lo[:, i, :], g_f[:, i % 2, :], g_hi[:, i, :].bitcast(F32),
                                              ALU.subtract).then_inc(glo_ready, 1)
                        for t in range(4):
                            dve.wait_ge(fc2_done, th * 4 + (t + 1))
                            dve.tensor_tensor(acc[:, bass.ds(th * 4 + t, 1), :], bank[4 + t][:, 0:DM][:, None, :],
                                              x2b[:, bass.ds(th * 4 + t, 1), :], ALU.add).then_inc(acc_ready, 1)

                @block.tensor
                def _(pe):
                    pe.wait_ge(s_const, 64)
                    for g in range(BATCH // 2):
                        pe.wait_ge(xhat_ready, 2 * g + 2)
                        for k in range(KT):
                            if 2 * g + k >= 4:
                                pe.wait_ge(hf_ready, 2 * g + k - 3)
                            for b in range(2):
                                mm = pe.transpose(bank[(2 * g + k) % 4][:, b * P:(b + 1) * P],
                                                  xhat[:, 2 * g + b, k * P:(k + 1) * P], ident[:, :])
                            mm.then_inc(hT_ready, 1)
                    pe.wait_ge(winlo_ready, KT)
                    pe.wait_ge(hlo_ready, BATCH // 2)
                    for th in range(2):
                        s = slice(th * HALF, (th + 1) * HALF)
                        for k in range(KT):
                            w = slice(DT0, DT0 + P)
                            mm = products(pe, bank[4 + th][:, :], (win_hi[:, k, w], win_lo[:, k, w]),
                                          (h_hi[:, k, s], h_lo[:, k, s]), k == 0, k == KT - 1)
                        mm.then_inc(dtp_ready, 1)
                    pe.wait_ge(dtrow_ready, 2)
                    for b in range(BATCH):
                        pe.transpose(bank[6][:, b * NH:(b + 1) * NH], dt_row[:, b * P:(b + 1) * P],
                                     ident[0:NH, 0:NH]).then_inc(dtT_ready, 1)
                    pe.wait_ge(fc1lo_ready, KT)
                    pe.wait_ge(fc2lo_ready, 2)
                    pe.wait_ge(sp, 1)
                    with pe.Fori(0, 2) as th:
                        tok = bass.ds(th * HALF, HALF)
                        for i in range(IT1):
                            if i < 4:
                                pe.wait_ge(gf_ready, th * IT1)
                            else:
                                pe.wait_ge(gf_ready, th * IT1 + (i - 3))
                            w = slice(i * P, (i + 1) * P)
                            for k in range(KT):
                                mm = products(pe, bank[i % 4][:, :], (fc1_hi[:, k, w], fc1_lo[:, k, w]),
                                              (h_hi[:, k, tok], h_lo[:, k, tok]), k == 0, k == KT - 1)
                            mm.then_inc(fc1_done, 1)
                        pe.wait_ge(glo_ready, th * IT1 + IT1)
                        pe.wait_ge(acc_ready, th * 4)
                        for t in range(4):
                            s = slice(t * P, (t + 1) * P)
                            for i in range(IT1):
                                mm = products(pe, bank[4 + t][:, 0:DM], (g_hi[:, i, s], g_lo[:, i, s]),
                                              (fc2_hi[:, i, :], fc2_lo[:, i, :]), i == 0, i == IT1 - 1)
                            mm.then_inc(fc2_done, 1)

        with ExitStack() as part:
            sb, ps, sem = scope(part)
            TW = 2 * P
            th_z = sb("th_z", [P, Z_T, TW])
            sz = sb("sz", [P, Z_T, TW])
            c_t = sb("c_t", [P, C_T, TW])
            b_t = sb("b_t", [P, B_T, TW])
            x_t = sb("x_t", [P, X_T, TW])
            xpad = sb("xpad", [P, NG, 2, P])
            tri = sb("tri", [P, NH, P])
            dec = sb("dec", [P, NH, P])
            decm = sb("decm", [P, NH, P])
            wts = sb("wts", [P, NH, P])
            yd = sb("yd", [P, PAIRS, P])
            yg = sb("yg", [P, PAIRS, P])
            sq = sb("sq", [P, PAIRS, P])
            sqs = sb("sqs", [P, P])
            ones = sb("ones", [P, 2])
            ve = sb("ve", [P, 1])
            ry = sb("ry", [P, 1])
            mh = sb("mh", [P, 1])
            pre = sb("pre", [P, DM])
            st = sb("st", [P, 6])
            mv2 = sb("mv2", [P, 2])
            ve2 = sb("ve2", [P, 1])
            r2 = sb("r2", [P, 1])
            bz = ps("bz", [P, 2, 512])
            bc = ps("bc", [P, 2, 512])
            bb = ps("bb", [P, 512])
            bx = ps("bx", [P, 512])
            b_out = ps("b_out", [P, 512])
            b_ss = ps("b_ss", [P, 512])

            names = ("m_const", "m_zp", "m_cp", "m_bp", "m_xp", "m_tanh", "m_sz", "m_c", "m_b", "m_x", "m_xt",
                     "m_xpad", "m_tri", "m_seg", "m_dec", "m_decm", "m_g", "m_w", "m_y", "m_yd", "m_yg", "m_sq",
                     "m_sqs", "m_ss", "m_ve", "m_ry", "m_out", "m_pre", "m_st", "m_mv", "m_ve2", "m_r2", "m_x1",
                     "m_ti")
            (m_const, m_zp, m_cp, m_bp, m_xp, m_tanh, m_sz, m_c, m_b, m_x, m_xt, m_xpad, m_tri, m_seg, m_dec,
             m_decm, m_g, m_w, m_y, m_yd, m_yg, m_sq, m_sqs, m_ss, m_ve, m_ry, m_out, m_pre, m_st, m_mv, m_ve2,
             m_r2, m_x1, m_ti) = [sem(n) for n in names]
            NPAIR = BATCH // 2

            with nc.Block() as block:
                @block.gpsimd
                def _(pool):
                    pool.memset(xpad[:, :, :, :], 0.0).then_inc(m_const, 1)
                    pool.memset(ones[:, :], 1.0).then_inc(m_const, 1)
                    pool.memset(mh[:, :], -0.5).then_inc(m_const, 1)
                    pool.wait_ge(m_const, 3)
                    dec_turn, mv_turn = counter(pool, "dec_turn", 1), counter(pool, "mv_turn", 1)
                    with pool.Fori(0, NPAIR) as j:
                        for c in range(2):
                            n = j * 2 + c
                            pool.wait_ge(m_seg, n)
                            pool.tensor_tensor(tri[:, :, :], upper[:, None, :].broadcast_to([P, NH, P]),
                                               dta[:, bass.ds(n, 1), :].rearrange("p b h -> p (b h)")[:, :, None]
                                               .broadcast_to([P, NH, P]), ALU.mult).then_inc(m_tri, 1)
                            pool.wait_ge(m_w, n)
                            wait_turn(pool, m_dec, dec_turn)
                            pool.affine_select(out=decm[:, :, :], in_=dec[:, :, :], pattern=[[0, NH], [1, P]],
                                               compare_op=ALU.is_ge, fill=0.0, base=0,
                                               channel_multiplier=-1).then_inc(m_decm, 1)
                            pool.wait_ge(m_ve, n + 1)
                            pool.wait_ge(m_pre, n)
                            pool.tensor_tensor(ry[:, :], ve[:, :], mh[:, :], ALU.pow).then_inc(m_ry, 1)
                            wait_turn(pool, m_mv, mv_turn)
                            pool.tensor_scalar(ve2[:, :], mv2[:, 1:2], 1.0, LN_EPS, ALU.mult,
                                               ALU.add).then_inc(m_ve2, 1)
                            pool.wait_ge(m_ve2, n + 1)
                            pool.tensor_tensor(r2[:, :], ve2[:, :], mh[:, :], ALU.pow).then_inc(m_r2, 1)

                @block.scalar
                def _(act):
                    with act.Fori(0, NPAIR) as j:
                        act.wait_ge(m_yg, j * 2)
                        for q in range(2):
                            act.wait_ge(m_zp, j * 2 + (q + 1))
                            act.activation(th_z[:, 2 * q:2 * q + 2, :], bz[:, q, :].rearrange("p (a t) -> p a t", a=2),
                                           ACT.Tanh, scale=0.5).then_inc(m_tanh, 1)
                        act.wait_ge(m_g, j * 2)
                        for q in range(2):
                            act.wait_ge(m_cp, j * 2 + (q + 1))
                            act.activation(c_t[:, 2 * q:2 * q + 2, :], bc[:, q, :].rearrange("p (a t) -> p a t", a=2),
                                           ACT.Copy).then_inc(m_c, 1)
                        act.wait_ge(m_bp, j + 1)
                        act.activation(b_t[:, :, :], bb[:, :].rearrange("p (a t) -> p a t", a=2),
                                       ACT.Copy).then_inc(m_b, 1)
                        act.wait_ge(m_xp, j + 1)
                        act.wait_ge(m_yd, j * 2)
                        act.activation(x_t[:, :, :], bx[:, :].rearrange("p (a t) -> p a t", a=2),
                                       ACT.Copy).then_inc(m_x, 1)
                        for c in range(2):
                            n = j * 2 + c
                            act.wait_ge(m_seg, n + 1)
                            act.wait_ge(m_decm, n)
                            act.activation(dec[:, :, :], bz[:, :, :].rearrange("p a (h l) -> p (a h) l", l=P),
                                           ACT.Exp).then_inc(m_dec, 1)
                            act.wait_ge(m_yg, n + 1)
                            act.wait_ge(m_sqs, n)
                            act.activation(sq[:, :, :], yg[:, :, :], ACT.Square).then_inc(m_sq, 1)

                @block.vector
                def _(dve):
                    dve.wait_ge(m_const, 3)
                    with dve.Fori(0, NPAIR) as j:
                        for q in range(2):
                            dve.wait_ge(m_tanh, j * 2 + (q + 1))
                            dve.scalar_tensor_tensor(sz[:, 2 * q:2 * q + 2, :], th_z[:, 2 * q:2 * q + 2, :], 1.0,
                                                     bz[:, q, :].rearrange("p (a t) -> p a t", a=2), ALU.add,
                                                     ALU.mult).then_inc(m_sz, 1)
                        for c in range(2):
                            n = j * 2 + c
                            tk = slice(c * P, (c + 1) * P)
                            dve.wait_ge(m_xt, n + 1)
                            dve.wait_ge(m_y, n)
                            for o in range(2):
                                dve.tensor_copy(xpad[:, :, o, o * HD:(o + 1) * HD],
                                                bx[:, 0:2 * P].rearrange("p (g d) -> p g d", g=2)[:, :, 0:HD]
                                                ).then_inc(m_xpad, 1)
                            dve.wait_ge(m_decm, n + 1)
                            dve.wait_ge(m_g, n + 1)
                            for h in range(NH):
                                dve.scalar_tensor_tensor(
                                    wts[:, h, :], bc[:, h % 2, (h // 2) * P:(h // 2 + 1) * P],
                                    dt[:, bass.ds(n, 1), h:h + 1].rearrange("p b h -> p (b h)"),
                                    decm[:, h, :], ALU.mult, ALU.mult).then_inc(m_ti if h < NH - 1 else m_w, 1)
                            dve.wait_ge(m_y, n + 1)
                            dve.wait_ge(m_x, j + 1)
                            for i in range(PAIRS):
                                dve.scalar_tensor_tensor(yd[:, i, :], x_t[:, i // 2, tk], d_col[:, i:i + 1],
                                                         bb[:, i * P:(i + 1) * P], ALU.mult,
                                                         ALU.add).then_inc(m_ti if i < PAIRS - 1 else m_yd, 1)
                            dve.wait_ge(m_yd, n + 1)
                            dve.wait_ge(m_ti, n * 10 + 10)
                            dve.wait_ge(m_sz, j * 2 + 2)
                            dve.wait_ge(m_out, n)
                            dve.wait_ge(m_sq, n)
                            dve.tensor_tensor(yg[:, :, :], yd[:, :, :], sz[:, :, tk], ALU.mult).then_inc(m_yg, 1)
                            dve.wait_ge(m_sq, n + 1)
                            dve.wait_ge(m_ss, n)
                            dve.tensor_reduce(sqs[:, :], sq[:, :, :].rearrange("p i l -> p l i"), AX_X,
                                              ALU.add).then_inc(m_sqs, 1)
                            dve.wait_ge(m_ss, n + 1)
                            dve.wait_ge(m_ry, n)
                            dve.tensor_scalar(ve[:, :], b_ss[:, 0:1], 1.0 / D_IN, 4 * LN_EPS, ALU.mult,
                                              ALU.add).then_inc(m_ve, 1)
                            dve.wait_ge(m_ry, n + 1)
                            dve.wait_ge(m_out, n + 1)
                            dve.wait_ge(m_x1, n)
                            dve.scalar_tensor_tensor(pre[:, None, :], b_out[:, None, 0:DM], ry[:, 0:1],
                                                     acc[:, bass.ds(n, 1), :], ALU.mult, ALU.add).then_inc(m_pre, 1)
                            dve.wait_ge(m_pre, n + 1)
                            dve.bn_stats(st[:, :], pre[:, :]).then_inc(m_st, 1)
                            met(dve, m_const)
                            dve.wait_ge(m_st, n + 1)
                            dve.wait_ge(m_ve2, n)
                            dve.bn_aggr(mv2[:, :], st[:, :]).then_inc(m_mv, 1)
                            dve.wait_ge(m_mv, n + 1)
                            dve.wait_ge(m_r2, n + 1)
                            dve.tensor_scalar(x_tok[:, bass.ds(n, 1), :], pre[:, None, :], mv2[:, 0:1], r2[:, 0:1],
                                              ALU.subtract, ALU.mult).then_inc(m_x1, 1)

                @block.tensor
                def _(pe):
                    pe.wait_ge(m_const, 3)
                    with pe.Fori(0, NPAIR) as j:
                        tok = bass.ds(j * TW, TW)

                        def project(dst, col):
                            for k in range(KT):
                                w = slice(col, col + P)
                                mm = products(pe, dst, (win_hi[:, k, w], win_lo[:, k, w]),
                                              (h_hi[:, k, tok], h_lo[:, k, tok]), k == 0, k == KT - 1)
                            return mm

                        pe.wait_ge(m_dec, j * 2)
                        for q in range(2):
                            for i in range(2):
                                mm = project(bz[:, q, i * TW:(i + 1) * TW], Z0 + (2 * q + i) * P)
                            mm.then_inc(m_zp, 1)
                        pe.wait_ge(m_yd, j * 2)
                        for i in range(2):
                            mm = project(bb[:, i * TW:(i + 1) * TW], B0 + i * P)
                        mm.then_inc(m_bp, 1)
                        pe.wait_ge(m_xpad, j * 4)
                        for i in range(2):
                            mm = project(bx[:, i * TW:(i + 1) * TW], X0 + i * P)
                        mm.then_inc(m_xp, 1)
                        pe.wait_ge(m_w, j * 2)
                        for q in range(2):
                            for i in range(2):
                                mm = project(bc[:, q, i * TW:(i + 1) * TW], C0 + (2 * q + i) * P)
                            mm.then_inc(m_cp, 1)
                        for c in range(2):
                            n = j * 2 + c
                            tk = slice(c * P, (c + 1) * P)
                            pe.wait_ge(m_x, j + 1)
                            if c:
                                pe.wait_ge(m_xpad, j * 4 + 2)
                            for g in range(NG):
                                mm = pe.transpose(bx[:, g * P:(g + 1) * P], x_t[:, g, tk], ident[:, :])
                            mm.then_inc(m_xt, 1)
                            pe.wait_ge(m_tri, n + 1)
                            if c:
                                pe.wait_ge(m_dec, j * 2 + 1)
                            pe.wait_ge(m_sz, j * 2 + 2)
                            for q in range(2):
                                mm = pe.matmul(bz[:, q, :], lower[:, :],
                                               tri[:, 4 * q:4 * q + 4, :].rearrange("p h l -> p (h l)"),
                                               start=True, stop=True)
                            mm.then_inc(m_seg, 1)
                            pe.wait_ge(m_b, j + 1)
                            pe.wait_ge(m_c, j * 2 + 2)
                            if c:
                                pe.wait_ge(m_w, j * 2 + 1)
                            for h in range(NH):
                                r = slice((h % 2) * HD, (h % 2 + 1) * HD)
                                mm = pe.matmul(bc[:, h % 2, (h // 2) * P:(h // 2 + 1) * P], b_t[r, h // REP, tk],
                                               c_t[r, h // 2, tk], start=True, stop=True)
                            mm.then_inc(m_g, 1)
                            pe.wait_ge(m_w, n + 1)
                            pe.wait_ge(m_ti, n * 10 + 7)
                            pe.wait_ge(m_xpad, n * 2 + 2)
                            if c:
                                pe.wait_ge(m_yd, j * 2 + 1)
                            for h in range(NH):
                                mm = pe.matmul(bb[:, (h // 2) * P:(h // 2 + 1) * P], xpad[:, h // REP, h % 2, :],
                                               wts[:, h, :], start=(h % 2 == 0), stop=(h % 2 == 1))
                            mm.then_inc(m_y, 1)
                            pe.wait_ge(m_yg, n + 1)
                            pe.wait_ge(m_pre, n)
                            for i in range(PAIRS):
                                mm = pe.matmul(b_out[:, 0:DM], yg[:, i, :], wout[:, i, :], start=(i == 0),
                                               stop=(i == PAIRS - 1))
                            mm.then_inc(m_out, 1)
                            pe.wait_ge(m_sqs, n + 1)
                            pe.wait_ge(m_ve, n)
                            pe.matmul(b_ss[:, 0:2], sqs[:, :], ones[:, :], start=True, stop=True).then_inc(m_ss, 1)


def cross_attention(nc, a, scope, ident, x_tok):
    NS = BATCH * KVH
    QW = AREP * AD
    MW = MT * P
    with ExitStack() as layer:
        sb, ps, sem = scope(layer)
        wq_hi = sb("wq_hi", [P, KT, KVH, QW], F32R)
        wq_lo = sb("wq_lo", [P, KT, KVH, QW], F32R)
        wkv_hi = sb("wkv_hi", [P, 2, KT, KVH, 2 * AD], F32R)
        wkv_lo = sb("wkv_lo", [P, 2, KT, KVH, 2 * AD], F32R)
        wo_hi = sb("wo_hi", [P, AH, DM], F32R)
        wo_lo = sb("wo_lo", [P, AH, DM], F32R)
        cq = sb("cq", [P, AD])
        sq_ = sb("sq_", [P, AD])
        ck = sb("ck", [P, AD])
        sk = sb("sk", [P, AD])
        kw = sb("kw", [P, AD])
        kw_c = sb("kw_c", [P, AD])
        mask = sb("mask", [P, MW], F32R)
        ident_r = sb("ident_r", [P, P], F32R)

        with ExitStack() as part:
            sb, ps, sem = scope(part)
            wq_raw = sb("wq_raw", [P, KT, KVH, QW])
            wkv_raw = sb("wkv_raw", [P, 2, KT, KVH, 2 * AD])
            wo_raw = sb("wo_raw", [P, AH, DM])
            cos = sb("cos", [P, AD])
            sin = sb("sin", [P, AD])
            qw = sb("qw", [P, AD])
            qwr = sb("qwr", [P, AD])
            kwr = sb("kwr", [P, AD])
            mask_raw = sb("mask_raw", [P, MW])
            w_q, w_kv, w_o, w_small, w_kw = [sem(n) for n in ("w_q", "w_kv", "w_o", "w_small", "w_kw")]
            w_hi = [sem(f"w_hi{i}") for i in range(3)]
            w_lo = [sem(f"w_lo{i}") for i in range(3)]
            w_tab = sem("w_tab")
            with nc.Block() as block:
                @block.sync
                def _(sp):
                    sp.dma_start(wq_raw[:, :, :, :].rearrange("p k g n -> p k (g n)"),
                                 a["wq"].rearrange("(k p) n -> p k n", p=P)).then_inc(w_q, 16)
                    sp.dma_start(wkv_raw[:, :, :, :, :].rearrange("p s k g n -> p s k (g n)"),
                                 a["wkv"].rearrange("s (k p) n -> p s k n", p=P)).then_inc(w_kv, 16)
                    sp.dma_start(wo_raw[:, :, :], a["wo"].rearrange("(h p) n -> p h n", p=P)).then_inc(w_o, 16)

                @block.scalar
                def _(act):
                    for t, name in ((cos, "cos"), (sin, "sin"), (qw, "qw"), (qwr, "qwr"), (kwr, "kwr"),
                                    (mask_raw, "mask")):
                        act.dma_start(t[:, :], a[name]).then_inc(w_small, 16)
                    act.dma_start(kw[:, :], a["kw"]).then_inc(w_kw, 16)
                    act.wait_ge(w_q, 16)
                    act.activation(wq_hi[:, :, :, :], wq_raw[:, :, :, :], ACT.Copy).then_inc(w_hi[0], 1)
                    act.wait_ge(w_kv, 16)
                    act.activation(wkv_hi[:, :, :, :, :].rearrange("p s k g n -> p (s k g n)"),
                                   wkv_raw[:, :, :, :, :].rearrange("p s k g n -> p (s k g n)"),
                                   ACT.Copy).then_inc(w_hi[1], 1)
                    act.wait_ge(w_o, 16)
                    act.activation(wo_hi[:, :, :], wo_raw[:, :, :], ACT.Copy).then_inc(w_hi[2], 1)

                def low(eng, lo, raw, hi, i):
                    eng.wait_ge(w_hi[i], 1)
                    eng.tensor_tensor(lo, raw, hi.bitcast(F32), ALU.subtract).then_inc(w_lo[i], 1)

                @block.vector
                def _(dve):
                    dve.wait_ge(w_small, 16 * 6)
                    dve.wait_ge(w_kw, 16)
                    dve.tensor_tensor(cq[:, :], cos[:, :], qw[:, :], ALU.mult).then_inc(w_tab, 1)
                    dve.tensor_tensor(sq_[:, :], sin[:, :], qwr[:, :], ALU.mult).then_inc(w_tab, 1)
                    dve.tensor_tensor(ck[:, :], cos[:, :], kw[:, :], ALU.mult).then_inc(w_tab, 1)
                    dve.tensor_tensor(sk[:, :], sin[:, :], kwr[:, :], ALU.mult).then_inc(w_tab, 1)
                    dve.tensor_scalar(kw_c[:, :], kw[:, :], float(AD) ** 0.5, None, ALU.mult).then_inc(w_tab, 1)
                    dve.tensor_copy(mask[:, :], mask_raw[:, :]).then_inc(w_tab, 1)
                    dve.tensor_copy(ident_r[:, :], ident[:, :]).then_inc(w_tab, 1)
                    flat = lambda t: t[:, :, :, :].rearrange("p k g n -> p (k g n)")
                    low(dve, flat(wq_lo), flat(wq_raw), flat(wq_hi), 0)
                    flat3 = lambda t: t[:, :, :].rearrange("p h n -> p (h n)")
                    low(dve, flat3(wo_lo), flat3(wo_raw), flat3(wo_hi), 2)

                @block.gpsimd
                def _(pool):
                    flat = lambda t: t[:, :, :, :, :].rearrange("p s k g n -> p (s k g n)")
                    low(pool, flat(wkv_lo), flat(wkv_raw), flat(wkv_hi), 1)

        with ExitStack() as part:
            sb, ps, sem = scope(part)
            x_cur = sb("x_cur", [P, DM])
            c_cur = sb("c_cur", [P, DM])
            xT_hi = sb("xT_hi", [P, 2, KT, P], F32R)
            xT_lo = sb("xT_lo", [P, 2, KT, P], F32R)
            q_s = sb("q_s", [P, AREP, AD])
            kv_s = sb("kv_s", [P, 2, 2, AD])
            sqr = sb("sqr", [P, AREP + 2, AD])
            ss = sb("ss", [P, AREP + 2])
            sse = sb("sse", [P, AREP + 2])
            rs = sb("rs", [P, KVH, AREP + 2])
            mh = sb("mh6", [P, AREP + 2])
            t1 = sb("t1", [P, AREP, AD])
            t2 = sb("t2", [P, AREP, AD])
            u1 = sb("u1", [P, AD])
            u2 = sb("u2", [P, AD])
            u3 = sb("u3", [P, AD])
            q_r = sb("q_r", [P, AREP, AD])
            k_r = sb("k_r", [P, 2, AD])
            qT_hi = sb("qT_hi", [P, KVH, QW], F32R)
            qT_lo = sb("qT_lo", [P, KVH, QW], F32R)
            kT_hi = sb("kT_hi", [P, KVH, MW], F32R)
            kT_lo = sb("kT_lo", [P, KVH, MW], F32R)
            v_hi = sb("v_hi", [P, KVH, 2, AD], F32R)
            v_lo = sb("v_lo", [P, KVH, 2, AD], F32R)
            mx = sb("mx", [P, AREP])
            nb = sb("nb", [P, AREP])
            prob = sb("prob", [P, AREP, MW])
            den = sb("den", [P, AREP])
            rec = sb("rec", [P, AREP])
            pT_hi = sb("pT_hi", [P, MT, QW], F32R)
            pT_lo = sb("pT_lo", [P, MT, QW], F32R)
            oT_hi = sb("oT_hi", [P, QW], F32R)
            oT_lo = sb("oT_lo", [P, QW], F32R)
            pre = sb("pre2", [P, DM])
            st = sb("st2", [P, 6])
            mv = sb("mvx", [P, 2])
            ve = sb("vex", [P, 1])
            r1 = sb("r1x", [P, 1])
            b_s = ps("b_s", [P, 2, 512])
            b_p = ps("b_p", [P, 2, 512])
            b_o = ps("b_o", [P, 512])
            b_q = ps("b_q", [P, 512])
            b_kv = ps("b_kv", [P, 512])
            b_w = ps("b_w", [P, 512])

            names = ("a_const", "a_xcur", "a_ctx", "a_xt", "a_xhi", "a_xlo", "a_pj", "a_qs", "a_kvs", "a_sqr", "a_ss",
                     "a_sse", "a_rs", "a_t", "a_qr", "a_u", "a_kr", "a_vhi", "a_vlo", "a_qt", "a_qhi", "a_qlo",
                     "a_khi", "a_klo", "a_s", "a_mx", "a_nb", "a_exp", "a_rec", "a_prob", "a_pt", "a_phi", "a_plo",
                     "a_pv", "a_ohi", "a_olo", "a_wo", "a_pre", "a_st", "a_mv", "a_ve", "a_r1", "a_x2")
            (a_const, a_xcur, a_ctx, a_xt, a_xhi, a_xlo, a_pj, a_qs, a_kvs, a_sqr, a_ss, a_sse, a_rs, a_t, a_qr,
             a_u, a_kr, a_vhi, a_vlo, a_qt, a_qhi, a_qlo, a_khi, a_klo, a_s, a_mx, a_nb, a_exp, a_rec, a_prob,
             a_pt, a_phi, a_plo, a_pv, a_ohi, a_olo, a_wo, a_pre, a_st, a_mv, a_ve, a_r1, a_x2) = [
                sem(n) for n in names]

            def pe_x(pe, b, n):
                pe.wait_ge(a_xcur, b + 1)
                pe.wait_ge(a_ctx, b * 16 + 16)
                if n is not None:
                    pe.wait_ge(a_olo, n - 1)
                for s, t in ((0, x_cur), (1, c_cur)):
                    for k in range(KT):
                        mm = pe.transpose(b_o[:, (2 * s + k) * P:(2 * s + k + 1) * P], t[:, k * P:(k + 1) * P],
                                          ident[:, :])
                mm.then_inc(a_xt, 1)

            def pe_project(pe, b, g, m):
                pe.wait_ge(a_xlo, b + 1)
                pe.wait_ge(a_qlo, m)
                pe.wait_ge(a_klo, m)
                for k in range(KT):
                    products(pe, b_q[:, :], (xT_hi[:, 0, k, :], xT_lo[:, 0, k, :]),
                             (wq_hi[:, k, g, :], wq_lo[:, k, g, :]), k == 0, k == KT - 1)
                for s in range(2):
                    for k in range(KT):
                        mm = products(pe, b_kv[:, s * 256:(s + 1) * 256], (xT_hi[:, s, k, :], xT_lo[:, s, k, :]),
                                      (wkv_hi[:, s, k, g, :], wkv_lo[:, s, k, g, :]), k == 0, k == KT - 1)
                mm.then_inc(a_pj, 1)

            def pe_turn_qk(pe, m):
                pe.wait_ge(a_qr, m + 1)
                pe.wait_ge(a_kr, m * 2 + 2)
                pe.wait_ge(a_qs, m + 1)
                pe.wait_ge(a_kvs, m + 1)
                for h in range(AREP):
                    pe.transpose(b_q[:, h * P:(h + 1) * P], q_r[:, h, :], ident[:, :])
                for s in range(2):
                    mm = pe.transpose(b_kv[:, s * P:(s + 1) * P], k_r[:, s, :], ident[:, :])
                mm.then_inc(a_qt, 1)

            def pe_scores(pe, g, n):
                pe.wait_ge(a_qlo, n + 1)
                pe.wait_ge(a_klo, n + 1)
                pe.wait_ge(a_exp, n * AREP)
                for h in range(AREP):
                    o = b_s[:, h // 2, (h % 2) * MW:(h % 2 + 1) * MW]
                    hs = slice(h * P, (h + 1) * P)
                    products(pe, o, (qT_hi[:, g, hs], qT_lo[:, g, hs]), (kT_hi[:, g, :], kT_lo[:, g, :]), True, False)
                    mm = pe.matmul(o, ident_r[:, :], mask[:, :], start=False, stop=True)
                    if h % 2:
                        mm.then_inc(a_s, 1)

            def pe_turn_p(pe, n):
                pe.wait_ge(a_prob, n * AREP + AREP)
                pe.wait_ge(a_plo, n)
                for t in range(MT):
                    for h in range(AREP):
                        mm = pe.transpose(b_p[:, t, h * P:(h + 1) * P], prob[:, h, t * P:(t + 1) * P], ident[:, :])
                mm.then_inc(a_pt, 1)

            def pe_values(pe, g, n, xt):
                pe.wait_ge(a_plo, n + 1)
                pe.wait_ge(a_vlo, n + 1)
                pe.wait_ge(a_olo, n)
                if xt is not None:
                    pe.wait_ge(a_xlo, xt + 1)
                for t in range(MT):
                    mm = products(pe, b_o[:, :], (v_hi[:, g, 1 - t, :], v_lo[:, g, 1 - t, :]),
                                  (pT_hi[:, t, :], pT_lo[:, t, :]), t == 0, t == MT - 1)
                mm.then_inc(a_pv, 1)

            def pe_out(pe, b, g, n):
                pe.wait_ge(a_olo, n + 1)
                if g == 0:
                    pe.wait_ge(a_pre, b)
                for h in range(AREP):
                    hs = slice(h * P, (h + 1) * P)
                    mm = products(pe, b_w[:, 0:DM], (oT_hi[:, hs], oT_lo[:, hs]),
                                  (wo_hi[:, g * AREP + h, :], wo_lo[:, g * AREP + h, :]),
                                  g == 0 and h == 0, g == KVH - 1 and h == AREP - 1)
                mm.then_inc(a_wo, 1)

            def pe_step(pe, b, g, first, last):
                n = b * KVH + g
                prev, ahead2, ahead3 = not (first and g == 0), not (last and g >= 2), not (last and g >= 1)
                x_ahead = g == 1 and not last
                if prev:
                    pe_turn_p(pe, n - 1)
                if x_ahead:
                    pe_x(pe, b + 1, n)
                pe_scores(pe, g, n)
                if ahead2:
                    pe_turn_qk(pe, n + 2)
                if prev:
                    pe_values(pe, (g + 3) % KVH, n - 1, b + 1 if x_ahead else None)
                if ahead3:
                    pe_project(pe, b if g == 0 else b + 1, (g + 3) % KVH, n + 3)
                if prev:
                    pe_out(pe, b if g else b - 1, (g + 3) % KVH, n - 1)

            def act_x(act, b, m):
                act.wait_ge(a_xt, b + 1)
                act.wait_ge(a_pj, m)
                act.activation(xT_hi[:, :, :, :].rearrange("p s k t -> p (s k t)"), b_o[:, :],
                               ACT.Copy).then_inc(a_xhi, 1)

            def act_copies(act, m):
                act.wait_ge(a_pj, m + 1)
                act.wait_ge(a_t, m * 3)
                act.activation(q_s[:, :, :].rearrange("p h d -> p (h d)"), b_q[:, :], ACT.Copy).then_inc(a_qs, 1)
                act.wait_ge(a_kr, m * 2)
                act.wait_ge(a_vlo, m)
                act.activation(kv_s[:, :, :, :].rearrange("p s c d -> p (s c d)"), b_kv[:, :],
                               ACT.Copy).then_inc(a_kvs, 1)
                act.wait_ge(a_qs, m + 1)
                act.wait_ge(a_ss, m)
                act.activation(sqr[:, 0:AREP, :], q_s[:, :, :], ACT.Square).then_inc(a_sqr, 1)
                act.wait_ge(a_kvs, m + 1)
                act.activation(sqr[:, AREP:AREP + 2, :], kv_s[:, :, 0, :], ACT.Square).then_inc(a_sqr, 1)

            def act_qk(act, g, m):
                act.wait_ge(a_qt, m + 1)
                act.activation(qT_hi[:, g, :], b_q[:, :], ACT.Copy).then_inc(a_qhi, 1)
                act.activation(kT_hi[:, g, :], b_kv[:, 0:MW], ACT.Copy).then_inc(a_khi, 1)

            def act_exp(act, g, n):
                act.wait_ge(a_pt, n)
                act.wait_ge(a_rec, n)
                for h in range(AREP):
                    if h % 2 == 0:
                        act.wait_ge(a_nb, n * 2 + (h // 2 + 1))
                    act.activation(prob[:, h, :], b_s[:, h // 2, (h % 2) * MW:(h % 2 + 1) * MW], ACT.Exp,
                                   bias=nb[:, h:h + 1], scale=rs[:, g, h:h + 1],
                                   accum_out=den[:, h:h + 1]).then_inc(a_exp, 1)

            def act_step(act, b, g, first, last):
                n = b * KVH + g
                prev, ahead2, ahead3 = not (first and g == 0), not (last and g >= 2), not (last and g >= 1)
                if prev:
                    act.wait_ge(a_pt, n)
                    act.wait_ge(a_pv, n - 1)
                    act.activation(pT_hi[:, :, :], b_p[:, :, :], ACT.Copy).then_inc(a_phi, 1)
                if g == 1 and not last:
                    act_x(act, b + 1, n + 3)
                act_exp(act, g, n)
                if ahead2:
                    act_qk(act, (g + 2) % KVH, n + 2)
                if prev:
                    act.wait_ge(a_pv, n)
                    act.wait_ge(a_wo, n - 1)
                    act.activation(oT_hi[:, :], b_o[:, :], ACT.Copy).then_inc(a_ohi, 1)
                if ahead3:
                    act_copies(act, n + 3)

            def dve_x(dve, b):
                dve.wait_ge(a_xhi, b + 1)
                dve.tensor_tensor(xT_lo[:, :, :, :].rearrange("p s k t -> p (s k t)"), b_o[:, :],
                                  xT_hi[:, :, :, :].rearrange("p s k t -> p (s k t)").bitcast(F32),
                                  ALU.subtract).then_inc(a_xlo, 1)

            def dve_rotate(dve, g, m):
                hd = AD // 2
                heads = lambda t: t[:, None, :].broadcast_to([P, AREP, AD])
                half = lambda t, o: t[:, None, o:o + hd].broadcast_to([P, AREP, hd])
                dve.wait_ge(a_qs, m + 1)
                dve.wait_ge(a_qr, m)
                dve.tensor_tensor(t2[:, :, 0:hd], q_s[:, :, hd:AD], half(sq_, 0), ALU.mult).then_inc(a_t, 1)
                dve.tensor_tensor(t2[:, :, hd:AD], q_s[:, :, 0:hd], half(sq_, hd), ALU.mult).then_inc(a_t, 1)
                dve.tensor_tensor(t1[:, :, :], q_s[:, :, :], heads(cq), ALU.mult).then_inc(a_t, 1)
                dve.wait_ge(a_sqr, m * 2 + 2)
                dve.wait_ge(a_sse, m)
                dve.tensor_reduce(ss[:, :], sqr[:, :, :], AX_X, ALU.add).then_inc(a_ss, 1)
                dve.wait_ge(a_kvs, m + 1)
                dve.tensor_tensor(u1[:, :], kv_s[:, 0, 0, :], ck[:, :], ALU.mult).then_inc(a_u, 1)
                dve.tensor_tensor(u2[:, 0:hd], kv_s[:, 0, 0, hd:AD], sk[:, 0:hd], ALU.mult).then_inc(a_u, 1)
                dve.tensor_tensor(u2[:, hd:AD], kv_s[:, 0, 0, 0:hd], sk[:, hd:AD], ALU.mult).then_inc(a_u, 1)
                dve.tensor_copy(v_hi[:, g, :, :], kv_s[:, :, 1, :]).then_inc(a_vhi, 1)
                dve.wait_ge(a_u, m * 4 + 3)
                dve.tensor_tensor(u3[:, :], u1[:, :], u2[:, :], ALU.add).then_inc(a_u, 1)
                dve.wait_ge(a_vhi, m + 1)
                dve.tensor_tensor(v_lo[:, g, :, :], kv_s[:, :, 1, :], v_hi[:, g, :, :].bitcast(F32),
                                  ALU.subtract).then_inc(a_vlo, 1)
                dve.wait_ge(a_rs, m + 1)
                dve.wait_ge(a_u, m * 4 + 4)
                dve.wait_ge(a_qt, m)
                dve.tensor_scalar(k_r[:, 1, :], u3[:, :], rs[:, g, AREP:AREP + 1], float(AD) ** 0.5, ALU.mult,
                                  ALU.mult).then_inc(a_kr, 1)
                dve.scalar_tensor_tensor(k_r[:, 0, :], kv_s[:, 1, 0, :], rs[:, g, AREP + 1:AREP + 2], kw_c[:, :],
                                         ALU.mult, ALU.mult).then_inc(a_kr, 1)

            def dve_qk(dve, g, m):
                dve.wait_ge(a_qhi, m + 1)
                dve.tensor_tensor(qT_lo[:, g, :], b_q[:, :], qT_hi[:, g, :].bitcast(F32),
                                  ALU.subtract).then_inc(a_qlo, 1)
                dve.wait_ge(a_khi, m + 1)
                dve.tensor_tensor(kT_lo[:, g, :], b_kv[:, 0:MW], kT_hi[:, g, :].bitcast(F32),
                                  ALU.subtract).then_inc(a_klo, 1)

            def dve_max(dve, g, n):
                dve.wait_ge(a_exp, n * AREP)
                for q in range(2):
                    hs = slice(2 * q, 2 * q + 2)
                    dve.wait_ge(a_s, n * 2 + (q + 1))
                    dve.tensor_reduce(mx[:, hs], b_s[:, q, :].rearrange("p (h m) -> p h m", h=2), AX_X,
                                      ALU.max).then_inc(a_mx, 1)
                    dve.wait_ge(a_mx, n * 2 + (q + 1))
                    dve.scalar_tensor_tensor(nb[:, hs], mx[:, hs], -1.0, rs[:, g, hs], ALU.mult,
                                             ALU.mult).then_inc(a_nb, 1)

            def dve_tail(dve, b):
                dve.wait_ge(a_wo, b * KVH + KVH)
                dve.tensor_tensor(pre[:, None, :], b_w[:, None, 0:DM], x_tok[:, bass.ds(b, 1), :],
                                  ALU.add).then_inc(a_pre, 1)
                dve.wait_ge(a_pre, b + 1)
                dve.bn_stats(st[:, :], pre[:, :]).then_inc(a_st, 1)
                met(dve, a_const)
                dve.wait_ge(a_st, b + 1)
                dve.bn_aggr(mv[:, :], st[:, :]).then_inc(a_mv, 1)

            def dve_tail2(dve, b):
                dve.wait_ge(a_r1, b + 1)
                dve.wait_ge(a_mv, b + 1)
                dve.tensor_scalar(x_tok[:, bass.ds(b, 1), :], pre[:, None, :], mv[:, 0:1], r1[:, 0:1],
                                  ALU.subtract, ALU.mult).then_inc(a_x2, 1)

            def dve_step(dve, b, g, first, last):
                n = b * KVH + g
                prev, ahead2, ahead3 = not (first and g == 0), not (last and g >= 2), not (last and g >= 1)
                if prev:
                    dve.wait_ge(a_phi, n)
                    dve.tensor_tensor(pT_lo[:, :, :], b_p[:, :, :], pT_hi[:, :, :].bitcast(F32),
                                      ALU.subtract).then_inc(a_plo, 1)
                if g == 1 and not last:
                    dve_x(dve, b + 1)
                dve_max(dve, g, n)
                if ahead2:
                    dve_qk(dve, (g + 2) % KVH, n + 2)
                if g == 1 and not first:
                    dve_tail(dve, b - 1)
                dve.wait_ge(a_exp, n * AREP + AREP)
                dve.wait_ge(a_prob, n * AREP)
                dve.reciprocal(rec[:, :], den[:, :]).then_inc(a_rec, 1)
                if prev:
                    dve.wait_ge(a_ohi, n)
                    dve.tensor_tensor(oT_lo[:, :], b_o[:, :], oT_hi[:, :].bitcast(F32),
                                      ALU.subtract).then_inc(a_olo, 1)
                if g == 2 and not first:
                    dve_tail2(dve, b - 1)
                if ahead3:
                    dve_rotate(dve, (g + 3) % KVH, n + 3)

            turn = {}

            def pool_wait(pool, sem, value, name):
                if isinstance(value, int):
                    pool.wait_ge(sem, value)
                else:
                    wait_turn(pool, sem, turn[name])

            def pool_rotate(pool, g, m):
                pool_wait(pool, a_ss, m + 1, "ss")
                pool.tensor_scalar(sse[:, :], ss[:, :], 1.0, AD * RMS_EPS, ALU.mult, ALU.add).then_inc(a_sse, 1)
                pool.wait_ge(a_sse, m + 1)
                pool.tensor_tensor(rs[:, g, :], sse[:, :], mh[:, :], ALU.pow).then_inc(a_rs, 1)
                pool.wait_ge(a_t, m * 3 + 3)
                pool.wait_ge(a_qt, m)
                pool.tensor_tensor(q_r[:, :, :], t1[:, :, :], t2[:, :, :], ALU.add).then_inc(a_qr, 1)

            def pool_step(pool, b, g, first, last):
                n = b * KVH + g
                pool_wait(pool, a_rec, n + 1, "rec")
                for h in range(AREP):
                    pool.tensor_scalar(prob[:, h, :], prob[:, h, :], rec[:, h:h + 1], 1.0, ALU.mult,
                                       ALU.mult).then_inc(a_prob, 1)
                if g == 0 and not last:
                    pool_wait(pool, a_xt, b + 1, "xt")
                    pool.tensor_copy(x_cur[:, None, :], x_tok[:, bass.ds(b + 1, 1), :]).then_inc(a_xcur, 1)
                if g == 1 and not first:
                    pool_wait(pool, a_mv, b, "mv")
                    pool.tensor_scalar(ve[:, :], mv[:, 1:2], 1.0, LN_EPS, ALU.mult, ALU.add).then_inc(a_ve, 1)
                    pool.wait_ge(a_ve, b)
                    pool.tensor_tensor(r1[:, :], ve[:, :], mh[:, 0:1], ALU.pow).then_inc(a_r1, 1)
                if not (last and g >= 1):
                    pool_rotate(pool, (g + 3) % KVH, n + 3)

            def over_batches(eng, step):
                for g in range(KVH):
                    step(eng, 0, g, True, False)
                with eng.Fori(1, BATCH - 1) as b:
                    for g in range(KVH):
                        step(eng, b, g, False, False)
                for g in range(KVH):
                    step(eng, BATCH - 1, g, False, True)

            with nc.Block() as block:
                @block.sync
                def _(sp):
                    sp.dma_start(c_cur[:, :], a["ctx"][0]).then_inc(a_ctx, 16)
                    with sp.Fori(1, BATCH) as b:
                        sp.wait_ge(a_xt, b)
                        sp.dma_start(c_cur[:, None, :], a["ctx"][bass.ds(b, 1)].rearrange("b s d -> s b d")
                                     ).then_inc(a_ctx, 16)

                @block.tensor
                def _(pe):
                    pe_x(pe, 0, None)
                    pe_project(pe, 0, 0, 0)
                    pe_turn_qk(pe, 0)
                    pe_project(pe, 0, 1, 1)
                    pe_turn_qk(pe, 1)
                    pe_project(pe, 0, 2, 2)
                    over_batches(pe, pe_step)
                    pe_turn_p(pe, NS - 1)
                    pe_values(pe, KVH - 1, NS - 1, None)
                    pe_out(pe, BATCH - 1, KVH - 1, NS - 1)

                @block.scalar
                def _(act):
                    act_x(act, 0, 0)
                    act_copies(act, 0)
                    act_qk(act, 0, 0)
                    act_copies(act, 1)
                    act_qk(act, 1, 1)
                    act_copies(act, 2)
                    over_batches(act, act_step)
                    act.wait_ge(a_pt, NS)
                    act.wait_ge(a_pv, NS - 1)
                    act.activation(pT_hi[:, :, :], b_p[:, :, :], ACT.Copy).then_inc(a_phi, 1)
                    act.wait_ge(a_pv, NS)
                    act.wait_ge(a_wo, NS - 1)
                    act.activation(oT_hi[:, :], b_o[:, :], ACT.Copy).then_inc(a_ohi, 1)

                @block.vector
                def _(dve):
                    dve_x(dve, 0)
                    dve_rotate(dve, 0, 0)
                    dve_qk(dve, 0, 0)
                    dve_rotate(dve, 1, 1)
                    dve_qk(dve, 1, 1)
                    dve_rotate(dve, 2, 2)
                    over_batches(dve, dve_step)
                    dve.wait_ge(a_phi, NS)
                    dve.tensor_tensor(pT_lo[:, :, :], b_p[:, :, :], pT_hi[:, :, :].bitcast(F32),
                                      ALU.subtract).then_inc(a_plo, 1)
                    dve.wait_ge(a_ohi, NS)
                    dve.tensor_tensor(oT_lo[:, :], b_o[:, :], oT_hi[:, :].bitcast(F32),
                                      ALU.subtract).then_inc(a_olo, 1)
                    dve_tail(dve, BATCH - 1)
                    dve_tail2(dve, BATCH - 1)

                @block.gpsimd
                def _(pool):
                    pool.tensor_scalar(x_cur[:, :], x_tok[:, 0, :], 1.0, 0.0, ALU.mult, ALU.add).then_inc(a_xcur, 1)
                    pool.memset(mh[:, :], -0.5).then_inc(a_const, 1)
                    pool.wait_ge(a_const, 1)
                    for name, first in (("ss", KVH + 4), ("rec", KVH + 1), ("xt", 2), ("mv", 1)):
                        turn[name] = counter(pool, f"attn_{name}_turn", first)
                    for m in range(3):
                        pool_rotate(pool, m, m)
                    over_batches(pool, pool_step)
                    pool.wait_ge(a_mv, BATCH)
                    pool.tensor_scalar(ve[:, :], mv[:, 1:2], 1.0, LN_EPS, ALU.mult, ALU.add).then_inc(a_ve, 1)
                    pool.wait_ge(a_ve, BATCH)
                    pool.tensor_tensor(r1[:, :], ve[:, :], mh[:, 0:1], ALU.pow).then_inc(a_r1, 1)


def experts(nc, a, scope, ident, x_tok, out):
    NT = TOK // HALF
    with ExitStack() as layer:
        sb, ps, sem = scope(layer)
        x_hi = sb("x_hi", [P, KT, TOK], F32R)
        x_lo = sb("x_lo", [P, KT, TOK], F32R)
        comb = sb("comb", [P, BATCH, NE])
        gu_raw = [sb(f"gu_raw{i}", [P, 2, KT, FI]) for i in range(2)]
        dn_raw = [sb(f"dn_raw{i}", [P, IT, DM]) for i in range(2)]
        gu_hi = [sb(f"gu_hi{i}", [P, 2, KT, FI], F32R) for i in range(2)]
        gu_lo = [sb(f"gu_lo{i}", [P, 2, KT, FI], F32R) for i in range(2)]
        dn_hi = [sb(f"dn_hi{i}", [P, IT, DM], F32R) for i in range(2)]
        dn_lo = [sb(f"dn_lo{i}", [P, IT, DM], F32R) for i in range(2)]
        e_gu = [sem(f"e_gu{i}") for i in range(2)]
        e_dn = [sem(f"e_dn{i}") for i in range(2)]

        with ExitStack() as part:
            sb, ps, sem = scope(part)
            wr = sb("wr", [P, KT, E])
            x_f = sb("x_f", [P, KT, TOK])
            logit = sb("logit", [P, BATCH, E])
            eneg = sb("eneg", [P, BATCH, E])
            e1 = sb("e1", [P, BATCH, E])
            sc = sb("sc", [P, BATCH, E])
            rank = sb("rank", [P, E])
            m1 = sb("m1", [P, BATCH])
            q1 = sb("q1", [P, BATCH, E])
            k1 = sb("k1", [P, BATCH])
            sel1 = sb("sel1", [P, BATCH, E])
            sc2 = sb("sc2", [P, BATCH, E])
            m2 = sb("m2", [P, BATCH])
            q2 = sb("q2", [P, BATCH, E])
            k2 = sb("k2", [P, BATCH])
            sel2 = sb("sel2", [P, BATCH, E])
            sel = sb("sel", [P, BATCH, E])
            tot = sb("tot", [P, BATCH])
            inv = sb("inv", [P, BATCH])
            picked = sb("picked", [P, BATCH, E])
            eq1 = sb("eq1", [P, BATCH, E])
            eq2 = sb("eq2", [P, BATCH, E])
            bx = [ps(f"bx{i}", [P, 512]) for i in range(4)]
            bl = ps("bl", [P, 512])
            names = ("r_w", "r_t", "r_f", "r_hi", "r_lo", "r_l", "r_c", "r_e", "r_v")
            r_w, r_t, r_f, r_hi, r_lo, r_l, r_c, r_e, r_v = [sem(n) for n in names]
            with nc.Block() as block:
                @block.sync
                def _(sp):
                    sp.dma_start(wr[:, :, :], a["w_router"].rearrange("(k p) e -> p k e", p=P)).then_inc(r_w, 16)
                    sp.dma_start(rank[:, :], a["rank"]).then_inc(r_w, 16)
                    for i in range(2):
                        sp.dma_start(gu_raw[i][:, :, :, :], a["gu"][i].rearrange("s (k p) n -> p s k n", p=P)
                                     ).then_inc(e_gu[i], 16)
                        sp.dma_start(dn_raw[i][:, :, :], a["dn"][i].rearrange("(i p) n -> p i n", p=P)
                                     ).then_inc(e_dn[i], 16)

                @block.tensor
                def _(pe):
                    for q in range(4):
                        for k in range(KT):
                            for b in range(2):
                                mm = pe.transpose(bx[q][:, k * 256 + b * P:k * 256 + (b + 1) * P],
                                                  x_tok[:, 2 * q + b, k * P:(k + 1) * P], ident[:, :])
                        mm.then_inc(r_t, 1)
                    pe.wait_ge(r_w, 32)
                    for b in range(BATCH):
                        pe.wait_ge(r_f, b // 2 + 1)
                        for k in range(KT):
                            mm = pe.matmul(bl[:, b * E:(b + 1) * E], x_f[:, k, b * P:(b + 1) * P], wr[:, k, :],
                                           start=(k == 0), stop=(k == KT - 1))
                    mm.then_inc(r_l, 1)

                @block.scalar
                def _(act):
                    for q in range(4):
                        act.wait_ge(r_t, q + 1)
                        act.activation(x_f[:, :, q * 256:(q + 1) * 256], bx[q][:, :].rearrange("p (k t) -> p k t", k=KT),
                                       ACT.Copy).then_inc(r_f, 1)
                    act.wait_ge(r_c, 1)
                    act.activation(eneg[:, :, :], logit[:, :, :], ACT.Exp, scale=-1.0).then_inc(r_e, 1)

                @block.gpsimd
                def _(pool):
                    for q in range(4):
                        s = slice(q * 256, (q + 1) * 256)
                        pool.wait_ge(r_hi, q + 1)
                        pool.tensor_tensor(x_lo[:, :, s], x_f[:, :, s], x_hi[:, :, s].bitcast(F32),
                                           ALU.subtract).then_inc(r_lo, 1)

                @block.vector
                def _(dve):
                    count = [0]

                    def step(ins):
                        count[0] += 1
                        ins.then_inc(r_v, 1)
                        dve.wait_ge(r_v, count[0])

                    per_tok = lambda t: t[:, :, None].broadcast_to([P, BATCH, E])
                    for q in range(4):
                        s = slice(q * 256, (q + 1) * 256)
                        dve.wait_ge(r_f, q + 1)
                        dve.tensor_copy(x_hi[:, :, s], x_f[:, :, s]).then_inc(r_hi, 1)
                    dve.wait_ge(r_w, 32)
                    dve.wait_ge(r_l, 1)
                    dve.tensor_scalar(logit[:, :, :], bl[:, 0:BATCH * E].rearrange("p (b e) -> p b e", e=E), -87.0,
                                      None, ALU.max).then_inc(r_c, 1)
                    dve.wait_ge(r_e, 1)
                    ranks = rank[:, None, :].broadcast_to([P, BATCH, E])
                    step(dve.tensor_scalar(e1[:, :, :], eneg[:, :, :], 1.0, None, ALU.add))
                    step(dve.reciprocal(sc[:, :, :], e1[:, :, :]))
                    step(dve.tensor_reduce(m1[:, :], sc[:, :, :], AX_X, ALU.max))
                    step(dve.tensor_tensor(eq1[:, :, :], sc[:, :, :], per_tok(m1), ALU.is_equal))
                    step(dve.tensor_tensor(q1[:, :, :], eq1[:, :, :], ranks, ALU.mult))
                    step(dve.tensor_reduce(k1[:, :], q1[:, :, :], AX_X, ALU.max))
                    step(dve.tensor_tensor(sel1[:, :, :], q1[:, :, :], per_tok(k1), ALU.is_equal))
                    step(dve.scalar_tensor_tensor(sc2[:, :, :], sel1[:, :, :], -2.0, sc[:, :, :], ALU.mult, ALU.add))
                    step(dve.tensor_reduce(m2[:, :], sc2[:, :, :], AX_X, ALU.max))
                    step(dve.tensor_tensor(eq2[:, :, :], sc2[:, :, :], per_tok(m2), ALU.is_equal))
                    step(dve.tensor_tensor(q2[:, :, :], eq2[:, :, :], ranks, ALU.mult))
                    step(dve.tensor_reduce(k2[:, :], q2[:, :, :], AX_X, ALU.max))
                    step(dve.tensor_tensor(sel2[:, :, :], q2[:, :, :], per_tok(k2), ALU.is_equal))
                    step(dve.tensor_tensor(sel[:, :, :], sel1[:, :, :], sel2[:, :, :], ALU.add))
                    step(dve.tensor_tensor(tot[:, :], m1[:, :], m2[:, :], ALU.add))
                    step(dve.reciprocal(inv[:, :], tot[:, :]))
                    step(dve.tensor_tensor(picked[:, :, :], sel[:, :, :], sc[:, :, :], ALU.mult))
                    step(dve.tensor_tensor(comb[:, :, 0:E], picked[:, :, :], per_tok(inv), ALU.mult))
                    step(dve.memset(comb[:, :, E:NE], 1.0))

        with ExitStack() as part:
            sb, ps, sem = scope(part)
            accm = sb("accm", [P, BATCH, DM])
            sg = sb("sg", [P, 2, HALF])
            hf = sb("hf", [P, 2, HALF])
            h_hi = sb("eh_hi", [P, IT, HALF], F32R)
            h_lo = sb("eh_lo", [P, IT, HALF], F32R)
            stats = sb("fstats", [P, BATCH, 6])
            mv = sb("fmv", [P, BATCH, 2])
            ve = sb("fve", [P, BATCH])
            rstd = sb("frstd", [P, BATCH])
            mh = sb("fmh", [P, BATCH])
            y = sb("y", [P, BATCH, DM])
            bg = [ps(f"bg{i}", [P, 512]) for i in range(2)]
            bu = [ps(f"bu{i}", [P, 512]) for i in range(2)]
            bd = [ps(f"bd{i}", [P, 512]) for i in range(4)]
            w_gh = [sem(f"w_gh{i}") for i in range(2)]
            w_gl = [sem(f"w_gl{i}") for i in range(2)]
            w_dh = [sem(f"w_dh{i}") for i in range(2)]
            w_dl = [sem(f"w_dl{i}") for i in range(2)]
            names = ("f_mh", "f_g", "f_sg", "f_h", "f_hhi", "f_hlo", "f_d", "f_acc", "f_st", "f_mv",
                     "f_ve", "f_r", "f_y", "f_out")
            (f_mh, f_g, f_sg, f_h, f_hhi, f_hlo, f_d, f_acc, f_st, f_mv, f_ve, f_r, f_y, f_out) = [
                sem(n) for n in names]
            GU, DN = NT * IT, BATCH

            with nc.Block() as block:
                @block.sync
                def _(sp):
                    with sp.Fori(1, NE // 2) as r:
                        for c in range(2):
                            sp.wait_ge(w_gl[c], r)
                            sp.dma_start(gu_raw[c][:, :, :, :].rearrange("p s k n -> p (s k) n"),
                                         a["gu"][bass.ds(r * 2 + c, 1)].rearrange("e s (k p) n -> p (e s k) n", p=P)
                                         ).then_inc(e_gu[c], 16)
                            sp.wait_ge(w_dl[c], r)
                            sp.dma_start(dn_raw[c][:, :, :],
                                         a["dn"][bass.ds(r * 2 + c, 1)].rearrange("e (i p) n -> p (e i) n", p=P)
                                         ).then_inc(e_dn[c], 16)
                    for b in range(BATCH):
                        sp.wait_ge(f_y, b + 1)
                        sp.dma_start(out[b], y[:, b, :]).then_inc(f_out, 16)
                    sp.wait_ge(f_out, 16 * BATCH)

                @block.gpsimd
                def _(pool):
                    pool.memset(mh[:, :], -0.5).then_inc(f_mh, 1)
                    gu_turn = [counter(pool, f"gu_turn{c}", 16) for c in range(2)]
                    dn_turn = [counter(pool, f"dn_turn{c}", 16) for c in range(2)]
                    with pool.Fori(0, NE // 2) as e2:
                        for c in range(2):
                            pool.wait_ge(f_acc, (e2 * 2 + c) * DN)
                            wait_turn(pool, e_gu[c], gu_turn[c], 16)
                            gr, gh, gl = (t[:, :, :, :].rearrange("p s k n -> p (s k n)") for t in
                                          (gu_raw[c], gu_hi[c], gu_lo[c]))
                            pool.tensor_scalar(gh, gr, 1.0, 0.0, ALU.mult, ALU.add).then_inc(w_gh[c], 1)
                            pool.wait_ge(w_gh[c], e2 + 1)
                            pool.tensor_tensor(gl, gr, gh.bitcast(F32), ALU.subtract).then_inc(w_gl[c], 1)
                            wait_turn(pool, e_dn[c], dn_turn[c], 16)
                            dr, dh, dl = (t[:, :, :].rearrange("p i n -> p (i n)") for t in
                                          (dn_raw[c], dn_hi[c], dn_lo[c]))
                            pool.tensor_scalar(dh, dr, 1.0, 0.0, ALU.mult, ALU.add).then_inc(w_dh[c], 1)
                            pool.wait_ge(w_dh[c], e2 + 1)
                            pool.tensor_tensor(dl, dr, dh.bitcast(F32), ALU.subtract).then_inc(w_dl[c], 1)
                    pool.wait_ge(f_mh, 1)
                    pool.wait_ge(f_mv, BATCH)
                    pool.tensor_scalar(ve[:, :], mv[:, :, 1], 1.0, LN_EPS, ALU.mult, ALU.add).then_inc(f_ve, 1)
                    pool.wait_ge(f_ve, 1)
                    pool.tensor_tensor(rstd[:, :], ve[:, :], mh[:, :], ALU.pow).then_inc(f_r, 1)

                @block.tensor
                def _(pe):
                    with pe.Fori(0, NE // 2) as r:
                        for c in range(2):
                            e = r * 2 + c
                            for th in range(NT):
                                s = slice(th * HALF, (th + 1) * HALF)
                                if th == 0:
                                    pe.wait_ge(w_gl[c], r + 1)
                                for i in range(IT):
                                    step = e * GU + (th * IT + i)
                                    w = slice(i * P, (i + 1) * P)
                                    slot = (th * IT + i) % 2
                                    if th * IT + i >= 2:
                                        pe.wait_ge(f_h, step - 1)
                                    else:
                                        pe.wait_ge(f_h, e * GU)
                                    for dst, u in ((bg[slot], 0), (bu[slot], 1)):
                                        for k in range(KT):
                                            mm = products(pe, dst[:, :], (gu_hi[c][:, u, k, w], gu_lo[c][:, u, k, w]),
                                                          (x_hi[:, k, s], x_lo[:, k, s]), k == 0, k == KT - 1)
                                    mm.then_inc(f_g, 1)
                                if th == 0:
                                    pe.wait_ge(w_dl[c], r + 1)
                                pe.wait_ge(f_hlo, e * GU + (th + 1) * IT)
                                for t in range(4):
                                    ts = slice(t * P, (t + 1) * P)
                                    if th:
                                        pe.wait_ge(f_acc, (e + 1) * DN + (t + 1))
                                    else:
                                        pe.wait_ge(f_acc, (e + 1) * DN)
                                    for i in range(IT):
                                        mm = products(pe, bd[t][:, 0:DM], (h_hi[:, i, ts], h_lo[:, i, ts]),
                                                      (dn_hi[c][:, i, :], dn_lo[c][:, i, :]), i == 0, i == IT - 1)
                                    mm.then_inc(f_d, 1)

                @block.scalar
                def _(act):
                    with act.Fori(0, NE) as e:
                        for n in range(GU):
                            if n >= 2:
                                act.wait_ge(f_h, e * GU + (n - 1))
                            else:
                                act.wait_ge(f_h, e * GU)
                            act.wait_ge(f_g, e * GU + (n + 1))
                            act.activation(sg[:, n % 2, :], bg[n % 2][:, :], ACT.Silu).then_inc(f_sg, 1)
                            act.wait_ge(f_h, e * GU + (n + 1))
                            if n < IT:
                                act.wait_ge(f_d, e * DN)
                            else:
                                act.wait_ge(f_d, e * DN + 4)
                            act.activation(h_hi[:, n % IT, :], hf[:, n % 2, :], ACT.Copy).then_inc(f_hhi, 1)

                @block.vector
                def _(dve):
                    for b in range(BATCH):
                        dve.tensor_copy(accm[:, b, :], x_tok[:, b, :]).then_inc(f_acc, 1)
                    with dve.Fori(0, NE) as e:
                        for th in range(NT):
                            for i in range(IT):
                                n = th * IT + i
                                dve.wait_ge(f_sg, e * GU + (n + 1))
                                if n >= 2:
                                    dve.wait_ge(f_hlo, e * GU + (n - 1))
                                else:
                                    dve.wait_ge(f_hlo, e * GU)
                                dve.tensor_tensor(hf[:, n % 2, :], sg[:, n % 2, :], bu[n % 2][:, :],
                                                  ALU.mult).then_inc(f_h, 1)
                                dve.wait_ge(f_hhi, e * GU + (n + 1))
                                dve.tensor_tensor(h_lo[:, i, :], hf[:, n % 2, :], h_hi[:, i, :].bitcast(F32),
                                                  ALU.subtract).then_inc(f_hlo, 1)
                            for t in range(4):
                                b = th * 4 + t
                                dve.wait_ge(f_d, e * DN + (b + 1))
                                dve.wait_ge(f_acc, (e + 1) * DN)
                                dve.scalar_tensor_tensor(accm[:, b, :], bd[t][:, 0:DM],
                                                         comb[:, b, bass.ds(e, 1)], accm[:, b, :], ALU.mult,
                                                         ALU.add).then_inc(f_acc, 1)
                    for b in range(BATCH):
                        dve.wait_ge(f_acc, (NE + 1) * DN)
                        dve.bn_stats(stats[:, b, :], accm[:, b, :]).then_inc(f_st, 1)
                    for b in range(BATCH):
                        dve.wait_ge(f_st, b + 1)
                        dve.bn_aggr(mv[:, b, :], stats[:, b, :]).then_inc(f_mv, 1)
                    dve.wait_ge(f_r, 1)
                    for b in range(BATCH):
                        dve.tensor_scalar(y[:, b, :], accm[:, b, :], mv[:, b, 0:1], rstd[:, b:b + 1],
                                          ALU.subtract, ALU.mult).then_inc(f_y, 1)


def _host_arrays(inputs):
    f = lambda name: np.asarray(inputs[name])
    at, xa, ff = "L0_attn_", "L0_xattn_", "L0_ffn_"
    col = lambda v, n: np.ascontiguousarray(v.reshape(n, P).T)
    w = f(at + "in_proj_w")
    z, xr, bm, cm, dtr = (w[s:e] for s, e in ((0, 512), (512, 640), (640, 768), (768, 1280), (1280, 1288)))
    twice = lambda m: np.concatenate([m[0:HD], m[0:HD], m[HD:P], m[HD:P]])
    win = np.concatenate([z, cm, twice(bm), twice(xr), dtr, z[0:P - NH]])
    rows = lambda v: np.broadcast_to(v, (P,) + v.shape)
    kw, qw = f(xa + "k_norm_w"), f(xa + "q_norm_w")
    turned = lambda v: np.concatenate([v[AD // 2:], v[:AD // 2]])
    inv_freq = np.float32(1) / np.float32(10000.0) ** (np.arange(0, AD, 2, dtype=np.float32) / np.float32(AD))
    emb = np.outer(np.arange(SEQ, dtype=np.float32), np.concatenate([inv_freq, inv_freq]))
    sign = np.concatenate([-np.ones(AD // 2), np.ones(AD // 2)]).astype(np.float32)
    mask = np.zeros((P, MT * P), np.float32)
    mask[:, P:] = np.where(np.arange(P)[None, :] > np.arange(P)[:, None], np.float32(-2.0 ** 100), np.float32(0))
    kv = lambda k, v: np.concatenate([f(xa + k).reshape(DM, KVH, AD), f(xa + v).reshape(DM, KVH, AD)],
                                     axis=2).reshape(DM, KVH * 2 * AD)
    return {
        "x": f("x"), "ctx": f("ctx_2048"),
        "ident": np.eye(P, dtype=np.float32),
        "upper": np.triu(np.ones((P, P), np.float32)),
        "lower": np.tril(np.ones((P, P), np.float32), -1),
        "ln_w": col(f(at + "ln_w"), KT), "ln_b": col(f(at + "ln_b"), KT),
        "fc1_b": col(f(at + "fc1_b"), IT1), "fc2_b": rows(f(at + "fc2_b")),
        "dt_bias": f(at + "dt_bias").reshape(NH, 1),
        "A_log": np.broadcast_to(f(at + "A_log"), (P, BATCH, NH)),
        "Dp": col(np.repeat(f(at + "Dp"), HD), PAIRS), "norm_w": col(f(at + "norm_w"), PAIRS),
        "winT": win.T, "fc1T": f(at + "fc1_w").T, "fc2T": f(at + "fc2_w").T, "woutT": f(at + "out_proj_w").T,
        "wq": f(xa + "wq"), "wkv": np.stack([kv("wk", "wv"), kv("wk_ctx", "wv_ctx")]), "wo": f(xa + "wo"),
        "cos": np.cos(emb), "sin": np.sin(emb) * sign,
        "qw": rows(qw), "qwr": rows(turned(qw)), "kw": rows(kw), "kwr": rows(turned(kw)), "mask": mask,
        "w_router": f(ff + "w_router").T,
        "rank": rows(np.arange(E, 0, -1).astype(np.float32)),
        "gu": np.stack([np.concatenate([f(ff + "wg"), f(ff + "sg")]).transpose(0, 2, 1),
                        np.concatenate([f(ff + "wu"), f(ff + "su")]).transpose(0, 2, 1)], axis=1),
        "dn": np.concatenate([f(ff + "wd"), f(ff + "sd")]).transpose(0, 2, 1),
    }


def kernel(**inputs):
    import concourse.bacc as bacc
    from concourse.bass_utils import run_bass_kernel_spmd

    nc = bacc.Bacc("TRN2", target_bir_lowering=False, num_devices=1)
    arrays, args = {}, {}
    for name, v in _host_arrays(inputs).items():
        v = np.ascontiguousarray(v)
        arrays[f"in_{name}"] = v
        args[name] = nc.dram_tensor(f"in_{name}", v.shape, mybir.dt.from_np(v.dtype), kind="ExternalInput").ap()
    out = nc.dram_tensor("out_y", (BATCH, SEQ, DM), F32, kind="ExternalOutput").ap()
    decoder_layer(nc, args, out)
    r = run_bass_kernel_spmd(nc, [arrays], core_ids=[0])
    return r.results[0]["out_y"]
```

```python
from contextlib import ExitStack

import numpy as np

import concourse.bass as bass
from concourse import mybir

ALU = mybir.AluOpType
ACT = mybir.ActivationFunctionType
AX_X = mybir.AxisListType.X
F32 = mybir.dt.float32
F32R = mybir.dt.float32r

P = 128
BATCH, SEQ, DM = 8, 128, 256
TOK = BATCH * SEQ
KT = DM // P
HALF = 512

D_IN, HD, NH, NG = 512, 64, 8, 2
REP = NH // NG
PAIRS = NH // 2
INTER = 1024
IT1 = INTER // P
LN_EPS = 1e-5

AH, KVH, AD = 16, 4, 128
AREP = AH // KVH
MT = 2
RMS_EPS = 1e-6

E, NSH, FI = 8, 2, 640
NE = E + NSH
IT = FI // P

Z0, C0, B0, X0, DT0 = 0, 512, 1024, 1280, 1536
WIN = 1664
Z_T, C_T, B_T, X_T = 4, 4, 2, 2


def products(pe, out, lhs, rhs, first, last):
    (lh, ll), (rh, rl) = lhs, rhs
    pe.matmul(out, lh, rh, start=first, stop=False)
    pe.matmul(out, lh, rl, start=False, stop=False)
    return pe.matmul(out, ll, rh, start=False, stop=last)


def met(eng, sem):
    eng.wait_ge(sem, 1)


def counter(eng, name, first):
    turn = eng.alloc_register(name)
    eng.reg_mov(turn, first)
    return turn


def pool_wait(pool, sem, value, turn, step=1):
    if isinstance(value, int):
        pool.wait_ge(sem, value)
    else:
        pool.wait_ge(sem, turn)
        pool.reg_add(turn, turn, step)


def decoder_layer(nc, a, out):
    with ExitStack() as whole:
        dram = lambda name: a[name]

        def scope(ctx):
            sb = lambda name, shape, dt=F32: ctx.enter_context(nc.sbuf_tensor(name, shape, dt))
            ps = lambda name, shape: ctx.enter_context(nc.psum_tensor(name, shape, F32))
            given = []

            def sem(name):
                given.append(nc.alloc_semaphore(name=name))
                return given[-1]

            def give_back():
                if given:
                    nc.clear_and_free_semaphores(given)
                    nc.all_engine_barrier()

            ctx.callback(give_back)
            return sb, ps, sem

        sb, ps, sem = scope(whole)
        ident = sb("ident", [P, P])
        x_tok = sb("x_tok", [P, BATCH, DM])
        acc = sb("acc", [P, BATCH, DM])
        s_const = sem("s_const")
        s_x = sem("s_x")

        state_space_layer(nc, a, scope, ident, x_tok, acc, s_const, s_x)
        cross_attention(nc, a, scope, ident, x_tok)
        experts(nc, a, scope, ident, x_tok, out)


def state_space_layer(nc, a, scope, ident, x_tok, acc, s_const, s_x):
    with ExitStack() as layer:
        sb, ps, sem = scope(layer)
        h_hi = sb("h_hi", [P, KT, TOK], F32R)
        h_lo = sb("h_lo", [P, KT, TOK], F32R)
        win_hi = sb("win_hi", [P, KT, WIN], F32R)
        win_lo = sb("win_lo", [P, KT, WIN], F32R)
        dt = sb("dt", [P, BATCH, NH])
        dta = sb("dta", [P, BATCH, NH])
        wout = sb("wout", [P, PAIRS, DM])
        d_col = sb("d_col", [P, PAIRS])
        nw_col = sb("nw_col", [P, PAIRS])
        upper = sb("upper", [P, P])
        lower = sb("lower", [P, P])
        s_wout = sem("s_wout")

        with ExitStack() as part:
            sb, ps, sem = scope(part)
            win_raw = sb("win_raw", [P, KT, WIN])
            fc1_raw = sb("fc1_raw", [P, KT, INTER])
            fc2_raw = sb("fc2_raw", [P, IT1, DM])
            fc1_hi = sb("fc1_hi", [P, KT, INTER], F32R)
            fc1_lo = sb("fc1_lo", [P, KT, INTER], F32R)
            fc2_hi = sb("fc2_hi", [P, IT1, DM], F32R)
            fc2_lo = sb("fc2_lo", [P, IT1, DM], F32R)
            g_f = sb("g_f", [P, 2, HALF])
            g_hi = sb("g_hi", [P, IT1, HALF], F32R)
            g_lo = sb("g_lo", [P, IT1, HALF], F32R)
            stats = sb("stats", [P, BATCH, 6])
            mv = sb("mv", [P, BATCH, 2])
            veps = sb("veps", [P, BATCH])
            rstd = sb("rstd", [P, BATCH])
            mhalf = sb("mhalf", [P, BATCH])
            xhat = sb("xhat", [P, BATCH, DM])
            h_f = sb("h_f", [P, KT, TOK])
            x2b = sb("x2b", [P, BATCH, DM])
            fc2_bias = sb("fc2_bias", [P, DM])
            lnw = sb("lnw", [P, KT])
            lnb = sb("lnb", [P, KT])
            fc1b = sb("fc1b", [P, IT1])
            dtb = sb("dtb", [NH, 1])
            alog = sb("alog", [P, BATCH, NH])
            dt_row = sb("dt_row", [NH, TOK])
            sp_x = sb("sp_x", [P, BATCH, NH])
            sp_abs = sb("sp_abs", [P, BATCH, NH])
            sp_e = sb("sp_e", [P, BATCH, NH])
            sp_u = sb("sp_u", [P, BATCH, NH])
            sp_ln = sb("sp_ln", [P, BATCH, NH])
            sp_d = sb("sp_d", [P, BATCH, NH])
            sp_r = sb("sp_r", [P, BATCH, NH])
            sp_t = sb("sp_t", [P, BATCH, NH])
            sp_s = sb("sp_s", [P, BATCH, NH])
            ea = sb("ea", [P, BATCH, NH])
            bank = [ps(f"bank{i}", [P, 512]) for i in range(8)]

            s_small = sem("s_small")
            s_fc1 = sem("s_fc1")
            s_fc2 = sem("s_fc2")
            s_win = sem("s_win")
            s_fc2b = sem("s_fc2b")
            stats_ready = sem("stats_ready")
            mv_ready = sem("mv_ready")
            veps_ready = sem("veps_ready")
            mhalf_ready = sem("mhalf_ready")
            rstd_ready = sem("rstd_ready")
            xhat_ready = sem("xhat_ready")
            hT_ready = sem("hT_ready")
            hf_ready = sem("hf_ready")
            hhi_ready = sem("hhi_ready")
            hlo_ready = sem("hlo_ready")
            fc1hi_ready = sem("fc1hi_ready")
            fc1lo_ready = sem("fc1lo_ready")
            fc2hi_ready = sem("fc2hi_ready")
            fc2lo_ready = sem("fc2lo_ready")
            winhi_ready = sem("winhi_ready")
            winlo_ready = sem("winlo_ready")
            dtp_ready = sem("dtp_ready")
            dtrow_ready = sem("dtrow_ready")
            dtT_ready = sem("dtT_ready")
            sp = sem("sp")
            spa = sem("spa")
            dta_ready = sem("dta_ready")
            x2b_ready = sem("x2b_ready")
            x2_ready = sem("x2_ready")
            fc1_done = sem("fc1_done")
            gf_ready = sem("gf_ready")
            ghi_ready = sem("ghi_ready")
            glo_ready = sem("glo_ready")
            fc2_done = sem("fc2_done")
            acc_ready = sem("acc_ready")
            wout_ready = sem("wout_ready")

            SMALL = 6
            with nc.Block() as block:
                @block.sync
                def _(sp_):
                    xv = a["x"].rearrange("b s d -> s b d")
                    for q in range(4):
                        sp_.dma_start(x_tok[:, 2 * q:2 * q + 2, :], xv[:, 2 * q:2 * q + 2, :]).then_inc(s_x, 16)
                    sp_.dma_start(fc1_raw[:, :, :], a["fc1T"].rearrange("(k p) n -> p k n", p=P)).then_inc(s_fc1, 16)
                    sp_.dma_start(win_raw[:, :, :], a["winT"].rearrange("(k p) n -> p k n", p=P)).then_inc(s_win, 16)
                    sp_.dma_start(fc2_raw[:, :, :], a["fc2T"].rearrange("(k p) n -> p k n", p=P)).then_inc(s_fc2, 16)

                @block.scalar
                def _(act):
                    act.dma_start(ident[:, :], a["ident"]).then_inc(s_const, 16)
                    act.dma_start(lnw[:, :], a["ln_w"]).then_inc(s_small, 16)
                    act.dma_start(lnb[:, :], a["ln_b"]).then_inc(s_small, 16)
                    act.dma_start(fc1b[:, :], a["fc1_b"]).then_inc(s_small, 16)
                    act.dma_start(dtb[:, :], a["dt_bias"]).then_inc(s_small, 16)
                    act.dma_start(alog[:, :, :], a["A_log"]).then_inc(s_small, 16)
                    act.dma_start(nw_col[:, :], a["norm_w"]).then_inc(s_small, 16)
                    act.dma_start(fc2_bias[:, :], a["fc2_b"]).then_inc(s_fc2b, 16)
                    act.dma_start(d_col[:, :], a["Dp"]).then_inc(s_const, 16)
                    act.dma_start(upper[:, :], a["upper"]).then_inc(s_const, 16)
                    act.dma_start(lower[:, :], a["lower"]).then_inc(s_const, 16)
                    act.dma_start(wout[:, :, :], a["woutT"].rearrange("(k p) n -> p k n", p=P)).then_inc(s_wout, 16)
                    act.wait_ge(s_small, 16 * SMALL)
                    for g in range(BATCH // 2):
                        for k in range(KT):
                            act.wait_ge(hT_ready, 2 * g + k + 1)
                            act.activation(h_f[:, k, g * 256:(g + 1) * 256], bank[(2 * g + k) % 4][:, 0:256],
                                           ACT.Identity, bias=lnb[:, k:k + 1],
                                           scale=lnw[:, k:k + 1]).then_inc(hf_ready, 1)
                    for th in range(2):
                        act.wait_ge(dtp_ready, th + 1)
                        act.activation(dt_row[:, th * HALF:(th + 1) * HALF], bank[4 + th][0:NH, :], ACT.Identity,
                                       bias=dtb[:, 0:1]).then_inc(dtrow_ready, 1)
                    act.activation(ea[:, :, :], alog[:, :, :], ACT.Exp).then_inc(spa, 1)
                    act.wait_ge(sp, 2)
                    act.activation(sp_e[:, :, :], sp_abs[:, :, :], ACT.Exp, scale=-1.0).then_inc(spa, 1)
                    act.wait_ge(sp, 3)
                    act.activation(sp_ln[:, :, :], sp_u[:, :, :], ACT.Ln).then_inc(spa, 1)
                    for th in range(2):
                        for i in range(IT1):
                            act.wait_ge(fc1_done, th * IT1 + (i + 1))
                            if i < 2:
                                act.wait_ge(glo_ready, th * IT1)
                            else:
                                act.wait_ge(glo_ready, th * IT1 + (i - 1))
                            act.activation(g_f[:, i % 2, :], bank[i % 4][:, :], ACT.Gelu_apprx_tanh,
                                           bias=fc1b[:, i:i + 1]).then_inc(gf_ready, 1)

                @block.gpsimd
                def _(pool):
                    pool.memset(mhalf[:, :], -0.5).then_inc(mhalf_ready, 1)
                    pool.wait_ge(mhalf_ready, 1)
                    pool.wait_ge(mv_ready, BATCH)
                    pool.tensor_scalar(veps[:, :], mv[:, :, 1], 1.0, LN_EPS, ALU.mult,
                                       ALU.add).then_inc(veps_ready, 1)
                    pool.wait_ge(veps_ready, 1)
                    pool.tensor_tensor(rstd[:, :], veps[:, :], mhalf[:, :], ALU.pow).then_inc(rstd_ready, 1)
                    pool.wait_ge(s_win, 16)
                    for k in range(KT):
                        pool.tensor_scalar(win_hi[:, k, :], win_raw[:, k, :], 1.0, 0.0, ALU.mult,
                                           ALU.add).then_inc(winhi_ready, 1)
                        pool.wait_ge(winhi_ready, k + 1)
                        pool.tensor_tensor(win_lo[:, k, :], win_raw[:, k, :], win_hi[:, k, :].bitcast(F32),
                                           ALU.subtract).then_inc(winlo_ready, 1)
                    pool.wait_ge(s_fc2, 16)
                    for k in range(2):
                        s = slice(4 * k, 4 * k + 4)
                        pool.tensor_scalar(fc2_hi[:, s, :], fc2_raw[:, s, :], 1.0, 0.0, ALU.mult,
                                           ALU.add).then_inc(fc2hi_ready, 1)
                        pool.wait_ge(fc2hi_ready, k + 1)
                        pool.tensor_tensor(fc2_lo[:, s, :], fc2_raw[:, s, :], fc2_hi[:, s, :].bitcast(F32),
                                           ALU.subtract).then_inc(fc2lo_ready, 1)

                @block.vector
                def _(dve):
                    for b in range(BATCH):
                        dve.wait_ge(s_x, 16 * 4 if b >= 6 else 16 * 4)
                        dve.bn_stats(stats[:, b, :], x_tok[:, b, :]).then_inc(stats_ready, 1)
                    for b in range(BATCH):
                        dve.wait_ge(stats_ready, b + 1)
                        dve.bn_aggr(mv[:, b, :], stats[:, b, :]).then_inc(mv_ready, 1)
                    dve.wait_ge(rstd_ready, 1)
                    for b in range(BATCH):
                        dve.tensor_scalar(xhat[:, b, :], x_tok[:, b, :], mv[:, b, 0:1], rstd[:, b:b + 1],
                                          ALU.subtract, ALU.mult).then_inc(xhat_ready, 1)
                    dve.wait_ge(s_fc1, 16)
                    for k in range(KT):
                        dve.tensor_copy(fc1_hi[:, k, :], fc1_raw[:, k, :]).then_inc(fc1hi_ready, 1)
                        dve.wait_ge(fc1hi_ready, k + 1)
                        dve.tensor_tensor(fc1_lo[:, k, :], fc1_raw[:, k, :], fc1_hi[:, k, :].bitcast(F32),
                                          ALU.subtract).then_inc(fc1lo_ready, 1)
                    for g in range(BATCH // 2):
                        s = slice(g * 256, (g + 1) * 256)
                        dve.wait_ge(hf_ready, 2 * g + 2)
                        dve.tensor_copy(h_hi[:, :, s], h_f[:, :, s]).then_inc(hhi_ready, 1)
                        dve.wait_ge(hhi_ready, g + 1)
                        dve.tensor_tensor(h_lo[:, :, s], h_f[:, :, s], h_hi[:, :, s].bitcast(F32),
                                          ALU.subtract).then_inc(hlo_ready, 1)
                    dve.wait_ge(s_fc2b, 16)
                    dve.scalar_tensor_tensor(x2b[:, :, :], x_tok[:, :, :], 2.0,
                                             fc2_bias[:, None, :].broadcast_to([P, BATCH, DM]),
                                             ALU.mult, ALU.add).then_inc(x2b_ready, 1)
                    dve.wait_ge(s_wout, 16)
                    dve.wait_ge(s_small, 16 * SMALL)
                    for j in range(PAIRS):
                        dve.tensor_scalar(wout[:, j, :], wout[:, j, :], nw_col[:, j:j + 1], None,
                                          ALU.mult).then_inc(wout_ready, 1)
                    dve.wait_ge(dtT_ready, BATCH)
                    dve.tensor_copy(sp_x[:, :, :],
                                    bank[6][:, 0:BATCH * NH].rearrange("p (b h) -> p b h", b=BATCH)).then_inc(sp, 1)
                    dve.wait_ge(sp, 1)
                    dve.scalar_tensor_tensor(sp_abs[:, :, :], sp_x[:, :, :], -1.0, sp_x[:, :, :], ALU.mult,
                                             ALU.max).then_inc(sp, 1)
                    dve.wait_ge(spa, 2)
                    dve.tensor_scalar(sp_u[:, :, :], sp_e[:, :, :], 1.0, None, ALU.add).then_inc(sp, 1)
                    dve.wait_ge(sp, 3)
                    dve.scalar_tensor_tensor(sp_d[:, :, :], sp_u[:, :, :], -1.0, sp_e[:, :, :], ALU.add,
                                             ALU.subtract).then_inc(sp, 1)
                    dve.reciprocal(sp_r[:, :, :], sp_u[:, :, :]).then_inc(sp, 1)
                    dve.wait_ge(sp, 5)
                    dve.tensor_tensor(sp_t[:, :, :], sp_d[:, :, :], sp_r[:, :, :], ALU.mult).then_inc(sp, 1)
                    dve.wait_ge(spa, 3)
                    dve.wait_ge(sp, 6)
                    dve.tensor_tensor(sp_s[:, :, :], sp_ln[:, :, :], sp_t[:, :, :], ALU.subtract).then_inc(sp, 1)
                    dve.wait_ge(sp, 7)
                    dve.scalar_tensor_tensor(dt[:, :, :], sp_x[:, :, :], 0.0, sp_s[:, :, :], ALU.max,
                                             ALU.add).then_inc(sp, 1)
                    dve.wait_ge(sp, 8)
                    dve.scalar_tensor_tensor(dta[:, :, :], dt[:, :, :], -1.0, ea[:, :, :], ALU.mult,
                                             ALU.mult).then_inc(dta_ready, 1)
                    dve.wait_ge(x2b_ready, 1)
                    for th in range(2):
                        for i in range(IT1):
                            dve.wait_ge(gf_ready, th * IT1 + (i + 1))
                            dve.wait_ge(fc2_done, th * 4)
                            dve.tensor_copy(g_hi[:, i, :], g_f[:, i % 2, :]).then_inc(ghi_ready, 1)
                            dve.wait_ge(ghi_ready, th * IT1 + (i + 1))
                            dve.tensor_tensor(g_lo[:, i, :], g_f[:, i % 2, :], g_hi[:, i, :].bitcast(F32),
                                              ALU.subtract).then_inc(glo_ready, 1)
                        for t in range(4):
                            dve.wait_ge(fc2_done, th * 4 + (t + 1))
                            dve.tensor_tensor(acc[:, bass.ds(th * 4 + t, 1), :], bank[4 + t][:, 0:DM][:, None, :],
                                              x2b[:, bass.ds(th * 4 + t, 1), :], ALU.add).then_inc(acc_ready, 1)

                @block.tensor
                def _(pe):
                    pe.wait_ge(s_const, 64)
                    for g in range(BATCH // 2):
                        pe.wait_ge(xhat_ready, 2 * g + 2)
                        for k in range(KT):
                            if 2 * g + k >= 4:
                                pe.wait_ge(hf_ready, 2 * g + k - 3)
                            for b in range(2):
                                mm = pe.transpose(bank[(2 * g + k) % 4][:, b * P:(b + 1) * P],
                                                  xhat[:, 2 * g + b, k * P:(k + 1) * P], ident[:, :])
                            mm.then_inc(hT_ready, 1)
                    pe.wait_ge(winlo_ready, KT)
                    pe.wait_ge(hlo_ready, BATCH // 2)
                    for th in range(2):
                        s = slice(th * HALF, (th + 1) * HALF)
                        for k in range(KT):
                            w = slice(DT0, DT0 + P)
                            mm = products(pe, bank[4 + th][:, :], (win_hi[:, k, w], win_lo[:, k, w]),
                                          (h_hi[:, k, s], h_lo[:, k, s]), k == 0, k == KT - 1)
                        mm.then_inc(dtp_ready, 1)
                    pe.wait_ge(dtrow_ready, 2)
                    for b in range(BATCH):
                        pe.transpose(bank[6][:, b * NH:(b + 1) * NH], dt_row[:, b * P:(b + 1) * P],
                                     ident[0:NH, 0:NH]).then_inc(dtT_ready, 1)
                    pe.wait_ge(fc1lo_ready, KT)
                    pe.wait_ge(fc2lo_ready, 2)
                    pe.wait_ge(sp, 1)
                    for th in range(2):
                        tok = bass.ds(th * HALF, HALF)
                        for i in range(IT1):
                            if i < 4:
                                pe.wait_ge(gf_ready, th * IT1)
                            else:
                                pe.wait_ge(gf_ready, th * IT1 + (i - 3))
                            w = slice(i * P, (i + 1) * P)
                            for k in range(KT):
                                mm = products(pe, bank[i % 4][:, :], (fc1_hi[:, k, w], fc1_lo[:, k, w]),
                                              (h_hi[:, k, tok], h_lo[:, k, tok]), k == 0, k == KT - 1)
                            mm.then_inc(fc1_done, 1)
                        pe.wait_ge(glo_ready, th * IT1 + IT1)
                        pe.wait_ge(acc_ready, th * 4)
                        for t in range(4):
                            s = slice(t * P, (t + 1) * P)
                            for i in range(IT1):
                                mm = products(pe, bank[4 + t][:, 0:DM], (g_hi[:, i, s], g_lo[:, i, s]),
                                              (fc2_hi[:, i, :], fc2_lo[:, i, :]), i == 0, i == IT1 - 1)
                            mm.then_inc(fc2_done, 1)

        with ExitStack() as part:
            sb, ps, sem = scope(part)
            TW = 2 * P
            th_z = sb("th_z", [P, Z_T, TW])
            sz = sb("sz", [P, Z_T, TW])
            c_t = sb("c_t", [P, C_T, TW])
            b_t = sb("b_t", [P, B_T, TW])
            x_t = sb("x_t", [P, X_T, TW])
            xpad = sb("xpad", [P, NG, 2, P])
            tri = sb("tri", [P, NH, P])
            dec = sb("dec", [P, NH, P])
            decm = sb("decm", [P, NH, P])
            wts = sb("wts", [P, NH, P])
            yd = sb("yd", [P, PAIRS, P])
            yg = sb("yg", [P, PAIRS, P])
            sq = sb("sq", [P, PAIRS, P])
            sqs = sb("sqs", [P, P])
            ones = sb("ones", [P, 2])
            ve = sb("ve", [P, 1])
            ry = sb("ry", [P, 1])
            mh = sb("mh", [P, 1])
            pre = sb("pre", [P, DM])
            st = sb("st", [P, 6])
            mv2 = sb("mv2", [P, 2])
            ve2 = sb("ve2", [P, 1])
            r2 = sb("r2", [P, 1])
            bz = ps("bz", [P, 2, 512])
            bc = ps("bc", [P, 2, 512])
            bb = ps("bb", [P, 512])
            bx = ps("bx", [P, 512])
            b_out = ps("b_out", [P, 512])
            b_ss = ps("b_ss", [P, 512])

            names = ("m_const", "m_zp", "m_cp", "m_bp", "m_xp", "m_tanh", "m_sz", "m_c", "m_b", "m_x", "m_xt",
                     "m_xpad", "m_tri", "m_seg", "m_dec", "m_decm", "m_g", "m_w", "m_y", "m_yd", "m_yg", "m_sq",
                     "m_sqs", "m_ss", "m_ve", "m_ry", "m_out", "m_pre", "m_st", "m_mv", "m_ve2", "m_r2", "m_x1",
                     "m_ti")
            (m_const, m_zp, m_cp, m_bp, m_xp, m_tanh, m_sz, m_c, m_b, m_x, m_xt, m_xpad, m_tri, m_seg, m_dec,
             m_decm, m_g, m_w, m_y, m_yd, m_yg, m_sq, m_sqs, m_ss, m_ve, m_ry, m_out, m_pre, m_st, m_mv, m_ve2,
             m_r2, m_x1, m_ti) = [sem(n) for n in names]
            NPAIR = BATCH // 2

            with nc.Block() as block:
                @block.gpsimd
                def _(pool):
                    pool.memset(xpad[:, :, :, :], 0.0).then_inc(m_const, 1)
                    pool.memset(ones[:, :], 1.0).then_inc(m_const, 1)
                    pool.memset(mh[:, :], -0.5).then_inc(m_const, 1)
                    pool.wait_ge(m_const, 3)
                    dec_turn, mv_turn = counter(pool, "dec_turn", 3), counter(pool, "mv_turn", 3)
                    def pair(j):
                        for c in range(2):
                            n = j * 2 + c
                            pool.wait_ge(m_seg, n)
                            pool.tensor_tensor(tri[:, :, :], upper[:, None, :].broadcast_to([P, NH, P]),
                                               dta[:, bass.ds(n, 1), :].rearrange("p b h -> p (b h)")[:, :, None]
                                               .broadcast_to([P, NH, P]), ALU.mult).then_inc(m_tri, 1)
                            pool.wait_ge(m_w, n)
                            pool_wait(pool, m_dec, n + 1, dec_turn)
                            pool.affine_select(out=decm[:, :, :], in_=dec[:, :, :], pattern=[[0, NH], [1, P]],
                                               compare_op=ALU.is_ge, fill=0.0, base=0,
                                               channel_multiplier=-1).then_inc(m_decm, 1)
                            pool.wait_ge(m_ve, n + 1)
                            pool.wait_ge(m_pre, n)
                            pool.tensor_tensor(ry[:, :], ve[:, :], mh[:, :], ALU.pow).then_inc(m_ry, 1)
                            pool_wait(pool, m_mv, n + 1, mv_turn)
                            pool.tensor_scalar(ve2[:, :], mv2[:, 1:2], 1.0, LN_EPS, ALU.mult,
                                               ALU.add).then_inc(m_ve2, 1)
                            pool.wait_ge(m_ve2, n + 1)
                            pool.tensor_tensor(r2[:, :], ve2[:, :], mh[:, :], ALU.pow).then_inc(m_r2, 1)

                    pair(0)
                    with pool.Fori(1, NPAIR) as j:
                        pair(j)

                @block.scalar
                def _(act):
                    def pair(j):
                        act.wait_ge(m_yg, j * 2)
                        for q in range(2):
                            act.wait_ge(m_zp, j * 2 + (q + 1))
                            act.activation(th_z[:, 2 * q:2 * q + 2, :], bz[:, q, :].rearrange("p (a t) -> p a t", a=2),
                                           ACT.Tanh, scale=0.5).then_inc(m_tanh, 1)
                        act.wait_ge(m_g, j * 2)
                        for q in range(2):
                            act.wait_ge(m_cp, j * 2 + (q + 1))
                            act.activation(c_t[:, 2 * q:2 * q + 2, :], bc[:, q, :].rearrange("p (a t) -> p a t", a=2),
                                           ACT.Copy).then_inc(m_c, 1)
                        act.wait_ge(m_bp, j + 1)
                        act.activation(b_t[:, :, :], bb[:, :].rearrange("p (a t) -> p a t", a=2),
                                       ACT.Copy).then_inc(m_b, 1)
                        act.wait_ge(m_xp, j + 1)
                        act.wait_ge(m_yd, j * 2)
                        act.activation(x_t[:, :, :], bx[:, :].rearrange("p (a t) -> p a t", a=2),
                                       ACT.Copy).then_inc(m_x, 1)
                        for c in range(2):
                            n = j * 2 + c
                            act.wait_ge(m_seg, n + 1)
                            act.wait_ge(m_decm, n)
                            act.activation(dec[:, :, :], bz[:, :, :].rearrange("p a (h l) -> p (a h) l", l=P),
                                           ACT.Exp).then_inc(m_dec, 1)
                            act.wait_ge(m_yg, n + 1)
                            act.wait_ge(m_sqs, n)
                            act.activation(sq[:, :, :], yg[:, :, :], ACT.Square).then_inc(m_sq, 1)

                    pair(0)
                    with act.Fori(1, NPAIR) as j:
                        pair(j)

                @block.vector
                def _(dve):
                    dve.wait_ge(m_const, 3)
                    def pair(j):
                        for q in range(2):
                            dve.wait_ge(m_tanh, j * 2 + (q + 1))
                            dve.scalar_tensor_tensor(sz[:, 2 * q:2 * q + 2, :], th_z[:, 2 * q:2 * q + 2, :], 1.0,
                                                     bz[:, q, :].rearrange("p (a t) -> p a t", a=2), ALU.add,
                                                     ALU.mult).then_inc(m_sz, 1)
                        for c in range(2):
                            n = j * 2 + c
                            tk = slice(c * P, (c + 1) * P)
                            dve.wait_ge(m_xt, n + 1)
                            dve.wait_ge(m_y, n)
                            for o in range(2):
                                dve.tensor_copy(xpad[:, :, o, o * HD:(o + 1) * HD],
                                                bx[:, 0:2 * P].rearrange("p (g d) -> p g d", g=2)[:, :, 0:HD]
                                                ).then_inc(m_xpad, 1)
                            dve.wait_ge(m_decm, n + 1)
                            dve.wait_ge(m_g, n + 1)
                            for h in range(NH):
                                dve.scalar_tensor_tensor(
                                    wts[:, h, :], bc[:, h % 2, (h // 2) * P:(h // 2 + 1) * P],
                                    dt[:, bass.ds(n, 1), h:h + 1].rearrange("p b h -> p (b h)"),
                                    decm[:, h, :], ALU.mult, ALU.mult).then_inc(m_ti if h < NH - 1 else m_w, 1)
                            dve.wait_ge(m_y, n + 1)
                            dve.wait_ge(m_x, j + 1)
                            for i in range(PAIRS):
                                dve.scalar_tensor_tensor(yd[:, i, :], x_t[:, i // 2, tk], d_col[:, i:i + 1],
                                                         bb[:, i * P:(i + 1) * P], ALU.mult,
                                                         ALU.add).then_inc(m_ti if i < PAIRS - 1 else m_yd, 1)
                            dve.wait_ge(m_yd, n + 1)
                            dve.wait_ge(m_ti, n * 10 + 10)
                            dve.wait_ge(m_sz, j * 2 + 2)
                            dve.wait_ge(m_out, n)
                            dve.wait_ge(m_sq, n)
                            dve.tensor_tensor(yg[:, :, :], yd[:, :, :], sz[:, :, tk], ALU.mult).then_inc(m_yg, 1)
                            dve.wait_ge(m_sq, n + 1)
                            dve.wait_ge(m_ss, n)
                            dve.tensor_reduce(sqs[:, :], sq[:, :, :].rearrange("p i l -> p l i"), AX_X,
                                              ALU.add).then_inc(m_sqs, 1)
                            dve.wait_ge(m_ss, n + 1)
                            dve.wait_ge(m_ry, n)
                            dve.tensor_scalar(ve[:, :], b_ss[:, 0:1], 1.0 / D_IN, 4 * LN_EPS, ALU.mult,
                                              ALU.add).then_inc(m_ve, 1)
                            dve.wait_ge(m_ry, n + 1)
                            dve.wait_ge(m_out, n + 1)
                            dve.wait_ge(m_x1, n)
                            dve.scalar_tensor_tensor(pre[:, None, :], b_out[:, None, 0:DM], ry[:, 0:1],
                                                     acc[:, bass.ds(n, 1), :], ALU.mult, ALU.add).then_inc(m_pre, 1)
                            dve.wait_ge(m_pre, n + 1)
                            dve.bn_stats(st[:, :], pre[:, :]).then_inc(m_st, 1)
                            met(dve, m_const)
                            dve.wait_ge(m_st, n + 1)
                            dve.wait_ge(m_ve2, n)
                            dve.bn_aggr(mv2[:, :], st[:, :]).then_inc(m_mv, 1)
                            dve.wait_ge(m_mv, n + 1)
                            dve.wait_ge(m_r2, n + 1)
                            dve.tensor_scalar(x_tok[:, bass.ds(n, 1), :], pre[:, None, :], mv2[:, 0:1], r2[:, 0:1],
                                              ALU.subtract, ALU.mult).then_inc(m_x1, 1)

                    pair(0)
                    with dve.Fori(1, NPAIR) as j:
                        pair(j)

                @block.tensor
                def _(pe):
                    pe.wait_ge(m_const, 3)
                    def pair(j):
                        tok = bass.ds(j * TW, TW)

                        def project(dst, col):
                            for k in range(KT):
                                w = slice(col, col + P)
                                mm = products(pe, dst, (win_hi[:, k, w], win_lo[:, k, w]),
                                              (h_hi[:, k, tok], h_lo[:, k, tok]), k == 0, k == KT - 1)
                            return mm

                        pe.wait_ge(m_dec, j * 2)
                        for q in range(2):
                            for i in range(2):
                                mm = project(bz[:, q, i * TW:(i + 1) * TW], Z0 + (2 * q + i) * P)
                            mm.then_inc(m_zp, 1)
                        pe.wait_ge(m_yd, j * 2)
                        for i in range(2):
                            mm = project(bb[:, i * TW:(i + 1) * TW], B0 + i * P)
                        mm.then_inc(m_bp, 1)
                        pe.wait_ge(m_xpad, j * 4)
                        for i in range(2):
                            mm = project(bx[:, i * TW:(i + 1) * TW], X0 + i * P)
                        mm.then_inc(m_xp, 1)
                        pe.wait_ge(m_w, j * 2)
                        for q in range(2):
                            for i in range(2):
                                mm = project(bc[:, q, i * TW:(i + 1) * TW], C0 + (2 * q + i) * P)
                            mm.then_inc(m_cp, 1)
                        for c in range(2):
                            n = j * 2 + c
                            tk = slice(c * P, (c + 1) * P)
                            pe.wait_ge(m_x, j + 1)
                            if c:
                                pe.wait_ge(m_xpad, j * 4 + 2)
                            for g in range(NG):
                                mm = pe.transpose(bx[:, g * P:(g + 1) * P], x_t[:, g, tk], ident[:, :])
                            mm.then_inc(m_xt, 1)
                            pe.wait_ge(m_tri, n + 1)
                            if c:
                                pe.wait_ge(m_dec, j * 2 + 1)
                            pe.wait_ge(m_sz, j * 2 + 2)
                            for q in range(2):
                                mm = pe.matmul(bz[:, q, :], lower[:, :],
                                               tri[:, 4 * q:4 * q + 4, :].rearrange("p h l -> p (h l)"),
                                               start=True, stop=True)
                            mm.then_inc(m_seg, 1)
                            pe.wait_ge(m_b, j + 1)
                            pe.wait_ge(m_c, j * 2 + 2)
                            if c:
                                pe.wait_ge(m_w, j * 2 + 1)
                            for h in range(NH):
                                r = slice((h % 2) * HD, (h % 2 + 1) * HD)
                                mm = pe.matmul(bc[:, h % 2, (h // 2) * P:(h // 2 + 1) * P], b_t[r, h // REP, tk],
                                               c_t[r, h // 2, tk], start=True, stop=True)
                            mm.then_inc(m_g, 1)
                            pe.wait_ge(m_w, n + 1)
                            pe.wait_ge(m_ti, n * 10 + 7)
                            pe.wait_ge(m_xpad, n * 2 + 2)
                            if c:
                                pe.wait_ge(m_yd, j * 2 + 1)
                            for h in range(NH):
                                mm = pe.matmul(bb[:, (h // 2) * P:(h // 2 + 1) * P], xpad[:, h // REP, h % 2, :],
                                               wts[:, h, :], start=(h % 2 == 0), stop=(h % 2 == 1))
                            mm.then_inc(m_y, 1)
                            pe.wait_ge(m_yg, n + 1)
                            pe.wait_ge(m_pre, n)
                            for i in range(PAIRS):
                                mm = pe.matmul(b_out[:, 0:DM], yg[:, i, :], wout[:, i, :], start=(i == 0),
                                               stop=(i == PAIRS - 1))
                            mm.then_inc(m_out, 1)
                            pe.wait_ge(m_sqs, n + 1)
                            pe.wait_ge(m_ve, n)
                            pe.matmul(b_ss[:, 0:2], sqs[:, :], ones[:, :], start=True, stop=True).then_inc(m_ss, 1)

                    pair(0)
                    with pe.Fori(1, NPAIR) as j:
                        pair(j)

def cross_attention(nc, a, scope, ident, x_tok):
    NS = BATCH * KVH
    QW = AREP * AD
    MW = MT * P
    with ExitStack() as layer:
        sb, ps, sem = scope(layer)
        wq_hi = sb("wq_hi", [P, KT, KVH, QW], F32R)
        wq_lo = sb("wq_lo", [P, KT, KVH, QW], F32R)
        wkv_hi = sb("wkv_hi", [P, 2, KT, KVH, 2 * AD], F32R)
        wkv_lo = sb("wkv_lo", [P, 2, KT, KVH, 2 * AD], F32R)
        wo_hi = sb("wo_hi", [P, AH, DM], F32R)
        wo_lo = sb("wo_lo", [P, AH, DM], F32R)
        cq = sb("cq", [P, AD])
        sq_ = sb("sq_", [P, AD])
        ck = sb("ck", [P, AD])
        sk = sb("sk", [P, AD])
        kw = sb("kw", [P, AD])
        kw_c = sb("kw_c", [P, AD])
        mask = sb("mask", [P, MW], F32R)
        ident_r = sb("ident_r", [P, P], F32R)

        with ExitStack() as part:
            sb, ps, sem = scope(part)
            wq_raw = sb("wq_raw", [P, KT, KVH, QW])
            wkv_raw = sb("wkv_raw", [P, 2, KT, KVH, 2 * AD])
            wo_raw = sb("wo_raw", [P, AH, DM])
            cos = sb("cos", [P, AD])
            sin = sb("sin", [P, AD])
            qw = sb("qw", [P, AD])
            qwr = sb("qwr", [P, AD])
            kwr = sb("kwr", [P, AD])
            mask_raw = sb("mask_raw", [P, MW])
            w_q, w_kv, w_o, w_small, w_kw = [sem(n) for n in ("w_q", "w_kv", "w_o", "w_small", "w_kw")]
            w_hi = [sem(f"w_hi{i}") for i in range(3)]
            w_lo = [sem(f"w_lo{i}") for i in range(3)]
            w_tab = sem("w_tab")
            with nc.Block() as block:
                @block.sync
                def _(sp):
                    sp.dma_start(wq_raw[:, :, :, :].rearrange("p k g n -> p k (g n)"),
                                 a["wq"].rearrange("(k p) n -> p k n", p=P)).then_inc(w_q, 16)
                    sp.dma_start(wkv_raw[:, :, :, :, :].rearrange("p s k g n -> p s k (g n)"),
                                 a["wkv"].rearrange("s (k p) n -> p s k n", p=P)).then_inc(w_kv, 16)
                    sp.dma_start(wo_raw[:, :, :], a["wo"].rearrange("(h p) n -> p h n", p=P)).then_inc(w_o, 16)

                @block.scalar
                def _(act):
                    for t, name in ((cos, "cos"), (sin, "sin"), (qw, "qw"), (qwr, "qwr"), (kwr, "kwr"),
                                    (mask_raw, "mask")):
                        act.dma_start(t[:, :], a[name]).then_inc(w_small, 16)
                    act.dma_start(kw[:, :], a["kw"]).then_inc(w_kw, 16)
                    act.wait_ge(w_q, 16)
                    act.activation(wq_hi[:, :, :, :], wq_raw[:, :, :, :], ACT.Copy).then_inc(w_hi[0], 1)
                    act.wait_ge(w_kv, 16)
                    act.activation(wkv_hi[:, :, :, :, :].rearrange("p s k g n -> p (s k g n)"),
                                   wkv_raw[:, :, :, :, :].rearrange("p s k g n -> p (s k g n)"),
                                   ACT.Copy).then_inc(w_hi[1], 1)
                    act.wait_ge(w_o, 16)
                    act.activation(wo_hi[:, :, :], wo_raw[:, :, :], ACT.Copy).then_inc(w_hi[2], 1)

                def low(eng, lo, raw, hi, i):
                    eng.wait_ge(w_hi[i], 1)
                    eng.tensor_tensor(lo, raw, hi.bitcast(F32), ALU.subtract).then_inc(w_lo[i], 1)

                @block.vector
                def _(dve):
                    dve.wait_ge(w_small, 16 * 6)
                    dve.wait_ge(w_kw, 16)
                    dve.tensor_tensor(cq[:, :], cos[:, :], qw[:, :], ALU.mult).then_inc(w_tab, 1)
                    dve.tensor_tensor(sq_[:, :], sin[:, :], qwr[:, :], ALU.mult).then_inc(w_tab, 1)
                    dve.tensor_tensor(ck[:, :], cos[:, :], kw[:, :], ALU.mult).then_inc(w_tab, 1)
                    dve.tensor_tensor(sk[:, :], sin[:, :], kwr[:, :], ALU.mult).then_inc(w_tab, 1)
                    dve.tensor_scalar(kw_c[:, :], kw[:, :], float(AD) ** 0.5, None, ALU.mult).then_inc(w_tab, 1)
                    dve.tensor_copy(mask[:, :], mask_raw[:, :]).then_inc(w_tab, 1)
                    dve.tensor_copy(ident_r[:, :], ident[:, :]).then_inc(w_tab, 1)
                    flat = lambda t: t[:, :, :, :].rearrange("p k g n -> p (k g n)")
                    low(dve, flat(wq_lo), flat(wq_raw), flat(wq_hi), 0)
                    flat3 = lambda t: t[:, :, :].rearrange("p h n -> p (h n)")
                    low(dve, flat3(wo_lo), flat3(wo_raw), flat3(wo_hi), 2)

                @block.gpsimd
                def _(pool):
                    flat = lambda t: t[:, :, :, :, :].rearrange("p s k g n -> p (s k g n)")
                    low(pool, flat(wkv_lo), flat(wkv_raw), flat(wkv_hi), 1)

        with ExitStack() as part:
            sb, ps, sem = scope(part)
            x_cur = sb("x_cur", [P, DM])
            c_cur = sb("c_cur", [P, DM])
            xT_hi = sb("xT_hi", [P, 2, KT, P], F32R)
            xT_lo = sb("xT_lo", [P, 2, KT, P], F32R)
            q_s = sb("q_s", [P, 2, AREP, AD])
            kv_s = sb("kv_s", [P, 2, 2, 2, AD])
            sqr = sb("sqr", [P, 2, AREP + 2, AD])
            ss = sb("ss", [P, AREP + 2])
            sse = sb("sse", [P, AREP + 2])
            rs = sb("rs", [P, KVH, AREP + 2])
            mh = sb("mh6", [P, AREP + 2])
            t1 = sb("t1", [P, 2, AREP, AD])
            t2 = sb("t2", [P, 2, AREP, AD])
            u1 = sb("u1", [P, AD])
            u2 = sb("u2", [P, AD])
            u3 = sb("u3", [P, AD])
            q_r = sb("q_r", [P, AREP, AD])
            k_r = sb("k_r", [P, 2, AD])
            qT_hi = sb("qT_hi", [P, KVH, QW], F32R)
            qT_lo = sb("qT_lo", [P, KVH, QW], F32R)
            kT_hi = sb("kT_hi", [P, KVH, MW], F32R)
            kT_lo = sb("kT_lo", [P, KVH, MW], F32R)
            v_hi = sb("v_hi", [P, KVH, 2, AD], F32R)
            v_lo = sb("v_lo", [P, KVH, 2, AD], F32R)
            mx = sb("mx", [P, AREP])
            nb = sb("nb", [P, AREP])
            prob = sb("prob", [P, 2, AREP, MW])
            den = sb("den", [P, AREP])
            rec = sb("rec", [P, AREP])
            pT_hi = sb("pT_hi", [P, MT, QW], F32R)
            pT_lo = sb("pT_lo", [P, MT, QW], F32R)
            oT_hi = sb("oT_hi", [P, QW], F32R)
            oT_lo = sb("oT_lo", [P, QW], F32R)
            pre = sb("pre2", [P, DM])
            st = sb("st2", [P, 6])
            mv = sb("mvx", [P, 2])
            ve = sb("vex", [P, 1])
            r1 = sb("r1x", [P, 1])
            b_s = ps("b_s", [P, 2, 512])
            b_p = ps("b_p", [P, 2, 512])
            b_o = ps("b_o", [P, 512])
            b_q = ps("b_q", [P, 512])
            b_kv = ps("b_kv", [P, 512])
            b_w = ps("b_w", [P, 512])

            names = ("a_const", "a_xcur", "a_ctx", "a_xt", "a_xhi", "a_xlo", "a_pj", "a_qs", "a_kvs", "a_sqr", "a_ss",
                     "a_sse", "a_rs", "a_t", "a_qr", "a_u", "a_kr", "a_vhi", "a_vlo", "a_qt", "a_qhi", "a_qlo",
                     "a_khi", "a_klo", "a_s", "a_mx", "a_nb", "a_exp", "a_rec", "a_prob", "a_pt", "a_phi", "a_plo",
                     "a_pv", "a_ohi", "a_olo", "a_wo", "a_pre", "a_st", "a_mv", "a_ve", "a_r1", "a_x2")
            (a_const, a_xcur, a_ctx, a_xt, a_xhi, a_xlo, a_pj, a_qs, a_kvs, a_sqr, a_ss, a_sse, a_rs, a_t, a_qr,
             a_u, a_kr, a_vhi, a_vlo, a_qt, a_qhi, a_qlo, a_khi, a_klo, a_s, a_mx, a_nb, a_exp, a_rec, a_prob,
             a_pt, a_phi, a_plo, a_pv, a_ohi, a_olo, a_wo, a_pre, a_st, a_mv, a_ve, a_r1, a_x2) = [
                sem(n) for n in names]

            def pe_x(pe, b, n):
                pe.wait_ge(a_xcur, b + 1)
                pe.wait_ge(a_ctx, b * 16 + 16)
                if n is not None:
                    pe.wait_ge(a_plo, n - 1)
                for s, t in ((0, x_cur), (1, c_cur)):
                    for k in range(KT):
                        mm = pe.transpose(b_p[:, 0, (2 * s + k) * P:(2 * s + k + 1) * P], t[:, k * P:(k + 1) * P],
                                          ident[:, :])
                mm.then_inc(a_xt, 1)

            def pe_project(pe, b, g, m):
                pe.wait_ge(a_xlo, b + 1)
                if not (isinstance(m, int) and m < 1):
                    pe.wait_ge(a_qlo, max(m - 1, 1) if isinstance(m, int) else m - 1)
                    pe.wait_ge(a_klo, max(m - 1, 1) if isinstance(m, int) else m - 1)
                if isinstance(m, int) and m == 2:
                    pe.wait_ge(a_qs, m)
                    pe.wait_ge(a_kvs, m)
                for k in range(KT):
                    products(pe, b_q[:, :], (xT_hi[:, 0, k, :], xT_lo[:, 0, k, :]),
                             (wq_hi[:, k, g, :], wq_lo[:, k, g, :]), k == 0, k == KT - 1)
                for s in range(2):
                    for k in range(KT):
                        mm = products(pe, b_kv[:, s * 256:(s + 1) * 256], (xT_hi[:, s, k, :], xT_lo[:, s, k, :]),
                                      (wkv_hi[:, s, k, g, :], wkv_lo[:, s, k, g, :]), k == 0, k == KT - 1)
                mm.then_inc(a_pj, 1)

            def pe_turn_qk(pe, m):
                pe.wait_ge(a_qr, m + 1)
                pe.wait_ge(a_kr, m * 2 + 2)
                out_ = m + 2 if not isinstance(m, int) else min(m + 2, NS) if m else 1
                pe.wait_ge(a_qs, out_)
                pe.wait_ge(a_kvs, out_)
                for h in range(AREP):
                    pe.transpose(b_q[:, h * P:(h + 1) * P], q_r[:, h, :], ident[:, :])
                for s in range(2):
                    mm = pe.transpose(b_kv[:, s * P:(s + 1) * P], k_r[:, s, :], ident[:, :])
                mm.then_inc(a_qt, 1)

            def pe_scores(pe, g, n):
                pe.wait_ge(a_qlo, n + 1)
                pe.wait_ge(a_klo, n + 1)
                pe.wait_ge(a_exp, n * AREP)
                for h in range(AREP):
                    o = b_s[:, h // 2, (h % 2) * MW:(h % 2 + 1) * MW]
                    hs = slice(h * P, (h + 1) * P)
                    products(pe, o, (qT_hi[:, g, hs], qT_lo[:, g, hs]), (kT_hi[:, g, :], kT_lo[:, g, :]), True, False)
                    mm = pe.matmul(o, ident_r[:, :], mask[:, :], start=False, stop=True)
                    if h % 2:
                        mm.then_inc(a_s, 1)

            def pe_turn_p(pe, g, n, xt):
                pe.wait_ge(a_prob, n * AREP + AREP)
                pe.wait_ge(a_plo, n)
                if xt is not None:
                    pe.wait_ge(a_xlo, xt + 1)
                for t in range(MT):
                    for h in range(AREP):
                        mm = pe.transpose(b_p[:, t, h * P:(h + 1) * P], prob[:, g % 2, h, t * P:(t + 1) * P],
                                          ident[:, :])
                mm.then_inc(a_pt, 1)

            def pe_values(pe, g, n):
                pe.wait_ge(a_plo, n + 1)
                pe.wait_ge(a_vlo, n + 1)
                pe.wait_ge(a_olo, n)
                for t in range(MT):
                    mm = products(pe, b_o[:, :], (v_hi[:, g, 1 - t, :], v_lo[:, g, 1 - t, :]),
                                  (pT_hi[:, t, :], pT_lo[:, t, :]), t == 0, t == MT - 1)
                mm.then_inc(a_pv, 1)

            def pe_out(pe, b, g, n):
                pe.wait_ge(a_olo, n + 1)
                if g == 0:
                    pe.wait_ge(a_pre, b)
                for h in range(AREP):
                    hs = slice(h * P, (h + 1) * P)
                    mm = products(pe, b_w[:, 0:DM], (oT_hi[:, hs], oT_lo[:, hs]),
                                  (wo_hi[:, g * AREP + h, :], wo_lo[:, g * AREP + h, :]),
                                  g == 0 and h == 0, g == KVH - 1 and h == AREP - 1)
                mm.then_inc(a_wo, 1)

            def pe_step(pe, b, g, first, last):
                n = b * KVH + g
                prev, prev2 = not (first and g == 0), not (first and g < 2)
                x_ahead = g == 1 and not last
                if x_ahead:
                    pe_x(pe, b + 1, n)
                if not (last and g == KVH - 1):
                    pe_turn_qk(pe, n + 1)
                pe_scores(pe, g, n)
                if prev2:
                    pe_out(pe, b if g >= 2 else b - 1, (g + 2) % KVH, n - 2)
                if prev:
                    pe_turn_p(pe, (g + 3) % KVH, n - 1, b + 1 if x_ahead else None)
                if not (last and g >= 1):
                    pe_project(pe, b if g == 0 else b + 1, (g + 3) % KVH, n + 3)
                if prev:
                    pe_values(pe, (g + 3) % KVH, n - 1)

            def act_x(act, b, m):
                act.wait_ge(a_xt, b + 1)
                act.wait_ge(a_pj, m)
                act.activation(xT_hi[:, :, :, :].rearrange("p s k t -> p (s k t)"), b_p[:, 0, :],
                               ACT.Copy).then_inc(a_xhi, 1)

            def act_copies(act, g, m):
                c = g % 2
                early = isinstance(m, int) and m < 2
                act.wait_ge(a_pj, m + 1)
                if not early:
                    act.wait_ge(a_t, (m - 1) * 3)
                act.activation(q_s[:, c, :, :].rearrange("p h d -> p (h d)"), b_q[:, :], ACT.Copy).then_inc(a_qs, 1)
                if not early:
                    act.wait_ge(a_kr, (m - 1) * 2)
                    act.wait_ge(a_vlo, m - 1)
                act.activation(kv_s[:, c, :, :, :].rearrange("p s c d -> p (s c d)"), b_kv[:, :],
                               ACT.Copy).then_inc(a_kvs, 1)
                act.wait_ge(a_qs, m + 1)
                if not early:
                    act.wait_ge(a_ss, m - 1)
                act.activation(sqr[:, c, 0:AREP, :], q_s[:, c, :, :], ACT.Square).then_inc(a_sqr, 1)
                act.wait_ge(a_kvs, m + 1)
                act.activation(sqr[:, c, AREP:AREP + 2, :], kv_s[:, c, :, 0, :], ACT.Square).then_inc(a_sqr, 1)

            def act_qk(act, g, m):
                act.wait_ge(a_qt, m + 1)
                act.activation(qT_hi[:, g, :], b_q[:, :], ACT.Copy).then_inc(a_qhi, 1)
                act.activation(kT_hi[:, g, :], b_kv[:, 0:MW], ACT.Copy).then_inc(a_khi, 1)

            def act_exp(act, g, n):
                if not (isinstance(n, int) and n < 2):
                    act.wait_ge(a_pt, n - 1)
                act.wait_ge(a_rec, n)
                for h in range(AREP):
                    if h % 2 == 0:
                        act.wait_ge(a_nb, n * 2 + (h // 2 + 1))
                    act.activation(prob[:, g % 2, h, :], b_s[:, h // 2, (h % 2) * MW:(h % 2 + 1) * MW], ACT.Exp,
                                   bias=nb[:, h:h + 1], scale=rs[:, g, h:h + 1],
                                   accum_out=den[:, h:h + 1]).then_inc(a_exp, 1)

            def act_p(act, n):
                act.wait_ge(a_pt, n + 1)
                act.wait_ge(a_pv, n)
                act.activation(pT_hi[:, :, :], b_p[:, :, :], ACT.Copy).then_inc(a_phi, 1)

            def act_o(act, n):
                act.wait_ge(a_pv, n + 1)
                act.wait_ge(a_wo, n)
                act.activation(oT_hi[:, :], b_o[:, :], ACT.Copy).then_inc(a_ohi, 1)

            def act_step(act, b, g, first, last):
                n = b * KVH + g
                if not (first and g < 2):
                    act_o(act, n - 2)
                if g == 1 and not last:
                    act_x(act, b + 1, n + 3)
                if not (last and g == KVH - 1):
                    act_qk(act, (g + 1) % KVH, n + 1)
                act_exp(act, g, n)
                if not (first and g == 0):
                    act_p(act, n - 1)
                if not (last and g >= 1):
                    act_copies(act, (g + 3) % KVH, n + 3)

            def dve_x(dve, b):
                dve.wait_ge(a_xhi, b + 1)
                dve.tensor_tensor(xT_lo[:, :, :, :].rearrange("p s k t -> p (s k t)"), b_p[:, 0, :],
                                  xT_hi[:, :, :, :].rearrange("p s k t -> p (s k t)").bitcast(F32),
                                  ALU.subtract).then_inc(a_xlo, 1)

            def dve_rotate(dve, g, m):
                hd = AD // 2
                heads = lambda t: t[:, None, :].broadcast_to([P, AREP, AD])
                half = lambda t, o: t[:, None, o:o + hd].broadcast_to([P, AREP, hd])
                c = g % 2
                dve.wait_ge(a_qs, m + 1)
                if not (isinstance(m, int) and m < 2):
                    dve.wait_ge(a_qr, m - 1)
                dve.tensor_tensor(t2[:, c, :, 0:hd], q_s[:, c, :, hd:AD], half(sq_, 0), ALU.mult).then_inc(a_t, 1)
                dve.tensor_tensor(t2[:, c, :, hd:AD], q_s[:, c, :, 0:hd], half(sq_, hd), ALU.mult).then_inc(a_t, 1)
                dve.tensor_tensor(t1[:, c, :, :], q_s[:, c, :, :], heads(cq), ALU.mult).then_inc(a_t, 1)

            def dve_squares(dve, g, m):
                c = g % 2
                dve.wait_ge(a_sqr, m * 2 + 2)
                dve.wait_ge(a_sse, m)
                dve.tensor_reduce(ss[:, :], sqr[:, c, :, :], AX_X, ALU.add).then_inc(a_ss, 1)

            def dve_v(dve, g, m):
                dve.wait_ge(a_kvs, m + 1)
                if not (isinstance(m, int) and m < KVH):
                    dve.wait_ge(a_pv, m - (KVH - 1))
                dve.tensor_copy(v_hi[:, g, :, :], kv_s[:, g % 2, :, 1, :]).then_inc(a_vhi, 1)

            def dve_k(dve, g, m):
                c = g % 2
                dve.wait_ge(a_rs, m + 1)
                dve.wait_ge(a_u, m * 4 + 4)
                dve.wait_ge(a_qt, m)
                dve.tensor_scalar(k_r[:, 1, :], u3[:, :], rs[:, g, AREP:AREP + 1], float(AD) ** 0.5, ALU.mult,
                                  ALU.mult).then_inc(a_kr, 1)
                dve.scalar_tensor_tensor(k_r[:, 0, :], kv_s[:, c, 1, 0, :], rs[:, g, AREP + 1:AREP + 2], kw_c[:, :],
                                         ALU.mult, ALU.mult).then_inc(a_kr, 1)

            def dve_qk(dve, g, m):
                dve.wait_ge(a_qhi, m + 1)
                dve.tensor_tensor(qT_lo[:, g, :], b_q[:, :], qT_hi[:, g, :].bitcast(F32),
                                  ALU.subtract).then_inc(a_qlo, 1)
                dve.wait_ge(a_khi, m + 1)
                dve.tensor_tensor(kT_lo[:, g, :], b_kv[:, 0:MW], kT_hi[:, g, :].bitcast(F32),
                                  ALU.subtract).then_inc(a_klo, 1)

            def dve_max(dve, g, n):
                dve.wait_ge(a_exp, n * AREP)
                for q in range(2):
                    hs = slice(2 * q, 2 * q + 2)
                    dve.wait_ge(a_s, n * 2 + (q + 1))
                    dve.tensor_reduce(mx[:, hs], b_s[:, q, :].rearrange("p (h m) -> p h m", h=2), AX_X,
                                      ALU.max).then_inc(a_mx, 1)
                    dve.wait_ge(a_mx, n * 2 + (q + 1))
                    dve.scalar_tensor_tensor(nb[:, hs], mx[:, hs], -1.0, rs[:, g, hs], ALU.mult,
                                             ALU.mult).then_inc(a_nb, 1)

            def dve_tail(dve, b):
                dve.wait_ge(a_wo, b * KVH + KVH)
                dve.tensor_tensor(pre[:, None, :], b_w[:, None, 0:DM], x_tok[:, bass.ds(b, 1), :],
                                  ALU.add).then_inc(a_pre, 1)
                dve.wait_ge(a_pre, b + 1)
                dve.bn_stats(st[:, :], pre[:, :]).then_inc(a_st, 1)
                met(dve, a_const)
                dve.wait_ge(a_st, b + 1)
                dve.bn_aggr(mv[:, :], st[:, :]).then_inc(a_mv, 1)

            def dve_tail2(dve, b):
                dve.wait_ge(a_r1, b + 1)
                dve.wait_ge(a_mv, b + 1)
                dve.tensor_scalar(x_tok[:, bass.ds(b, 1), :], pre[:, None, :], mv[:, 0:1], r1[:, 0:1],
                                  ALU.subtract, ALU.mult).then_inc(a_x2, 1)

            def dve_step(dve, b, g, first, last):
                n = b * KVH + g
                ahead2 = not (last and g >= 2)
                if ahead2:
                    dve_rotate(dve, (g + 2) % KVH, n + 2)
                if g == 1 and not last:
                    dve_x(dve, b + 1)
                if not (first and g < 2):
                    dve_o(dve, n - 2)
                dve_max(dve, g, n)
                if not (last and g == KVH - 1):
                    dve_qk(dve, (g + 1) % KVH, n + 1)
                if ahead2:
                    dve_v(dve, (g + 2) % KVH, n + 2)
                if ahead2:
                    dve_squares(dve, (g + 2) % KVH, n + 2)
                if g == 1 and not first:
                    dve_tail(dve, b - 1)
                dve.wait_ge(a_exp, n * AREP + AREP)
                dve.wait_ge(a_prob, n * AREP)
                dve.reciprocal(rec[:, :], den[:, :]).then_inc(a_rec, 1)
                if not (first and g == 0):
                    dve_p(dve, n - 1)
                if ahead2:
                    dve_k(dve, (g + 2) % KVH, n + 2)
                if g == 2 and not first:
                    dve_tail2(dve, b - 1)

            def dve_p(dve, n):
                dve.wait_ge(a_phi, n + 1)
                dve.tensor_tensor(pT_lo[:, :, :], b_p[:, :, :], pT_hi[:, :, :].bitcast(F32),
                                  ALU.subtract).then_inc(a_plo, 1)

            def dve_o(dve, n):
                dve.wait_ge(a_ohi, n + 1)
                dve.tensor_tensor(oT_lo[:, :], b_o[:, :], oT_hi[:, :].bitcast(F32),
                                  ALU.subtract).then_inc(a_olo, 1)

            turn = {}

            def pool_kv(pool, g, m):
                hd, c = AD // 2, g % 2
                pool.wait_ge(a_kvs, m + 1)
                pool.wait_ge(a_kr, m * 2)
                pool.tensor_tensor(u1[:, :], kv_s[:, c, 0, 0, :], ck[:, :], ALU.mult).then_inc(a_u, 1)
                pool.tensor_tensor(u2[:, 0:hd], kv_s[:, c, 0, 0, hd:AD], sk[:, 0:hd], ALU.mult).then_inc(a_u, 1)
                pool.tensor_tensor(u2[:, hd:AD], kv_s[:, c, 0, 0, 0:hd], sk[:, hd:AD], ALU.mult).then_inc(a_u, 1)
                pool.wait_ge(a_u, m * 4 + 3)
                pool.tensor_tensor(u3[:, :], u1[:, :], u2[:, :], ALU.add).then_inc(a_u, 1)
                pool.wait_ge(a_vhi, m + 1)
                pool.tensor_tensor(v_lo[:, g, :, :], kv_s[:, c, :, 1, :], v_hi[:, g, :, :].bitcast(F32),
                                   ALU.subtract).then_inc(a_vlo, 1)

            def pool_rotate(pool, g, m):
                pool_wait(pool, a_ss, m + 1, turn.get("ss"))
                pool.tensor_scalar(sse[:, :], ss[:, :], 1.0, AD * RMS_EPS, ALU.mult, ALU.add).then_inc(a_sse, 1)
                pool.wait_ge(a_sse, m + 1)
                pool.tensor_tensor(rs[:, g, :], sse[:, :], mh[:, :], ALU.pow).then_inc(a_rs, 1)

            def pool_q(pool, g, m):
                pool.wait_ge(a_t, m * 3 + 3)
                pool.wait_ge(a_qt, m)
                pool.tensor_tensor(q_r[:, :, :], t1[:, g % 2, :, :], t2[:, g % 2, :, :], ALU.add).then_inc(a_qr, 1)

            def pool_step(pool, b, g, first, last):
                n = b * KVH + g
                if g == 0 and not last:
                    pool_wait(pool, a_xt, b + 1, turn.get("xt"))
                    pool.tensor_copy(x_cur[:, None, :], x_tok[:, bass.ds(b + 1, 1), :]).then_inc(a_xcur, 1)
                if not (last and g >= 2):
                    pool_kv(pool, (g + 2) % KVH, n + 2)
                    pool_rotate(pool, (g + 2) % KVH, n + 2)
                    pool_q(pool, (g + 2) % KVH, n + 2)
                pool_wait(pool, a_rec, n + 1, turn.get("rec"))
                for h in range(AREP):
                    pool.tensor_scalar(prob[:, g % 2, h, :], prob[:, g % 2, h, :], rec[:, h:h + 1], 1.0, ALU.mult,
                                       ALU.mult).then_inc(a_prob, 1)
                if g == 1 and not first:
                    pool_wait(pool, a_mv, b, turn.get("mv"))
                    pool.tensor_scalar(ve[:, :], mv[:, 1:2], 1.0, LN_EPS, ALU.mult, ALU.add).then_inc(a_ve, 1)
                    pool.wait_ge(a_ve, b)
                    pool.tensor_tensor(r1[:, :], ve[:, :], mh[:, 0:1], ALU.pow).then_inc(a_r1, 1)

            def over_batches(eng, step):
                for g in range(KVH):
                    step(eng, 0, g, True, False)
                with eng.Fori(1, BATCH - 1) as b:
                    for g in range(KVH):
                        step(eng, b, g, False, False)
                for g in range(KVH):
                    step(eng, BATCH - 1, g, False, True)

            with nc.Block() as block:
                @block.sync
                def _(sp):
                    sp.dma_start(c_cur[:, :], a["ctx"][0]).then_inc(a_ctx, 16)
                    with sp.Fori(1, BATCH) as b:
                        sp.wait_ge(a_xt, b)
                        sp.dma_start(c_cur[:, None, :], a["ctx"][bass.ds(b, 1)].rearrange("b s d -> s b d")
                                     ).then_inc(a_ctx, 16)

                @block.tensor
                def _(pe):
                    pe_x(pe, 0, None)
                    pe_project(pe, 0, 0, 0)
                    pe_turn_qk(pe, 0)
                    pe_project(pe, 0, 1, 1)
                    pe_project(pe, 0, 2, 2)
                    over_batches(pe, pe_step)
                    pe_out(pe, BATCH - 1, KVH - 2, NS - 2)
                    pe_turn_p(pe, KVH - 1, NS - 1, None)
                    pe_values(pe, KVH - 1, NS - 1)
                    pe_out(pe, BATCH - 1, KVH - 1, NS - 1)

                @block.scalar
                def _(act):
                    act_x(act, 0, 0)
                    act_copies(act, 0, 0)
                    act_qk(act, 0, 0)
                    act_copies(act, 1, 1)
                    act_copies(act, 2, 2)
                    over_batches(act, act_step)
                    act_o(act, NS - 2)
                    act_p(act, NS - 1)
                    act_o(act, NS - 1)

                @block.vector
                def _(dve):
                    dve_x(dve, 0)
                    dve_rotate(dve, 0, 0)
                    dve_squares(dve, 0, 0)
                    dve_v(dve, 0, 0)
                    dve_k(dve, 0, 0)
                    dve_qk(dve, 0, 0)
                    dve_rotate(dve, 1, 1)
                    dve_squares(dve, 1, 1)
                    dve_v(dve, 1, 1)
                    dve_k(dve, 1, 1)
                    over_batches(dve, dve_step)
                    dve_o(dve, NS - 2)
                    dve_p(dve, NS - 1)
                    dve_o(dve, NS - 1)
                    dve_tail(dve, BATCH - 1)
                    dve_tail2(dve, BATCH - 1)

                @block.gpsimd
                def _(pool):
                    pool.tensor_scalar(x_cur[:, :], x_tok[:, 0, :], 1.0, 0.0, ALU.mult, ALU.add).then_inc(a_xcur, 1)
                    pool.memset(mh[:, :], -0.5).then_inc(a_const, 1)
                    pool.wait_ge(a_const, 1)
                    for name, first in (("ss", KVH + 3), ("rec", KVH + 1), ("xt", 2), ("mv", 1)):
                        turn[name] = counter(pool, f"attn_{name}_turn", first)
                    for m in range(2):
                        pool_kv(pool, m, m)
                        pool_rotate(pool, m, m)
                        pool_q(pool, m, m)
                    over_batches(pool, pool_step)
                    pool.wait_ge(a_mv, BATCH)
                    pool.tensor_scalar(ve[:, :], mv[:, 1:2], 1.0, LN_EPS, ALU.mult, ALU.add).then_inc(a_ve, 1)
                    pool.wait_ge(a_ve, BATCH)
                    pool.tensor_tensor(r1[:, :], ve[:, :], mh[:, 0:1], ALU.pow).then_inc(a_r1, 1)


def experts(nc, a, scope, ident, x_tok, out):
    NT = TOK // HALF
    with ExitStack() as layer:
        sb, ps, sem = scope(layer)
        x_hi = sb("x_hi", [P, KT, TOK], F32R)
        x_lo = sb("x_lo", [P, KT, TOK], F32R)
        comb = sb("comb", [P, BATCH, NE])
        gu_raw = [sb(f"gu_raw{i}", [P, 2, KT, FI]) for i in range(2)]
        dn_raw = [sb(f"dn_raw{i}", [P, IT, DM]) for i in range(2)]
        gu_hi = [sb(f"gu_hi{i}", [P, 2, KT, FI], F32R) for i in range(2)]
        gu_lo = [sb(f"gu_lo{i}", [P, 2, KT, FI], F32R) for i in range(2)]
        dn_hi = [sb(f"dn_hi{i}", [P, IT, DM], F32R) for i in range(2)]
        dn_lo = [sb(f"dn_lo{i}", [P, IT, DM], F32R) for i in range(2)]
        e_gu = [sem(f"e_gu{i}") for i in range(2)]
        e_dn = [sem(f"e_dn{i}") for i in range(2)]

        with ExitStack() as part:
            sb, ps, sem = scope(part)
            wr = sb("wr", [P, KT, E])
            x_f = sb("x_f", [P, KT, TOK])
            logit = sb("logit", [P, BATCH, E])
            eneg = sb("eneg", [P, BATCH, E])
            e1 = sb("e1", [P, BATCH, E])
            sc = sb("sc", [P, BATCH, E])
            rank = sb("rank", [P, E])
            m1 = sb("m1", [P, BATCH])
            q1 = sb("q1", [P, BATCH, E])
            k1 = sb("k1", [P, BATCH])
            sel1 = sb("sel1", [P, BATCH, E])
            sc2 = sb("sc2", [P, BATCH, E])
            m2 = sb("m2", [P, BATCH])
            q2 = sb("q2", [P, BATCH, E])
            k2 = sb("k2", [P, BATCH])
            sel2 = sb("sel2", [P, BATCH, E])
            sel = sb("sel", [P, BATCH, E])
            tot = sb("tot", [P, BATCH])
            inv = sb("inv", [P, BATCH])
            picked = sb("picked", [P, BATCH, E])
            eq1 = sb("eq1", [P, BATCH, E])
            eq2 = sb("eq2", [P, BATCH, E])
            bx = [ps(f"bx{i}", [P, 512]) for i in range(4)]
            bl = ps("bl", [P, 512])
            names = ("r_w", "r_t", "r_f", "r_hi", "r_lo", "r_l", "r_c", "r_e", "r_v")
            r_w, r_t, r_f, r_hi, r_lo, r_l, r_c, r_e, r_v = [sem(n) for n in names]
            with nc.Block() as block:
                @block.sync
                def _(sp):
                    sp.dma_start(wr[:, :, :], a["w_router"].rearrange("(k p) e -> p k e", p=P)).then_inc(r_w, 16)
                    sp.dma_start(rank[:, :], a["rank"]).then_inc(r_w, 16)
                    for i in range(2):
                        sp.dma_start(gu_raw[i][:, :, :, :], a["gu"][i].rearrange("s (k p) n -> p s k n", p=P)
                                     ).then_inc(e_gu[i], 16)
                        sp.dma_start(dn_raw[i][:, :, :], a["dn"][i].rearrange("(i p) n -> p i n", p=P)
                                     ).then_inc(e_dn[i], 16)

                @block.tensor
                def _(pe):
                    for q in range(4):
                        for k in range(KT):
                            for b in range(2):
                                mm = pe.transpose(bx[q][:, k * 256 + b * P:k * 256 + (b + 1) * P],
                                                  x_tok[:, 2 * q + b, k * P:(k + 1) * P], ident[:, :])
                        mm.then_inc(r_t, 1)
                    pe.wait_ge(r_w, 32)
                    for b in range(BATCH):
                        pe.wait_ge(r_f, b // 2 + 1)
                        for k in range(KT):
                            mm = pe.matmul(bl[:, b * E:(b + 1) * E], x_f[:, k, b * P:(b + 1) * P], wr[:, k, :],
                                           start=(k == 0), stop=(k == KT - 1))
                    mm.then_inc(r_l, 1)

                @block.scalar
                def _(act):
                    for q in range(4):
                        act.wait_ge(r_t, q + 1)
                        act.activation(x_f[:, :, q * 256:(q + 1) * 256], bx[q][:, :].rearrange("p (k t) -> p k t", k=KT),
                                       ACT.Copy).then_inc(r_f, 1)
                    act.wait_ge(r_c, 1)
                    act.activation(eneg[:, :, :], logit[:, :, :], ACT.Exp, scale=-1.0).then_inc(r_e, 1)

                @block.gpsimd
                def _(pool):
                    for q in range(4):
                        s = slice(q * 256, (q + 1) * 256)
                        pool.wait_ge(r_hi, q + 1)
                        pool.tensor_tensor(x_lo[:, :, s], x_f[:, :, s], x_hi[:, :, s].bitcast(F32),
                                           ALU.subtract).then_inc(r_lo, 1)

                @block.vector
                def _(dve):
                    count = [0]

                    def step(ins):
                        count[0] += 1
                        ins.then_inc(r_v, 1)
                        dve.wait_ge(r_v, count[0])

                    per_tok = lambda t: t[:, :, None].broadcast_to([P, BATCH, E])
                    for q in range(4):
                        s = slice(q * 256, (q + 1) * 256)
                        dve.wait_ge(r_f, q + 1)
                        dve.tensor_copy(x_hi[:, :, s], x_f[:, :, s]).then_inc(r_hi, 1)
                    dve.wait_ge(r_w, 32)
                    dve.wait_ge(r_l, 1)
                    dve.tensor_scalar(logit[:, :, :], bl[:, 0:BATCH * E].rearrange("p (b e) -> p b e", e=E), -87.0,
                                      None, ALU.max).then_inc(r_c, 1)
                    dve.wait_ge(r_e, 1)
                    ranks = rank[:, None, :].broadcast_to([P, BATCH, E])
                    step(dve.tensor_scalar(e1[:, :, :], eneg[:, :, :], 1.0, None, ALU.add))
                    step(dve.reciprocal(sc[:, :, :], e1[:, :, :]))
                    step(dve.tensor_reduce(m1[:, :], sc[:, :, :], AX_X, ALU.max))
                    step(dve.tensor_tensor(eq1[:, :, :], sc[:, :, :], per_tok(m1), ALU.is_equal))
                    step(dve.tensor_tensor(q1[:, :, :], eq1[:, :, :], ranks, ALU.mult))
                    step(dve.tensor_reduce(k1[:, :], q1[:, :, :], AX_X, ALU.max))
                    step(dve.tensor_tensor(sel1[:, :, :], q1[:, :, :], per_tok(k1), ALU.is_equal))
                    step(dve.scalar_tensor_tensor(sc2[:, :, :], sel1[:, :, :], -2.0, sc[:, :, :], ALU.mult, ALU.add))
                    step(dve.tensor_reduce(m2[:, :], sc2[:, :, :], AX_X, ALU.max))
                    step(dve.tensor_tensor(eq2[:, :, :], sc2[:, :, :], per_tok(m2), ALU.is_equal))
                    step(dve.tensor_tensor(q2[:, :, :], eq2[:, :, :], ranks, ALU.mult))
                    step(dve.tensor_reduce(k2[:, :], q2[:, :, :], AX_X, ALU.max))
                    step(dve.tensor_tensor(sel2[:, :, :], q2[:, :, :], per_tok(k2), ALU.is_equal))
                    step(dve.tensor_tensor(sel[:, :, :], sel1[:, :, :], sel2[:, :, :], ALU.add))
                    step(dve.tensor_tensor(tot[:, :], m1[:, :], m2[:, :], ALU.add))
                    step(dve.reciprocal(inv[:, :], tot[:, :]))
                    step(dve.tensor_tensor(picked[:, :, :], sel[:, :, :], sc[:, :, :], ALU.mult))
                    step(dve.tensor_tensor(comb[:, :, 0:E], picked[:, :, :], per_tok(inv), ALU.mult))
                    step(dve.memset(comb[:, :, E:NE], 1.0))

        with ExitStack() as part:
            sb, ps, sem = scope(part)
            accm = sb("accm", [P, BATCH, DM])
            sg = sb("sg", [P, 2, HALF])
            hf = sb("hf", [P, 2, HALF])
            h_hi = sb("eh_hi", [P, NT, IT, HALF], F32R)
            h_lo = sb("eh_lo", [P, NT, IT, HALF], F32R)
            stats = sb("fstats", [P, BATCH, 6])
            mv = sb("fmv", [P, BATCH, 2])
            ve = sb("fve", [P, BATCH])
            rstd = sb("frstd", [P, BATCH])
            mh = sb("fmh", [P, BATCH])
            y = sb("y", [P, BATCH, DM])
            bg = [ps(f"bg{i}", [P, 512]) for i in range(2)]
            bu = [ps(f"bu{i}", [P, 512]) for i in range(2)]
            bd = [ps(f"bd{i}", [P, 512]) for i in range(4)]
            w_gh = [sem(f"w_gh{i}") for i in range(2)]
            w_gl = [sem(f"w_gl{i}") for i in range(2)]
            w_dh = [sem(f"w_dh{i}") for i in range(2)]
            w_dl = [sem(f"w_dl{i}") for i in range(2)]
            names = ("f_mh", "f_g", "f_sg", "f_h", "f_hhi", "f_hlo", "f_d", "f_acc", "f_st", "f_mv",
                     "f_ve", "f_r", "f_y", "f_out")
            (f_mh, f_g, f_sg, f_h, f_hhi, f_hlo, f_d, f_acc, f_st, f_mv, f_ve, f_r, f_y, f_out) = [
                sem(n) for n in names]
            GU, DN = NT * IT, BATCH

            with nc.Block() as block:
                @block.sync
                def _(sp):
                    with sp.Fori(1, NE // 2) as r:
                        for c in range(2):
                            sp.wait_ge(w_gl[c], r)
                            sp.dma_start(gu_raw[c][:, :, :, :].rearrange("p s k n -> p (s k) n"),
                                         a["gu"][bass.ds(r * 2 + c, 1)].rearrange("e s (k p) n -> p (e s k) n", p=P)
                                         ).then_inc(e_gu[c], 16)
                            sp.wait_ge(w_dl[c], r)
                            sp.dma_start(dn_raw[c][:, :, :],
                                         a["dn"][bass.ds(r * 2 + c, 1)].rearrange("e (i p) n -> p (e i) n", p=P)
                                         ).then_inc(e_dn[c], 16)
                    for b in range(BATCH):
                        sp.wait_ge(f_y, b + 1)
                        sp.dma_start(out[b], y[:, b, :]).then_inc(f_out, 16)
                    sp.wait_ge(f_out, 16 * BATCH)

                @block.gpsimd
                def _(pool):
                    pool.memset(mh[:, :], -0.5).then_inc(f_mh, 1)
                    def split(r, c):
                        pool.wait_ge(f_acc, (r * 2 + c) * DN)
                        pool_wait(pool, e_gu[c], r * 16 + 16, gu_turn[c], 16)
                        gr, gh, gl = (t[:, :, :, :].rearrange("p s k n -> p (s k n)") for t in
                                      (gu_raw[c], gu_hi[c], gu_lo[c]))
                        pool.tensor_scalar(gh, gr, 1.0, 0.0, ALU.mult, ALU.add).then_inc(w_gh[c], 1)
                        pool.wait_ge(w_gh[c], r + 1)
                        pool.tensor_tensor(gl, gr, gh.bitcast(F32), ALU.subtract).then_inc(w_gl[c], 1)
                        pool_wait(pool, e_dn[c], r * 16 + 16, dn_turn[c], 16)
                        dr, dh, dl = (t[:, :, :].rearrange("p i n -> p (i n)") for t in
                                      (dn_raw[c], dn_hi[c], dn_lo[c]))
                        pool.tensor_scalar(dh, dr, 1.0, 0.0, ALU.mult, ALU.add).then_inc(w_dh[c], 1)
                        pool.wait_ge(w_dh[c], r + 1)
                        pool.tensor_tensor(dl, dr, dh.bitcast(F32), ALU.subtract).then_inc(w_dl[c], 1)

                    gu_turn = [counter(pool, f"gu_turn{c}", 32) for c in range(2)]
                    dn_turn = [counter(pool, f"dn_turn{c}", 32) for c in range(2)]
                    for c in range(2):
                        split(0, c)
                    with pool.Fori(1, NE // 2) as r:
                        for c in range(2):
                            split(r, c)
                    pool.wait_ge(f_mh, 1)
                    pool.wait_ge(f_mv, BATCH)
                    pool.tensor_scalar(ve[:, :], mv[:, :, 1], 1.0, LN_EPS, ALU.mult, ALU.add).then_inc(f_ve, 1)
                    pool.wait_ge(f_ve, 1)
                    pool.tensor_tensor(rstd[:, :], ve[:, :], mh[:, :], ALU.pow).then_inc(f_r, 1)

                @block.tensor
                def _(pe):
                    def gate_up(e, c, th, i):
                        step, slot = e * GU + (th * IT + i), (th * IT + i) % 2
                        s, w = slice(th * HALF, (th + 1) * HALF), slice(i * P, (i + 1) * P)
                        if not (isinstance(step, int) and step < 2):
                            pe.wait_ge(f_h, step - 1)
                        for dst, u in ((bg[slot], 0), (bu[slot], 1)):
                            for k in range(KT):
                                mm = products(pe, dst[:, :], (gu_hi[c][:, u, k, w], gu_lo[c][:, u, k, w]),
                                              (x_hi[:, k, s], x_lo[:, k, s]), k == 0, k == KT - 1)
                        mm.then_inc(f_g, 1)

                    def down(e, r, c, th):
                        pe.wait_ge(w_dl[c], r + 1)
                        pe.wait_ge(f_hlo, e * GU + (th + 1) * IT)
                        for t in range(4):
                            ts = slice(t * P, (t + 1) * P)
                            pe.wait_ge(f_acc, e * DN + (DN + 4 * (th - 1) + t + 1))
                            for i in range(IT):
                                mm = products(pe, bd[t][:, 0:DM], (h_hi[:, th, i, ts], h_lo[:, th, i, ts]),
                                              (dn_hi[c][:, i, :], dn_lo[c][:, i, :]), i == 0, i == IT - 1)
                            mm.then_inc(f_d, 1)

                    def pair(r, first):
                        for c in range(2):
                            e = r * 2 + c
                            for th in range(NT):
                                if th == 0:
                                    pe.wait_ge(w_gl[c], r + 1)
                                gate_up(e, c, th, 0)
                                gate_up(e, c, th, 1)
                                if th:
                                    down(e, r, c, 0)
                                elif c:
                                    down(e - 1, r, 0, 1)
                                elif not first:
                                    down(e - 1, r - 1, 1, 1)
                                for i in range(2, IT):
                                    gate_up(e, c, th, i)

                    pair(0, True)
                    with pe.Fori(1, NE // 2) as r:
                        pair(r, False)
                    down(NE - 1, NE // 2 - 1, 1, 1)

                @block.scalar
                def _(act):
                    def expert(e, first):
                        for n in range(GU):
                            if not first or n >= 2:
                                act.wait_ge(f_h, e * GU + (n - 1))
                            act.wait_ge(f_g, e * GU + (n + 1))
                            act.activation(sg[:, n % 2, :], bg[n % 2][:, :], ACT.Silu).then_inc(f_sg, 1)
                            act.wait_ge(f_h, e * GU + (n + 1))
                            if not first:
                                act.wait_ge(f_d, e * DN - (4 if n < IT else 0))
                            act.activation(h_hi[:, n // IT, n % IT, :], hf[:, n % 2, :], ACT.Copy).then_inc(f_hhi, 1)

                    expert(0, True)
                    with act.Fori(1, NE) as e:
                        expert(e, False)

                @block.vector
                def _(dve):
                    def gated(e, n, first):
                        dve.wait_ge(f_sg, e * GU + (n + 1))
                        if not first or n >= 2:
                            dve.wait_ge(f_hlo, e * GU + (n - 1))
                        dve.tensor_tensor(hf[:, n % 2, :], sg[:, n % 2, :], bu[n % 2][:, :],
                                          ALU.mult).then_inc(f_h, 1)
                        dve.wait_ge(f_hhi, e * GU + (n + 1))
                        dve.tensor_tensor(h_lo[:, n // IT, n % IT, :], hf[:, n % 2, :],
                                          h_hi[:, n // IT, n % IT, :].bitcast(F32), ALU.subtract).then_inc(f_hlo, 1)

                    def add(e, th):
                        for t in range(4):
                            b = th * 4 + t
                            dve.wait_ge(f_d, e * DN + (b + 1))
                            dve.wait_ge(f_acc, e * DN + (b + 1))
                            dve.scalar_tensor_tensor(accm[:, b, :], bd[t][:, 0:DM], comb[:, b, bass.ds(e, 1)],
                                                     accm[:, b, :], ALU.mult, ALU.add).then_inc(f_acc, 1)

                    def expert(e, first):
                        for th in range(NT):
                            for i in range(IT):
                                if i == 2 and th:
                                    add(e, 0)
                                elif i == 2 and not first:
                                    add(e - 1, 1)
                                gated(e, th * IT + i, first)

                    for b in range(BATCH):
                        dve.tensor_copy(accm[:, b, :], x_tok[:, b, :]).then_inc(f_acc, 1)
                    expert(0, True)
                    with dve.Fori(1, NE) as e:
                        expert(e, False)
                    add(NE - 1, 1)
                    for b in range(BATCH):
                        dve.wait_ge(f_acc, (NE + 1) * DN)
                        dve.bn_stats(stats[:, b, :], accm[:, b, :]).then_inc(f_st, 1)
                    for b in range(BATCH):
                        dve.wait_ge(f_st, b + 1)
                        dve.bn_aggr(mv[:, b, :], stats[:, b, :]).then_inc(f_mv, 1)
                    dve.wait_ge(f_r, 1)
                    for b in range(BATCH):
                        dve.tensor_scalar(y[:, b, :], accm[:, b, :], mv[:, b, 0:1], rstd[:, b:b + 1],
                                          ALU.subtract, ALU.mult).then_inc(f_y, 1)


def _host_arrays(inputs):
    f = lambda name: np.asarray(inputs[name])
    at, xa, ff = "L0_attn_", "L0_xattn_", "L0_ffn_"
    col = lambda v, n: np.ascontiguousarray(v.reshape(n, P).T)
    w = f(at + "in_proj_w")
    z, xr, bm, cm, dtr = (w[s:e] for s, e in ((0, 512), (512, 640), (640, 768), (768, 1280), (1280, 1288)))
    twice = lambda m: np.concatenate([m[0:HD], m[0:HD], m[HD:P], m[HD:P]])
    win = np.concatenate([z, cm, twice(bm), twice(xr), dtr, z[0:P - NH]])
    rows = lambda v: np.broadcast_to(v, (P,) + v.shape)
    kw, qw = f(xa + "k_norm_w"), f(xa + "q_norm_w")
    turned = lambda v: np.concatenate([v[AD // 2:], v[:AD // 2]])
    inv_freq = np.float32(1) / np.float32(10000.0) ** (np.arange(0, AD, 2, dtype=np.float32) / np.float32(AD))
    emb = np.outer(np.arange(SEQ, dtype=np.float32), np.concatenate([inv_freq, inv_freq]))
    sign = np.concatenate([-np.ones(AD // 2), np.ones(AD // 2)]).astype(np.float32)
    mask = np.zeros((P, MT * P), np.float32)
    mask[:, P:] = np.where(np.arange(P)[None, :] > np.arange(P)[:, None], np.float32(-2.0 ** 100), np.float32(0))
    kv = lambda k, v: np.concatenate([f(xa + k).reshape(DM, KVH, AD), f(xa + v).reshape(DM, KVH, AD)],
                                     axis=2).reshape(DM, KVH * 2 * AD)
    return {
        "x": f("x"), "ctx": f("ctx_2048"),
        "ident": np.eye(P, dtype=np.float32),
        "upper": np.triu(np.ones((P, P), np.float32)),
        "lower": np.tril(np.ones((P, P), np.float32), -1),
        "ln_w": col(f(at + "ln_w"), KT), "ln_b": col(f(at + "ln_b"), KT),
        "fc1_b": col(f(at + "fc1_b"), IT1), "fc2_b": rows(f(at + "fc2_b")),
        "dt_bias": f(at + "dt_bias").reshape(NH, 1),
        "A_log": np.broadcast_to(f(at + "A_log"), (P, BATCH, NH)),
        "Dp": col(np.repeat(f(at + "Dp"), HD), PAIRS), "norm_w": col(f(at + "norm_w"), PAIRS),
        "winT": win.T, "fc1T": f(at + "fc1_w").T, "fc2T": f(at + "fc2_w").T, "woutT": f(at + "out_proj_w").T,
        "wq": f(xa + "wq"), "wkv": np.stack([kv("wk", "wv"), kv("wk_ctx", "wv_ctx")]), "wo": f(xa + "wo"),
        "cos": np.cos(emb), "sin": np.sin(emb) * sign,
        "qw": rows(qw), "qwr": rows(turned(qw)), "kw": rows(kw), "kwr": rows(turned(kw)), "mask": mask,
        "w_router": f(ff + "w_router").T,
        "rank": rows(np.arange(E, 0, -1).astype(np.float32)),
        "gu": np.stack([np.concatenate([f(ff + "wg"), f(ff + "sg")]).transpose(0, 2, 1),
                        np.concatenate([f(ff + "wu"), f(ff + "su")]).transpose(0, 2, 1)], axis=1),
        "dn": np.concatenate([f(ff + "wd"), f(ff + "sd")]).transpose(0, 2, 1),
    }


def kernel(**inputs):
    import concourse.bacc as bacc
    from concourse.bass_utils import run_bass_kernel_spmd

    nc = bacc.Bacc("TRN2", target_bir_lowering=False, num_devices=1)
    arrays, args = {}, {}
    for name, v in _host_arrays(inputs).items():
        v = np.ascontiguousarray(v)
        arrays[f"in_{name}"] = v
        args[name] = nc.dram_tensor(f"in_{name}", v.shape, mybir.dt.from_np(v.dtype), kind="ExternalInput").ap()
    out = nc.dram_tensor("out_y", (BATCH, SEQ, DM), F32, kind="ExternalOutput").ap()
    decoder_layer(nc, args, out)
    r = run_bass_kernel_spmd(nc, [arrays], core_ids=[0])
    return r.results[0]["out_y"]
```

```python
from contextlib import ExitStack

import numpy as np

import concourse.bass as bass
from concourse import mybir

ALU = mybir.AluOpType
ACT = mybir.ActivationFunctionType
AX_X = mybir.AxisListType.X
F32 = mybir.dt.float32
F32R = mybir.dt.float32r

P = 128
BATCH, SEQ, DM = 8, 128, 256
TOK = BATCH * SEQ
KT = DM // P
HALF = 512

D_IN, HD, NH, NG = 512, 64, 8, 2
REP = NH // NG
PAIRS = NH // 2
INTER = 1024
IT1 = INTER // P
LN_EPS = 1e-5

AH, KVH, AD = 16, 4, 128
AREP = AH // KVH
MT = 2
RMS_EPS = 1e-6

E, NSH, FI = 8, 2, 640
NE = E + NSH
IT = FI // P

Z0, C0, B0, X0, DT0 = 0, 512, 1024, 1280, 1536
WIN = 1664
Z_T, C_T, B_T, X_T = 4, 4, 2, 2


def products(pe, out, lhs, rhs, first, last):
    (lh, ll), (rh, rl) = lhs, rhs
    pe.matmul(out, lh, rh, start=first, stop=False)
    pe.matmul(out, lh, rl, start=False, stop=False)
    return pe.matmul(out, ll, rh, start=False, stop=last)


def met(eng, sem):
    eng.wait_ge(sem, 1)


def counter(eng, name, first):
    turn = eng.alloc_register(name)
    eng.reg_mov(turn, first)
    return turn


def pool_wait(pool, sem, value, turn, step=1):
    if isinstance(value, int):
        pool.wait_ge(sem, value)
    else:
        pool.wait_ge(sem, turn)
        pool.reg_add(turn, turn, step)


def decoder_layer(nc, a, out):
    with ExitStack() as whole:
        dram = lambda name: a[name]

        def scope(ctx):
            sb = lambda name, shape, dt=F32, side=None: ctx.enter_context(nc.sbuf_tensor(name, shape, dt, side=side))
            ps = lambda name, shape: ctx.enter_context(nc.psum_tensor(name, shape, F32))
            given = []

            def sem(name):
                given.append(nc.alloc_semaphore(name=name))
                return given[-1]

            def give_back():
                if given:
                    nc.clear_and_free_semaphores(given)
                    nc.all_engine_barrier()

            ctx.callback(give_back)
            return sb, ps, sem

        sb, ps, sem = scope(whole)
        ident = sb("ident", [P, P])
        x_tok = sb("x_tok", [P, BATCH, DM])
        acc = sb("acc", [P, BATCH, DM])
        s_const = sem("s_const")
        s_x = sem("s_x")
        wr = sb("wr", [P, KT, E])
        rank = sb("rank", [P, E])
        s_router = sem("s_router")

        with ExitStack() as both:
            weights = AttentionWeights(scope(both)[0])
            state_space_layer(nc, a, scope, ident, x_tok, acc, s_const, s_x, weights, wr, rank, s_router)
            cross_attention(nc, a, scope, ident, x_tok, weights)
        experts(nc, a, scope, ident, x_tok, wr, rank, s_router, out)


class AttentionWeights:

    def __init__(self, sb):
        self.sb = sb

    def place(self):
        sb = lambda name, shape, dt=F32: self.sb(name, shape, dt, side="right")
        self.wq_hi = sb("wq_hi", [P, KT, KVH, AREP * AD], F32R)
        self.wq_lo = sb("wq_lo", [P, KT, KVH, AREP * AD], F32R)
        self.wkv_hi = sb("wkv_hi", [P, 2 * KT, KVH, 2 * AD], F32R)
        self.wkv_lo = sb("wkv_lo", [P, 2 * KT, KVH, 2 * AD], F32R)
        self.cq = sb("cq", [P, AD])
        self.sq = sb("sq_t", [P, AD])
        self.ck = sb("ck", [P, AD])
        self.sk = sb("sk", [P, AD])
        self.kw_c = sb("kw_c", [P, AD])
        self.mask = sb("mask", [P, MT * P], F32R)
        self.ident = sb("ident_r", [P, P], F32R)
        self.x_cur = sb("x_cur", [P, DM])
        self.c_cur = sb("c_cur", [P, DM])


def state_space_layer(nc, a, scope, ident, x_tok, acc, s_const, s_x, aw, wr, rank, s_router):
    with ExitStack() as layer:
        sb, ps, sem = scope(layer)
        h_hi = sb("h_hi", [P, KT, TOK], F32R)
        h_lo = sb("h_lo", [P, KT, TOK], F32R)
        win_hi = sb("win_hi", [P, KT, WIN], F32R)
        win_lo = sb("win_lo", [P, KT, WIN], F32R)
        dt = sb("dt", [P, BATCH, NH])
        dta = sb("dta", [P, BATCH, NH])
        wout = sb("wout", [P, PAIRS, DM])
        d_col = sb("d_col", [P, PAIRS])
        nw_col = sb("nw_col", [P, PAIRS])
        upper = sb("upper", [P, P])
        lower = sb("lower", [P, P])
        s_wout = sem("s_wout")

        with ExitStack() as part:
            sb, ps, sem = scope(part)
            win_raw = sb("win_raw", [P, KT, WIN])
            fc1_raw = sb("fc1_raw", [P, KT, INTER])
            fc2_raw = sb("fc2_raw", [P, IT1, DM])
            fc1_hi = sb("fc1_hi", [P, KT, INTER], F32R)
            fc1_lo = sb("fc1_lo", [P, KT, INTER], F32R)
            fc2_hi = sb("fc2_hi", [P, IT1, DM], F32R)
            fc2_lo = sb("fc2_lo", [P, IT1, DM], F32R)
            g_f = sb("g_f", [P, 2, HALF])
            g_hi = sb("g_hi", [P, IT1, HALF], F32R)
            g_lo = sb("g_lo", [P, IT1, HALF], F32R)
            stats = sb("stats", [P, BATCH, 6])
            mv = sb("mv", [P, BATCH, 2])
            veps = sb("veps", [P, BATCH])
            rstd = sb("rstd", [P, BATCH])
            mhalf = sb("mhalf", [P, BATCH])
            xhat = sb("xhat", [P, BATCH, DM])
            h_f = sb("h_f", [P, KT, TOK])
            x2b = sb("x2b", [P, BATCH, DM])
            fc2_bias = sb("fc2_bias", [P, DM])
            lnw = sb("lnw", [P, KT])
            lnb = sb("lnb", [P, KT])
            fc1b = sb("fc1b", [P, IT1])
            dtb = sb("dtb", [NH, 1])
            alog = sb("alog", [P, BATCH, NH])
            dt_row = sb("dt_row", [NH, TOK])
            sp_x = sb("sp_x", [P, BATCH, NH])
            sp_abs = sb("sp_abs", [P, BATCH, NH])
            sp_e = sb("sp_e", [P, BATCH, NH])
            sp_u = sb("sp_u", [P, BATCH, NH])
            sp_ln = sb("sp_ln", [P, BATCH, NH])
            sp_d = sb("sp_d", [P, BATCH, NH])
            sp_r = sb("sp_r", [P, BATCH, NH])
            sp_t = sb("sp_t", [P, BATCH, NH])
            sp_s = sb("sp_s", [P, BATCH, NH])
            ea = sb("ea", [P, BATCH, NH])
            bank = [ps(f"bank{i}", [P, 512]) for i in range(8)]

            s_small = sem("s_small")
            s_ident = sem("s_ident")
            s_ln = sem("s_ln")
            s_fc1 = sem("s_fc1")
            s_fc2 = sem("s_fc2")
            s_win = sem("s_win")
            s_fc2b = sem("s_fc2b")
            stats_ready = sem("stats_ready")
            mv_ready = sem("mv_ready")
            veps_ready = sem("veps_ready")
            mhalf_ready = sem("mhalf_ready")
            rstd_ready = sem("rstd_ready")
            xhat_ready = sem("xhat_ready")
            hT_ready = sem("hT_ready")
            hf_ready = sem("hf_ready")
            hhi_ready = sem("hhi_ready")
            hlo_ready = sem("hlo_ready")
            fc1hi_ready = sem("fc1hi_ready")
            fc1lo_ready = sem("fc1lo_ready")
            fc2hi_ready = sem("fc2hi_ready")
            fc2lo_ready = sem("fc2lo_ready")
            winhi_ready = sem("winhi_ready")
            winlo_ready = sem("winlo_ready")
            dtp_ready = sem("dtp_ready")
            dtrow_ready = sem("dtrow_ready")
            dtT_ready = sem("dtT_ready")
            sp = sem("sp")
            spa = sem("spa")
            dta_ready = sem("dta_ready")
            x2b_ready = sem("x2b_ready")
            x2_ready = sem("x2_ready")
            fc1_done = sem("fc1_done")
            gf_ready = sem("gf_ready")
            ghi_ready = sem("ghi_ready")
            glo_ready = sem("glo_ready")
            fc2_done = sem("fc2_done")
            acc_ready = sem("acc_ready")
            wout_ready = sem("wout_ready")

            SMALL = 4
            with nc.Block() as block:
                @block.sync
                def _(sp_):
                    xv = a["x"].rearrange("b s d -> s b d")
                    for q in range(4):
                        sp_.dma_start(x_tok[:, 2 * q:2 * q + 2, :], xv[:, 2 * q:2 * q + 2, :]).then_inc(s_x, 16)
                    sp_.dma_start(fc1_raw[:, :, :], a["fc1T"].rearrange("(k p) n -> p k n", p=P)).then_inc(s_fc1, 16)
                    sp_.dma_start(win_raw[:, :, :], a["winT"].rearrange("(k p) n -> p k n", p=P)).then_inc(s_win, 16)
                    sp_.dma_start(fc2_raw[:, :, :], a["fc2T"].rearrange("(k p) n -> p k n", p=P)).then_inc(s_fc2, 16)

                @block.scalar
                def _(act):
                    act.dma_start(ident[:, :], a["ident"]).then_inc(s_ident, 16)
                    act.dma_start(lnw[:, :], a["ln_w"]).then_inc(s_ln, 16)
                    act.dma_start(lnb[:, :], a["ln_b"]).then_inc(s_ln, 16)
                    act.dma_start(fc1b[:, :], a["fc1_b"]).then_inc(s_small, 16)
                    act.dma_start(dtb[:, :], a["dt_bias"]).then_inc(s_small, 16)
                    act.dma_start(alog[:, :, :], a["A_log"]).then_inc(s_small, 16)
                    act.dma_start(nw_col[:, :], a["norm_w"]).then_inc(s_small, 16)
                    act.dma_start(fc2_bias[:, :], a["fc2_b"]).then_inc(s_fc2b, 16)
                    act.dma_start(d_col[:, :], a["Dp"]).then_inc(s_const, 16)
                    act.dma_start(upper[:, :], a["upper"]).then_inc(s_const, 16)
                    act.dma_start(lower[:, :], a["lower"]).then_inc(s_const, 16)
                    act.dma_start(wout[:, :, :], a["woutT"].rearrange("(k p) n -> p k n", p=P)).then_inc(s_wout, 16)
                    act.wait_ge(s_fc1, 16)
                    for k in range(KT):
                        act.activation(fc1_hi[:, k, :], fc1_raw[:, k, :], ACT.Copy).then_inc(fc1hi_ready, 1)
                    act.wait_ge(s_ln, 32)
                    for g in range(BATCH // 2):
                        for k in range(KT):
                            act.wait_ge(hT_ready, 2 * g + k + 1)
                            act.activation(h_f[:, k, g * 256:(g + 1) * 256], bank[(2 * g + k) % 4][:, 0:256],
                                           ACT.Identity, bias=lnb[:, k:k + 1],
                                           scale=lnw[:, k:k + 1]).then_inc(hf_ready, 1)
                    def hidden(th):
                        for i in range(IT1):
                            act.wait_ge(fc1_done, th * IT1 + i + 1)
                            if th or i >= 2:
                                act.wait_ge(glo_ready, th * IT1 + i - 1)
                            act.activation(g_f[:, i % 2, :], bank[i % 4][:, :], ACT.Gelu_apprx_tanh,
                                           bias=fc1b[:, i:i + 1]).then_inc(gf_ready, 1)

                    act.wait_ge(s_small, 16 * SMALL)
                    hidden(0)
                    for th in range(2):
                        act.wait_ge(dtp_ready, th + 1)
                        act.activation(dt_row[:, th * HALF:(th + 1) * HALF], bank[th][0:NH, :], ACT.Identity,
                                       bias=dtb[:, 0:1]).then_inc(dtrow_ready, 1)
                    act.activation(ea[:, :, :], alog[:, :, :], ACT.Exp).then_inc(spa, 1)
                    act.wait_ge(sp, 2)
                    act.activation(sp_e[:, :, :], sp_abs[:, :, :], ACT.Exp, scale=-1.0).then_inc(spa, 1)
                    act.wait_ge(sp, 3)
                    act.activation(sp_ln[:, :, :], sp_u[:, :, :], ACT.Ln).then_inc(spa, 1)
                    hidden(1)

                @block.gpsimd
                def _(pool):
                    pool.memset(mhalf[:, :], -0.5).then_inc(mhalf_ready, 1)
                    pool.wait_ge(mhalf_ready, 1)
                    pool.wait_ge(mv_ready, BATCH)
                    pool.tensor_scalar(veps[:, :], mv[:, :, 1], 1.0, LN_EPS, ALU.mult,
                                       ALU.add).then_inc(veps_ready, 1)
                    pool.wait_ge(veps_ready, 1)
                    pool.tensor_tensor(rstd[:, :], veps[:, :], mhalf[:, :], ALU.pow).then_inc(rstd_ready, 1)
                    pool.wait_ge(s_win, 16)
                    for k in range(KT):
                        pool.tensor_scalar(win_hi[:, k, :], win_raw[:, k, :], 1.0, 0.0, ALU.mult,
                                           ALU.add).then_inc(winhi_ready, 1)
                        pool.wait_ge(winhi_ready, k + 1)
                        pool.tensor_tensor(win_lo[:, k, :], win_raw[:, k, :], win_hi[:, k, :].bitcast(F32),
                                           ALU.subtract).then_inc(winlo_ready, 1)
                    pool.wait_ge(s_fc2, 16)
                    for k in range(2):
                        s = slice(4 * k, 4 * k + 4)
                        pool.tensor_scalar(fc2_hi[:, s, :], fc2_raw[:, s, :], 1.0, 0.0, ALU.mult,
                                           ALU.add).then_inc(fc2hi_ready, 1)
                        pool.wait_ge(fc2hi_ready, k + 1)
                        pool.tensor_tensor(fc2_lo[:, s, :], fc2_raw[:, s, :], fc2_hi[:, s, :].bitcast(F32),
                                           ALU.subtract).then_inc(fc2lo_ready, 1)

                @block.vector
                def _(dve):
                    for b in range(BATCH):
                        dve.wait_ge(s_x, 16 * 4)
                        dve.bn_stats(stats[:, b, :], x_tok[:, b, :]).then_inc(stats_ready, 1)
                    for b in range(BATCH):
                        dve.wait_ge(stats_ready, b + 1)
                        dve.bn_aggr(mv[:, b, :], stats[:, b, :]).then_inc(mv_ready, 1)
                    dve.wait_ge(rstd_ready, 1)
                    for b in range(BATCH):
                        dve.tensor_scalar(xhat[:, b, :], x_tok[:, b, :], mv[:, b, 0:1], rstd[:, b:b + 1],
                                          ALU.subtract, ALU.mult).then_inc(xhat_ready, 1)
                    for k in range(KT):
                        dve.wait_ge(fc1hi_ready, k + 1)
                        dve.tensor_tensor(fc1_lo[:, k, :], fc1_raw[:, k, :], fc1_hi[:, k, :].bitcast(F32),
                                          ALU.subtract).then_inc(fc1lo_ready, 1)
                    for g in range(BATCH // 2):
                        s = slice(g * 256, (g + 1) * 256)
                        dve.wait_ge(hf_ready, 2 * g + 2)
                        dve.tensor_copy(h_hi[:, :, s], h_f[:, :, s]).then_inc(hhi_ready, 1)
                        dve.wait_ge(hhi_ready, g + 1)
                        dve.tensor_tensor(h_lo[:, :, s], h_f[:, :, s], h_hi[:, :, s].bitcast(F32),
                                          ALU.subtract).then_inc(hlo_ready, 1)
                    dve.wait_ge(s_fc2b, 16)
                    dve.scalar_tensor_tensor(x2b[:, :, :], x_tok[:, :, :], 2.0,
                                             fc2_bias[:, None, :].broadcast_to([P, BATCH, DM]),
                                             ALU.mult, ALU.add).then_inc(x2b_ready, 1)
                    dve.wait_ge(s_wout, 16)
                    dve.wait_ge(s_small, 16 * SMALL)
                    for j in range(PAIRS):
                        dve.tensor_scalar(wout[:, j, :], wout[:, j, :], nw_col[:, j:j + 1], None,
                                          ALU.mult).then_inc(wout_ready, 1)
                    def softplus():
                        dve.wait_ge(dtT_ready, BATCH)
                        dve.tensor_copy(sp_x[:, :, :],
                                        bank[2][:, 0:BATCH * NH].rearrange("p (b h) -> p b h", b=BATCH)).then_inc(sp, 1)
                        dve.wait_ge(sp, 1)
                        dve.scalar_tensor_tensor(sp_abs[:, :, :], sp_x[:, :, :], -1.0, sp_x[:, :, :], ALU.mult,
                                                 ALU.max).then_inc(sp, 1)
                        dve.wait_ge(spa, 2)
                        dve.tensor_scalar(sp_u[:, :, :], sp_e[:, :, :], 1.0, None, ALU.add).then_inc(sp, 1)
                        dve.wait_ge(sp, 3)
                        dve.scalar_tensor_tensor(sp_d[:, :, :], sp_u[:, :, :], -1.0, sp_e[:, :, :], ALU.add,
                                                 ALU.subtract).then_inc(sp, 1)
                        dve.reciprocal(sp_r[:, :, :], sp_u[:, :, :]).then_inc(sp, 1)
                        dve.wait_ge(sp, 5)
                        dve.tensor_tensor(sp_t[:, :, :], sp_d[:, :, :], sp_r[:, :, :], ALU.mult).then_inc(sp, 1)
                        dve.wait_ge(spa, 3)
                        dve.wait_ge(sp, 6)
                        dve.tensor_tensor(sp_s[:, :, :], sp_ln[:, :, :], sp_t[:, :, :], ALU.subtract).then_inc(sp, 1)
                        dve.wait_ge(sp, 7)
                        dve.scalar_tensor_tensor(dt[:, :, :], sp_x[:, :, :], 0.0, sp_s[:, :, :], ALU.max,
                                                 ALU.add).then_inc(sp, 1)
                        dve.wait_ge(sp, 8)
                        dve.scalar_tensor_tensor(dta[:, :, :], dt[:, :, :], -1.0, ea[:, :, :], ALU.mult,
                                                 ALU.mult).then_inc(dta_ready, 1)

                    dve.wait_ge(x2b_ready, 1)
                    for th in range(2):
                        for i in range(IT1):
                            dve.wait_ge(gf_ready, th * IT1 + i + 1)
                            dve.wait_ge(fc2_done, th * 4)
                            dve.tensor_copy(g_hi[:, i, :], g_f[:, i % 2, :]).then_inc(ghi_ready, 1)
                            dve.wait_ge(ghi_ready, th * IT1 + i + 1)
                            dve.tensor_tensor(g_lo[:, i, :], g_f[:, i % 2, :], g_hi[:, i, :].bitcast(F32),
                                              ALU.subtract).then_inc(glo_ready, 1)
                        for t in range(4):
                            dve.wait_ge(fc2_done, th * 4 + t + 1)
                            dve.tensor_tensor(acc[:, th * 4 + t, :], bank[4 + t][:, 0:DM], x2b[:, th * 4 + t, :],
                                              ALU.add).then_inc(acc_ready, 1)
                            if th == 0 and t == 1:
                                softplus()

                @block.tensor
                def _(pe):
                    pe.wait_ge(s_ident, 16)
                    for g in range(BATCH // 2):
                        pe.wait_ge(xhat_ready, 2 * g + 2)
                        for k in range(KT):
                            if 2 * g + k >= 4:
                                pe.wait_ge(hf_ready, 2 * g + k - 3)
                            for b in range(2):
                                mm = pe.transpose(bank[(2 * g + k) % 4][:, b * P:(b + 1) * P],
                                                  xhat[:, 2 * g + b, k * P:(k + 1) * P], ident[:, :])
                            mm.then_inc(hT_ready, 1)
                    def dt_rows():
                        pe.wait_ge(winlo_ready, KT)
                        pe.wait_ge(hlo_ready, BATCH // 2)
                        for th in range(2):
                            pe.wait_ge(gf_ready, IT1 - 3 + th)
                            s = slice(th * HALF, (th + 1) * HALF)
                            for k in range(KT):
                                w = slice(DT0, DT0 + P)
                                mm = products(pe, bank[th][:, :], (win_hi[:, k, w], win_lo[:, k, w]),
                                              (h_hi[:, k, s], h_lo[:, k, s]), k == 0, k == KT - 1)
                            mm.then_inc(dtp_ready, 1)

                    def dt_turned():
                        pe.wait_ge(dtrow_ready, 2)
                        pe.wait_ge(gf_ready, IT1 - 1)
                        for b in range(BATCH):
                            pe.transpose(bank[2][:, b * NH:(b + 1) * NH], dt_row[:, b * P:(b + 1) * P],
                                         ident[0:NH, 0:NH]).then_inc(dtT_ready, 1)

                    pe.wait_ge(fc1lo_ready, KT)
                    for th in range(2):
                        tok = slice(th * HALF, (th + 1) * HALF)
                        pe.wait_ge(hlo_ready, th * 2 + 2)
                        if th:
                            pe.wait_ge(dtrow_ready, 2)
                            pe.wait_ge(sp, 1)
                        for i in range(IT1):
                            if th == 0 and i < 4:
                                pe.wait_ge(hf_ready, 4 + i + 1)
                            else:
                                pe.wait_ge(gf_ready, th * IT1 + i - 3)
                            w = slice(i * P, (i + 1) * P)
                            for k in range(KT):
                                mm = products(pe, bank[i % 4][:, :], (fc1_hi[:, k, w], fc1_lo[:, k, w]),
                                              (h_hi[:, k, tok], h_lo[:, k, tok]), k == 0, k == KT - 1)
                            mm.then_inc(fc1_done, 1)
                        if th == 0:
                            dt_rows()
                            pe.wait_ge(fc2lo_ready, 2)
                        pe.wait_ge(glo_ready, th * IT1 + IT1)
                        for t in range(4):
                            if th:
                                pe.wait_ge(acc_ready, t + 1)
                            s = slice(t * P, (t + 1) * P)
                            for i in range(IT1):
                                mm = products(pe, bank[4 + t][:, 0:DM], (g_hi[:, i, s], g_lo[:, i, s]),
                                              (fc2_hi[:, i, :], fc2_lo[:, i, :]), i == 0, i == IT1 - 1)
                            mm.then_inc(fc2_done, 1)
                            if th == 0 and t == 1:
                                dt_turned()

        with ExitStack() as part:
            sb, ps, sem = scope(part)
            TW = 2 * P
            th_z = sb("th_z", [P, Z_T, TW])
            sz = sb("sz", [P, Z_T, TW])
            c_t = sb("c_t", [P, C_T, TW])
            b_t = sb("b_t", [P, B_T, TW])
            x_t = sb("x_t", [P, X_T, TW])
            xpad = sb("xpad", [P, NG, 2, P])
            tri = sb("tri", [P, NH, P])
            dec = sb("dec", [P, NH, P])
            wts = sb("wts", [P, NH, P])
            yd = sb("yd", [P, PAIRS, P])
            yg = sb("yg", [P, PAIRS, P])
            sq = sb("sq", [P, PAIRS, P])
            sqs = sb("sqs", [P, P])
            ones = sb("ones", [P, 2])
            ve = sb("ve", [P, 1])
            ry = sb("ry", [P, 1])
            mh = sb("mh", [P, 1])
            pre = sb("pre", [P, DM])
            st = sb("st", [P, 6])
            mv2 = sb("mv2", [P, 2])
            ve2 = sb("ve2", [P, 1])
            r2 = sb("r2", [P, 1])
            aw.place()
            right = lambda name, shape: sb(name, shape, F32, side="right")
            wq_raw = right("wq_raw", [P, KT, KVH, AREP * AD])
            wkv_raw = right("wkv_raw", [P, 2 * KT, KVH, 2 * AD])
            cos, sin, qw, qwr, kw, kwr = [right(name, [P, AD]) for name in ("cos", "sin", "qw", "qwr", "kw", "kwr")]
            mask_raw = pre
            bz = ps("bz", [P, 2, 512])
            bc = ps("bc", [P, 2, 512])
            bb = ps("bb", [P, 512])
            bx = ps("bx", [P, 512])
            b_out = ps("b_out", [P, 512])
            b_ss = ps("b_ss", [P, 512])

            names = ("m_const", "m_zp", "m_cp", "m_bp", "m_xp", "m_tanh", "m_sz", "m_c", "m_b", "m_x", "m_xt",
                     "m_xpad", "m_tri", "m_seg", "m_dec", "m_decm", "m_g", "m_w", "m_y", "m_yd", "m_yg", "m_sq",
                     "m_sqs", "m_ss", "m_ve", "m_ry", "m_out", "m_pre", "m_st", "m_mv", "m_ve2", "m_r2", "m_x1",
                     "m_ti")
            (m_const, m_zp, m_cp, m_bp, m_xp, m_tanh, m_sz, m_c, m_b, m_x, m_xt, m_xpad, m_tri, m_seg, m_dec,
             m_decm, m_g, m_w, m_y, m_yd, m_yg, m_sq, m_sqs, m_ss, m_ve, m_ry, m_out, m_pre, m_st, m_mv, m_ve2,
             m_r2, m_x1, m_ti) = [sem(n) for n in names]
            w_q, w_kv, w_small, w_tab, w_hi, w_lo = [sem(n) for n in ("w_q", "w_kv", "w_small", "w_tab", "w_hi", "w_lo")]
            NPAIR = BATCH // 2

            def chunk(c, j):
                pick = lambda t: t[:, :, bass.ds(j, 1), :].rearrange("p k g n -> p k (g n)")
                if c == 0:
                    return pick(wq_raw), pick(aw.wq_hi), pick(aw.wq_lo)
                return pick(wkv_raw), pick(aw.wkv_hi), pick(aw.wkv_lo)

            def over_pairs(eng, step):
                for c in range(2):
                    step(0, c, True, False)
                with eng.Fori(1, NPAIR - 1) as j:
                    for c in range(2):
                        step(j, c, False, False)
                for c in range(2):
                    step(NPAIR - 1, c, False, True)

            with nc.Block() as block:
                @block.sync
                def _(sp):
                    sp.dma_start(wr[:, :, :], a["w_router"].rearrange("(k p) e -> p k e", p=P)).then_inc(s_router, 16)
                    sp.dma_start(rank[:, :], a["rank"]).then_inc(s_router, 16)
                    sp.dma_start(aw.c_cur[:, :], a["ctx"][0]).then_inc(w_small, 16)
                    for t, name in ((cos, "cos"), (sin, "sin"), (qw, "qw"), (qwr, "qwr"), (kw, "kw"), (kwr, "kwr"),
                                    (mask_raw, "mask")):
                        sp.dma_start(t[:, :], a[name]).then_inc(w_small, 16)
                    sp.dma_start(wq_raw[:, :, :, :].rearrange("p k g n -> p k (g n)"),
                                 a["wq"].rearrange("(k p) n -> p k n", p=P)).then_inc(w_q, 16)
                    sp.dma_start(wkv_raw[:, :, :, :].rearrange("p k g n -> p k (g n)"),
                                 a["wkv"].rearrange("s (k p) n -> p (s k) n", p=P)).then_inc(w_kv, 16)

                @block.gpsimd
                def _(pool):
                    def triangle(n):
                        pool.wait_ge(m_seg, n)
                        pool.tensor_tensor(tri[:, :, :], upper[:, None, :].broadcast_to([P, NH, P]),
                                           dta[:, bass.ds(n, 1), :].rearrange("p b h -> p (b h)")[:, :, None]
                                           .broadcast_to([P, NH, P]), ALU.mult).then_inc(m_tri, 1)

                    def mask_decays(n, turn):
                        pool_wait(pool, m_dec, n + 1, turn)
                        pool.affine_select(out=dec[:, :, :], in_=dec[:, :, :], pattern=[[0, NH], [1, P]],
                                           compare_op=ALU.is_ge, fill=0.0, base=0,
                                           channel_multiplier=-1).then_inc(m_decm, 1)

                    def norm_scale(n, turn):
                        pool_wait(pool, m_mv, n + 1, turn)
                        pool.tensor_scalar(ve2[:, :], mv2[:, 1:2], 1.0, LN_EPS, ALU.mult, ALU.add).then_inc(m_ve2, 1)
                        pool.wait_ge(m_ve2, n + 1)
                        pool.tensor_tensor(r2[:, :], ve2[:, :], mh[:, :], ALU.pow).then_inc(m_r2, 1)

                    def split_chunk(j, c):
                        raw, hi, lo = chunk(c, j)
                        pool.wait_ge(w_hi, j * 2 + (c + 1))
                        pool.tensor_tensor(lo, raw, hi.bitcast(F32), ALU.subtract).then_inc(w_lo, 1)

                    def step(j, c, first, last):
                        n = j * 2 + c
                        if last and c:
                            split_chunk(j, c)
                        if not (last and c):
                            mask_decays(n + 1, turn_dec)
                        if not last:
                            triangle(n + 2)
                        if not (first and c == 0):
                            norm_scale(n - 1, turn_mv)
                        if not (last and c):
                            split_chunk(j, c)
                        pool.wait_ge(m_ve, n + 1)
                        pool.wait_ge(m_pre, n)
                        pool.tensor_tensor(ry[:, :], ve[:, :], mh[:, :], ALU.pow).then_inc(m_ry, 1)

                    pool.memset(xpad[:, :, :, :], 0.0).then_inc(m_const, 1)
                    pool.memset(ones[:, :], 1.0).then_inc(m_const, 1)
                    pool.memset(mh[:, :], -0.5).then_inc(m_const, 1)
                    pool.wait_ge(m_const, 3)
                    pool.wait_ge(s_const, 16 * 3)
                    turn_dec, turn_mv = counter(pool, "turn_dec", 4), counter(pool, "turn_mv", 2)
                    triangle(0)
                    triangle(1)
                    mask_decays(0, None)
                    over_pairs(pool, step)
                    pool.tensor_scalar(aw.x_cur[:, :], x_tok[:, 0, :], 1.0, 0.0, ALU.mult, ALU.add).then_inc(w_lo, 1)
                    norm_scale(BATCH - 1, None)

                @block.scalar
                def _(act):
                    def decays(n):
                        act.wait_ge(m_seg, n + 1)
                        act.wait_ge(m_w, n)
                        act.activation(dec[:, :, :], bz[:, :, :].rearrange("p a (h l) -> p (a h) l", l=P),
                                       ACT.Exp).then_inc(m_dec, 1)

                    def copies(j):
                        two = lambda b: b.rearrange("p (a t) -> p a t", a=2)
                        act.wait_ge(m_g, j * 2)
                        for q in range(2):
                            act.wait_ge(m_cp, j * 2 + (q + 1))
                            act.activation(c_t[:, 2 * q:2 * q + 2, :], two(bc[:, q, :]), ACT.Copy).then_inc(m_c, 1)
                        act.wait_ge(m_bp, j + 1)
                        act.activation(b_t[:, :, :], two(bb[:, :]), ACT.Copy).then_inc(m_b, 1)
                        act.wait_ge(m_xp, j + 1)
                        act.wait_ge(m_yd, j * 2)
                        act.activation(x_t[:, :, :], two(bx[:, :]), ACT.Copy).then_inc(m_x, 1)

                    def gates(j):
                        act.wait_ge(m_yg, j * 2)
                        for q in range(2):
                            act.wait_ge(m_zp, j * 2 + (q + 1))
                            act.activation(th_z[:, 2 * q:2 * q + 2, :], bz[:, q, :].rearrange("p (a t) -> p a t", a=2),
                                           ACT.Tanh, scale=0.5).then_inc(m_tanh, 1)

                    def step(j, c, first, last):
                        n = j * 2 + c
                        if not (last and c):
                            decays(n + 1)
                        raw, hi, lo = chunk(c, j)
                        if first:
                            act.wait_ge(w_kv if c else w_q, 16)
                        act.activation(hi, raw, ACT.Copy).then_inc(w_hi, 1)
                        act.wait_ge(m_yg, n + 1)
                        act.wait_ge(m_sqs, n)
                        act.activation(sq[:, :, :], yg[:, :, :], ACT.Square).then_inc(m_sq, 1)
                        if c and not last:
                            copies(j + 1)
                            gates(j + 1)

                    gates(0)
                    copies(0)
                    decays(0)
                    over_pairs(act, step)

                @block.vector
                def _(dve):
                    def gates(j):
                        for q in range(2):
                            dve.wait_ge(m_tanh, j * 2 + (q + 1))
                            dve.scalar_tensor_tensor(sz[:, 2 * q:2 * q + 2, :], th_z[:, 2 * q:2 * q + 2, :], 1.0,
                                                     bz[:, q, :].rearrange("p (a t) -> p a t", a=2), ALU.add,
                                                     ALU.mult).then_inc(m_sz, 1)

                    def pad_x(n):
                        dve.wait_ge(m_xt, n + 1)
                        dve.wait_ge(m_y, n)
                        for o in range(2):
                            dve.tensor_copy(xpad[:, :, o, o * HD:(o + 1) * HD],
                                            bx[:, 0:2 * P].rearrange("p (g d) -> p g d", g=2)[:, :, 0:HD]
                                            ).then_inc(m_xpad, 1)

                    def weights(n):
                        dve.wait_ge(m_decm, n + 1)
                        dve.wait_ge(m_g, n + 1)
                        dve.wait_ge(m_y, n)
                        for h in range(NH):
                            dve.scalar_tensor_tensor(
                                wts[:, h, :], bc[:, h % 2, (h // 2) * P:(h // 2 + 1) * P],
                                dt[:, bass.ds(n, 1), h:h + 1].rearrange("p b h -> p (b h)"),
                                dec[:, h, :], ALU.mult, ALU.mult).then_inc(m_ti if h < NH - 1 else m_w, 1)

                    def norm_stats(n):
                        dve.wait_ge(m_ry, n + 1)
                        dve.wait_ge(m_out, n + 1)
                        dve.wait_ge(m_x1, n)
                        dve.scalar_tensor_tensor(pre[:, None, :], b_out[:, None, 0:DM], ry[:, 0:1],
                                                 acc[:, bass.ds(n, 1), :], ALU.mult, ALU.add).then_inc(m_pre, 1)
                        dve.wait_ge(m_pre, n + 1)
                        dve.bn_stats(st[:, :], pre[:, :]).then_inc(m_st, 1)
                        met(dve, m_const)
                        dve.wait_ge(m_st, n + 1)
                        dve.wait_ge(m_ve2, n)
                        dve.bn_aggr(mv2[:, :], st[:, :]).then_inc(m_mv, 1)

                    def norm(n):
                        dve.wait_ge(m_mv, n + 1)
                        dve.wait_ge(m_r2, n + 1)
                        dve.tensor_scalar(x_tok[:, bass.ds(n, 1), :], pre[:, None, :], mv2[:, 0:1], r2[:, 0:1],
                                          ALU.subtract, ALU.mult).then_inc(m_x1, 1)

                    def step(j, c, first, last):
                        n = j * 2 + c
                        tk = slice(c * P, (c + 1) * P)
                        dve.wait_ge(m_y, n + 1)
                        dve.wait_ge(m_x, j + 1)
                        for i in range(PAIRS):
                            dve.scalar_tensor_tensor(yd[:, i, :], x_t[:, i // 2, tk], d_col[:, i:i + 1],
                                                     bb[:, i * P:(i + 1) * P], ALU.mult,
                                                     ALU.add).then_inc(m_ti if i < PAIRS - 1 else m_yd, 1)
                        dve.wait_ge(m_yd, n + 1)
                        dve.wait_ge(m_ti, n * 10 + 10)
                        dve.wait_ge(m_sz, j * 2 + 2)
                        dve.wait_ge(m_out, n)
                        dve.wait_ge(m_sq, n)
                        dve.tensor_tensor(yg[:, :, :], yd[:, :, :], sz[:, :, tk], ALU.mult).then_inc(m_yg, 1)
                        if not (first and c == 0):
                            norm_stats(n - 1)
                        dve.wait_ge(m_sq, n + 1)
                        dve.wait_ge(m_ss, n)
                        dve.tensor_reduce(sqs[:, :], sq[:, :, :].rearrange("p i l -> p l i"), AX_X,
                                          ALU.add).then_inc(m_sqs, 1)
                        if not (last and c):
                            weights(n + 1)
                        if not (last and c):
                            pad_x(n + 1)
                        if not (first and c == 0):
                            norm(n - 1)
                        dve.wait_ge(m_ss, n + 1)
                        dve.wait_ge(m_ry, n)
                        dve.tensor_scalar(ve[:, :], b_ss[:, 0:1], 1.0 / D_IN, 4 * LN_EPS, ALU.mult,
                                          ALU.add).then_inc(m_ve, 1)
                        if c and not last:
                            gates(j + 1)

                    dve.wait_ge(m_const, 3)
                    dve.wait_ge(s_const, 16 * 3)
                    gates(0)
                    pad_x(0)
                    weights(0)
                    dve.wait_ge(w_small, 16 * 8)
                    dve.tensor_tensor(aw.cq[:, :], cos[:, :], qw[:, :], ALU.mult).then_inc(w_tab, 1)
                    dve.tensor_tensor(aw.sq[:, :], sin[:, :], qwr[:, :], ALU.mult).then_inc(w_tab, 1)
                    dve.tensor_tensor(aw.ck[:, :], cos[:, :], kw[:, :], ALU.mult).then_inc(w_tab, 1)
                    dve.tensor_tensor(aw.sk[:, :], sin[:, :], kwr[:, :], ALU.mult).then_inc(w_tab, 1)
                    dve.tensor_scalar(aw.kw_c[:, :], kw[:, :], float(AD) ** 0.5, None, ALU.mult).then_inc(w_tab, 1)
                    dve.tensor_copy(aw.mask[:, :], mask_raw[:, :]).then_inc(w_tab, 1)
                    dve.tensor_copy(aw.ident[:, :], ident[:, :]).then_inc(w_tab, 1)
                    over_pairs(dve, step)
                    norm_stats(BATCH - 1)
                    norm(BATCH - 1)

                @block.tensor
                def _(pe):
                    def project(j, dst, col, tiles):
                        tok = bass.ds(j * TW, TW)
                        for i in range(tiles):
                            w = slice(col + i * P, col + (i + 1) * P)
                            for k in range(KT):
                                mm = products(pe, dst[:, i * TW:(i + 1) * TW], (win_hi[:, k, w], win_lo[:, k, w]),
                                              (h_hi[:, k, tok], h_lo[:, k, tok]), k == 0, k == KT - 1)
                        return mm

                    def project_z(j):
                        if not (isinstance(j, int) and j == 0):
                            pe.wait_ge(m_dec, j * 2 + 1)
                        for q in range(2):
                            project(j, bz[:, q, :], Z0 + 2 * q * P, 2).then_inc(m_zp, 1)

                    def project_cbx(j):
                        pe.wait_ge(m_w, j * 2)
                        for q in range(2):
                            project(j, bc[:, q, :], C0 + 2 * q * P, 2).then_inc(m_cp, 1)
                        pe.wait_ge(m_yd, j * 2)
                        project(j, bb[:, :], B0, 2).then_inc(m_bp, 1)
                        pe.wait_ge(m_xpad, j * 4)
                        project(j, bx[:, :], X0, 2).then_inc(m_xp, 1)

                    def sums(n, sz_):
                        pe.wait_ge(m_tri, n + 1)
                        pe.wait_ge(m_dec, n)
                        pe.wait_ge(m_sz, sz_)
                        for q in range(2):
                            mm = pe.matmul(bz[:, q, :], lower[:, :],
                                           tri[:, 4 * q:4 * q + 4, :].rearrange("p h l -> p (h l)"),
                                           start=True, stop=True)
                        mm.then_inc(m_seg, 1)

                    def b_dot_c(j, c):
                        n = j * 2 + c
                        tk = slice(c * P, (c + 1) * P)
                        pe.wait_ge(m_b, j + 1)
                        pe.wait_ge(m_c, j * 2 + 2)
                        pe.wait_ge(m_w, n)
                        for h in range(NH):
                            r = slice((h % 2) * HD, (h % 2 + 1) * HD)
                            mm = pe.matmul(bc[:, h % 2, (h // 2) * P:(h // 2 + 1) * P], b_t[r, h // REP, tk],
                                           c_t[r, h // 2, tk], start=True, stop=True)
                        mm.then_inc(m_g, 1)
                        pe.wait_ge(m_x, j + 1)
                        pe.wait_ge(m_xpad, n * 2)
                        for g in range(NG):
                            mm = pe.transpose(bx[:, g * P:(g + 1) * P], x_t[:, g, tk], ident[:, :])
                        mm.then_inc(m_xt, 1)

                    def step(j, c, first, last):
                        n = j * 2 + c
                        if c and not last:
                            sums(n + 1, j * 2 + 2)
                        pe.wait_ge(m_w, n + 1)
                        pe.wait_ge(m_ti, n * 10 + 7)
                        pe.wait_ge(m_xpad, n * 2 + 2)
                        pe.wait_ge(m_yd, n)
                        for h in range(NH):
                            mm = pe.matmul(bb[:, (h // 2) * P:(h // 2 + 1) * P], xpad[:, h // REP, h % 2, :],
                                           wts[:, h, :], start=(h % 2 == 0), stop=(h % 2 == 1))
                        mm.then_inc(m_y, 1)
                        if c == 0:
                            sums(n + 1, j * 2 + 2)
                            b_dot_c(j, 1)
                        elif not last:
                            project_cbx(j + 1)
                            b_dot_c(j + 1, 0)
                        pe.wait_ge(m_yg, n + 1)
                        pe.wait_ge(m_pre, n)
                        for i in range(PAIRS):
                            mm = pe.matmul(b_out[:, 0:DM], yg[:, i, :], wout[:, i, :], start=(i == 0),
                                           stop=(i == PAIRS - 1))
                        mm.then_inc(m_out, 1)
                        pe.wait_ge(m_sqs, n + 1)
                        pe.wait_ge(m_ve, n)
                        pe.matmul(b_ss[:, 0:2], sqs[:, :], ones[:, :], start=True, stop=True).then_inc(m_ss, 1)
                        if c and not last:
                            project_z(j + 1)

                    pe.wait_ge(m_const, 3)
                    pe.wait_ge(s_const, 16 * 3)
                    project_z(0)
                    project_cbx(0)
                    b_dot_c(0, 0)
                    sums(0, 2)
                    over_pairs(pe, step)


def cross_attention(nc, a, scope, ident, x_tok, aw):
    NS = BATCH * KVH
    QW = AREP * AD
    MW = MT * P
    with ExitStack() as layer:
        sb, ps, sem = scope(layer)
        wo_hi = sb("wo_hi", [P, AH, DM], F32R)
        wo_lo = sb("wo_lo", [P, AH, DM], F32R)
        wo_raw = sb("wo_raw", [P, AREP, DM])

        with ExitStack() as part:
            sb, ps, sem = scope(part)
            x_cur, c_cur = aw.x_cur, aw.c_cur
            xT_hi = sb("xT_hi", [P, 2, KT, P], F32R)
            xT_lo = sb("xT_lo", [P, 2, KT, P], F32R)
            q_s = sb("q_s", [P, 2, AREP, AD])
            kv_s = sb("kv_s", [P, 2, 2, 2, AD])
            sqr = sb("sqr", [P, 2, AREP + 2, AD])
            ss = sb("ss", [P, AREP + 2])
            sse = sb("sse", [P, AREP + 2])
            rs = sb("rs", [P, KVH, AREP + 2])
            mh = sb("mh6", [P, AREP + 2])
            t1 = sb("t1", [P, 2, AREP, AD])
            t2 = sb("t2", [P, 2, AREP, AD])
            u1 = sb("u1", [P, AD])
            u2 = sb("u2", [P, AD])
            u3 = sb("u3", [P, AD])
            q_r = sb("q_r", [P, AREP, AD])
            k_r = sb("k_r", [P, 2, AD])
            qT_hi = sb("qT_hi", [P, KVH, QW], F32R)
            qT_lo = sb("qT_lo", [P, KVH, QW], F32R)
            kT_hi = sb("kT_hi", [P, KVH, MW], F32R)
            kT_lo = sb("kT_lo", [P, KVH, MW], F32R)
            v_hi = sb("v_hi", [P, KVH, 2, AD], F32R)
            v_lo = sb("v_lo", [P, KVH, 2, AD], F32R)
            mx = sb("mx", [P, AREP])
            nb = sb("nb", [P, AREP])
            prob = sb("prob", [P, 2, AREP, MW])
            den = sb("den", [P, AREP])
            rec = sb("rec", [P, AREP])
            pT_hi = sb("pT_hi", [P, MT, QW], F32R)
            pT_lo = sb("pT_lo", [P, MT, QW], F32R)
            oT_hi = sb("oT_hi", [P, QW], F32R)
            oT_lo = sb("oT_lo", [P, QW], F32R)
            pre = sb("pre2", [P, DM])
            st = sb("st2", [P, 6])
            mv = sb("mvx", [P, 2])
            ve = sb("vex", [P, 1])
            r1 = sb("r1x", [P, 1])
            b_s = ps("b_s", [P, 2, 512])
            b_p = ps("b_p", [P, 2, 512])
            b_o = ps("b_o", [P, 512])
            b_q = ps("b_q", [P, 512])
            b_kv = ps("b_kv", [P, 512])
            b_w = ps("b_w", [P, 512])

            names = ("a_const", "a_xcur", "a_ctx", "a_xt", "a_xhi", "a_xlo", "a_pj", "a_qs", "a_kvs", "a_sqr", "a_ss",
                     "a_sse", "a_rs", "a_t", "a_qr", "a_u", "a_kr", "a_vhi", "a_vlo", "a_qt", "a_qhi", "a_qlo",
                     "a_khi", "a_klo", "a_s", "a_mx", "a_nb", "a_exp", "a_rec", "a_prob", "a_pt", "a_phi", "a_plo",
                     "a_pv", "a_ohi", "a_olo", "a_wo", "a_pre", "a_st", "a_mv", "a_ve", "a_r1", "a_x2",
                     "w_o", "w_ohi", "w_olo")
            (a_const, a_xcur, a_ctx, a_xt, a_xhi, a_xlo, a_pj, a_qs, a_kvs, a_sqr, a_ss, a_sse, a_rs, a_t, a_qr,
             a_u, a_kr, a_vhi, a_vlo, a_qt, a_qhi, a_qlo, a_khi, a_klo, a_s, a_mx, a_nb, a_exp, a_rec, a_prob,
             a_pt, a_phi, a_plo, a_pv, a_ohi, a_olo, a_wo, a_pre, a_st, a_mv, a_ve, a_r1, a_x2,
             w_o, w_ohi, w_olo) = [
                sem(n) for n in names]

            def pe_x(pe, b, n):
                if not (isinstance(b, int) and b == 0):
                    pe.wait_ge(a_xcur, b)
                    pe.wait_ge(a_ctx, b * 16)
                if n is not None:
                    pe.wait_ge(a_plo, n - 1)
                for s, t in ((0, x_cur), (1, c_cur)):
                    for k in range(KT):
                        mm = pe.transpose(b_p[:, 0, (2 * s + k) * P:(2 * s + k + 1) * P], t[:, k * P:(k + 1) * P],
                                          ident[:, :])
                mm.then_inc(a_xt, 1)

            def pe_project(pe, b, g, m):
                pe.wait_ge(a_xlo, b + 1)
                if isinstance(m, int) and m in (1, 2):
                    pe.wait_ge(a_qs, m)
                    pe.wait_ge(a_kvs, m)
                elif not (isinstance(m, int) and m == 0):
                    pe.wait_ge(a_qlo, m - 1)
                    pe.wait_ge(a_klo, m - 1)
                for k in range(KT):
                    products(pe, b_q[:, :], (xT_hi[:, 0, k, :], xT_lo[:, 0, k, :]),
                             (aw.wq_hi[:, k, g, :], aw.wq_lo[:, k, g, :]), k == 0, k == KT - 1)
                for s in range(2):
                    for k in range(KT):
                        mm = products(pe, b_kv[:, s * 256:(s + 1) * 256], (xT_hi[:, s, k, :], xT_lo[:, s, k, :]),
                                      (aw.wkv_hi[:, s * KT + k, g, :], aw.wkv_lo[:, s * KT + k, g, :]), k == 0, k == KT - 1)
                mm.then_inc(a_pj, 1)

            def pe_turn_qk(pe, m):
                pe.wait_ge(a_qr, m + 1)
                pe.wait_ge(a_kr, m * 2 + 2)
                copied = min(max(m, 1) + 2, NS) if isinstance(m, int) else m + 2
                pe.wait_ge(a_qs, copied)
                pe.wait_ge(a_kvs, copied)
                for h in range(AREP):
                    pe.transpose(b_q[:, h * P:(h + 1) * P], q_r[:, h, :], ident[:, :])
                for s in range(2):
                    mm = pe.transpose(b_kv[:, s * P:(s + 1) * P], k_r[:, s, :], ident[:, :])
                mm.then_inc(a_qt, 1)

            def pe_scores(pe, g, n):
                pe.wait_ge(a_qlo, n + 1)
                pe.wait_ge(a_klo, n + 1)
                pe.wait_ge(a_exp, n * AREP)
                for h in range(AREP):
                    o = b_s[:, h // 2, (h % 2) * MW:(h % 2 + 1) * MW]
                    hs = slice(h * P, (h + 1) * P)
                    products(pe, o, (qT_hi[:, g, hs], qT_lo[:, g, hs]), (kT_hi[:, g, :], kT_lo[:, g, :]), True, False)
                    mm = pe.matmul(o, aw.ident[:, :], aw.mask[:, :], start=False, stop=True)
                    if h % 2:
                        mm.then_inc(a_s, 1)

            def pe_turn_p(pe, g, n, xt):
                pe.wait_ge(a_prob, n * AREP + AREP)
                pe.wait_ge(a_plo, n)
                if xt is not None:
                    pe.wait_ge(a_xlo, xt + 1)
                for t in range(MT):
                    for h in range(AREP):
                        mm = pe.transpose(b_p[:, t, h * P:(h + 1) * P], prob[:, g % 2, h, t * P:(t + 1) * P],
                                          ident[:, :])
                mm.then_inc(a_pt, 1)

            def pe_values(pe, g, n):
                pe.wait_ge(a_plo, n + 1)
                pe.wait_ge(a_vlo, n + 1)
                pe.wait_ge(a_olo, n)
                for t in range(MT):
                    mm = products(pe, b_o[:, :], (v_hi[:, g, 1 - t, :], v_lo[:, g, 1 - t, :]),
                                  (pT_hi[:, t, :], pT_lo[:, t, :]), t == 0, t == MT - 1)
                mm.then_inc(a_pv, 1)

            def pe_out(pe, b, g, n):
                if isinstance(n, int) and n < KVH:
                    pe.wait_ge(w_olo, g + 1)
                pe.wait_ge(a_olo, n + 1)
                if g == 0:
                    pe.wait_ge(a_pre, b)
                for h in range(AREP):
                    hs = slice(h * P, (h + 1) * P)
                    mm = products(pe, b_w[:, 0:DM], (oT_hi[:, hs], oT_lo[:, hs]),
                                  (wo_hi[:, g * AREP + h, :], wo_lo[:, g * AREP + h, :]),
                                  g == 0 and h == 0, g == KVH - 1 and h == AREP - 1)
                mm.then_inc(a_wo, 1)

            def pe_step(pe, b, g, first, last):
                n = b * KVH + g
                prev, prev2 = not (first and g == 0), not (first and g < 2)
                x_ahead = g == 1 and not last
                if x_ahead:
                    pe_x(pe, b + 1, n)
                if not (last and g == KVH - 1):
                    pe_turn_qk(pe, n + 1)
                pe_scores(pe, g, n)
                if prev2:
                    pe_out(pe, b if g >= 2 else b - 1, (g + 2) % KVH, n - 2)
                if prev:
                    pe_turn_p(pe, (g + 3) % KVH, n - 1, b + 1 if x_ahead else None)
                if not (last and g >= 1):
                    pe_project(pe, b if g == 0 else b + 1, (g + 3) % KVH, n + 3)
                if prev:
                    pe_values(pe, (g + 3) % KVH, n - 1)

            def act_x(act, b, m):
                act.wait_ge(a_xt, b + 1)
                act.wait_ge(a_pj, m)
                act.activation(xT_hi[:, :, :, :].rearrange("p s k t -> p (s k t)"), b_p[:, 0, :],
                               ACT.Copy).then_inc(a_xhi, 1)

            def act_copies(act, g, m):
                c = g % 2
                early = isinstance(m, int) and m < 2
                act.wait_ge(a_pj, m + 1)
                if not early:
                    act.wait_ge(a_t, (m - 1) * 3)
                act.activation(q_s[:, c, :, :].rearrange("p h d -> p (h d)"), b_q[:, :], ACT.Copy).then_inc(a_qs, 1)
                if not early:
                    act.wait_ge(a_kr, (m - 1) * 2)
                    act.wait_ge(a_vlo, m - 1)
                act.activation(kv_s[:, c, :, :, :].rearrange("p s c d -> p (s c d)"), b_kv[:, :],
                               ACT.Copy).then_inc(a_kvs, 1)
                act.wait_ge(a_qs, m + 1)
                if not early:
                    act.wait_ge(a_ss, m - 1)
                act.activation(sqr[:, c, 0:AREP, :], q_s[:, c, :, :], ACT.Square).then_inc(a_sqr, 1)
                act.wait_ge(a_kvs, m + 1)
                act.activation(sqr[:, c, AREP:AREP + 2, :], kv_s[:, c, :, 0, :], ACT.Square).then_inc(a_sqr, 1)

            def act_qk(act, g, m):
                act.wait_ge(a_qt, m + 1)
                act.activation(qT_hi[:, g, :], b_q[:, :], ACT.Copy).then_inc(a_qhi, 1)
                act.activation(kT_hi[:, g, :], b_kv[:, 0:MW], ACT.Copy).then_inc(a_khi, 1)

            def act_exp(act, g, n):
                if not (isinstance(n, int) and n < 2):
                    act.wait_ge(a_pt, n - 1)
                act.wait_ge(a_rec, n)
                for h in range(AREP):
                    if h % 2 == 0:
                        act.wait_ge(a_nb, n * 2 + (h // 2 + 1))
                    act.activation(prob[:, g % 2, h, :], b_s[:, h // 2, (h % 2) * MW:(h % 2 + 1) * MW], ACT.Exp,
                                   bias=nb[:, h:h + 1], scale=rs[:, g, h:h + 1],
                                   accum_out=den[:, h:h + 1]).then_inc(a_exp, 1)

            def act_p(act, n):
                act.wait_ge(a_pt, n + 1)
                act.wait_ge(a_pv, n)
                act.activation(pT_hi[:, :, :], b_p[:, :, :], ACT.Copy).then_inc(a_phi, 1)

            def act_o(act, n):
                act.wait_ge(a_pv, n + 1)
                act.wait_ge(a_wo, n)
                act.activation(oT_hi[:, :], b_o[:, :], ACT.Copy).then_inc(a_ohi, 1)

            def act_step(act, b, g, first, last):
                n = b * KVH + g
                if not (first and g < 2):
                    act_o(act, n - 2)
                if g == 1 and not last:
                    act_x(act, b + 1, n + 3)
                if not (last and g == KVH - 1):
                    act_qk(act, (g + 1) % KVH, n + 1)
                act_exp(act, g, n)
                if not (first and g == 0):
                    act_p(act, n - 1)
                if not (last and g >= 1):
                    act_copies(act, (g + 3) % KVH, n + 3)
                if first:
                    act.wait_ge(w_o, 16 * (g + 1))
                    act.activation(wo_hi[:, g * AREP:(g + 1) * AREP, :], wo_raw[:, :, :], ACT.Copy).then_inc(w_ohi, 1)

            def dve_x(dve, b):
                dve.wait_ge(a_xhi, b + 1)
                dve.tensor_tensor(xT_lo[:, :, :, :].rearrange("p s k t -> p (s k t)"), b_p[:, 0, :],
                                  xT_hi[:, :, :, :].rearrange("p s k t -> p (s k t)").bitcast(F32),
                                  ALU.subtract).then_inc(a_xlo, 1)

            def dve_rotate(dve, g, m):
                hd = AD // 2
                heads = lambda t: t[:, None, :].broadcast_to([P, AREP, AD])
                half = lambda t, o: t[:, None, o:o + hd].broadcast_to([P, AREP, hd])
                c = g % 2
                dve.wait_ge(a_qs, m + 1)
                if not (isinstance(m, int) and m < 2):
                    dve.wait_ge(a_qr, m - 1)
                dve.tensor_tensor(t2[:, c, :, 0:hd], q_s[:, c, :, hd:AD], half(aw.sq, 0), ALU.mult).then_inc(a_t, 1)
                dve.tensor_tensor(t2[:, c, :, hd:AD], q_s[:, c, :, 0:hd], half(aw.sq, hd), ALU.mult).then_inc(a_t, 1)
                dve.tensor_tensor(t1[:, c, :, :], q_s[:, c, :, :], heads(aw.cq), ALU.mult).then_inc(a_t, 1)

            def dve_squares(dve, g, m):
                c = g % 2
                dve.wait_ge(a_sqr, m * 2 + 2)
                dve.wait_ge(a_sse, m)
                dve.tensor_reduce(ss[:, :], sqr[:, c, :, :], AX_X, ALU.add).then_inc(a_ss, 1)

            def dve_v(dve, g, m):
                dve.wait_ge(a_kvs, m + 1)
                if not (isinstance(m, int) and m < KVH):
                    dve.wait_ge(a_pv, m - (KVH - 1))
                dve.tensor_copy(v_hi[:, g, :, :], kv_s[:, g % 2, :, 1, :]).then_inc(a_vhi, 1)

            def dve_k(dve, g, m):
                c = g % 2
                dve.wait_ge(a_rs, m + 1)
                dve.wait_ge(a_u, m * 4 + 4)
                dve.wait_ge(a_qt, m)
                dve.tensor_scalar(k_r[:, 1, :], u3[:, :], rs[:, g, AREP:AREP + 1], float(AD) ** 0.5, ALU.mult,
                                  ALU.mult).then_inc(a_kr, 1)
                dve.scalar_tensor_tensor(k_r[:, 0, :], kv_s[:, c, 1, 0, :], rs[:, g, AREP + 1:AREP + 2], aw.kw_c[:, :],
                                         ALU.mult, ALU.mult).then_inc(a_kr, 1)

            def dve_qk(dve, g, m):
                dve.wait_ge(a_qhi, m + 1)
                dve.tensor_tensor(qT_lo[:, g, :], b_q[:, :], qT_hi[:, g, :].bitcast(F32),
                                  ALU.subtract).then_inc(a_qlo, 1)
                dve.wait_ge(a_khi, m + 1)
                dve.tensor_tensor(kT_lo[:, g, :], b_kv[:, 0:MW], kT_hi[:, g, :].bitcast(F32),
                                  ALU.subtract).then_inc(a_klo, 1)

            def dve_max(dve, g, n):
                dve.wait_ge(a_exp, n * AREP)
                for q in range(2):
                    hs = slice(2 * q, 2 * q + 2)
                    dve.wait_ge(a_s, n * 2 + (q + 1))
                    dve.tensor_reduce(mx[:, hs], b_s[:, q, :].rearrange("p (h m) -> p h m", h=2), AX_X,
                                      ALU.max).then_inc(a_mx, 1)
                    dve.wait_ge(a_mx, n * 2 + (q + 1))
                    dve.scalar_tensor_tensor(nb[:, hs], mx[:, hs], -1.0, rs[:, g, hs], ALU.mult,
                                             ALU.mult).then_inc(a_nb, 1)

            def dve_tail(dve, b):
                dve.wait_ge(a_wo, b * KVH + KVH)
                dve.tensor_tensor(pre[:, None, :], b_w[:, None, 0:DM], x_tok[:, bass.ds(b, 1), :],
                                  ALU.add).then_inc(a_pre, 1)
                dve.wait_ge(a_pre, b + 1)
                dve.bn_stats(st[:, :], pre[:, :]).then_inc(a_st, 1)
                met(dve, a_const)
                dve.wait_ge(a_st, b + 1)
                dve.bn_aggr(mv[:, :], st[:, :]).then_inc(a_mv, 1)

            def dve_tail2(dve, b):
                dve.wait_ge(a_r1, b + 1)
                dve.wait_ge(a_mv, b + 1)
                dve.tensor_scalar(x_tok[:, bass.ds(b, 1), :], pre[:, None, :], mv[:, 0:1], r1[:, 0:1],
                                  ALU.subtract, ALU.mult).then_inc(a_x2, 1)

            def dve_step(dve, b, g, first, last):
                n = b * KVH + g
                ahead2 = not (last and g >= 2)
                if ahead2:
                    dve_rotate(dve, (g + 2) % KVH, n + 2)
                if g == 1 and not last:
                    dve_x(dve, b + 1)
                if not (first and g < 2):
                    dve_o(dve, n - 2)
                dve_max(dve, g, n)
                if not (last and g == KVH - 1):
                    dve_qk(dve, (g + 1) % KVH, n + 1)
                if ahead2:
                    dve_squares(dve, (g + 2) % KVH, n + 2)
                    dve_v(dve, (g + 2) % KVH, n + 2)
                dve_rec(dve, n)
                if not (first and g == 0):
                    dve_p(dve, n - 1)
                if g == 1 and not first:
                    dve_tail(dve, b - 1)
                if ahead2:
                    dve_k(dve, (g + 2) % KVH, n + 2)
                if g == 2 and not first:
                    dve_tail2(dve, b - 1)

            def dve_rec(dve, n):
                dve.wait_ge(a_exp, n * AREP + AREP)
                dve.wait_ge(a_prob, n * AREP)
                dve.reciprocal(rec[:, :], den[:, :]).then_inc(a_rec, 1)

            def dve_p(dve, n):
                dve.wait_ge(a_phi, n + 1)
                dve.tensor_tensor(pT_lo[:, :, :], b_p[:, :, :], pT_hi[:, :, :].bitcast(F32),
                                  ALU.subtract).then_inc(a_plo, 1)

            def dve_o(dve, n):
                dve.wait_ge(a_ohi, n + 1)
                dve.tensor_tensor(oT_lo[:, :], b_o[:, :], oT_hi[:, :].bitcast(F32),
                                  ALU.subtract).then_inc(a_olo, 1)

            turn = {}

            def pool_kv(pool, g, m):
                hd, c = AD // 2, g % 2
                pool.wait_ge(a_kvs, m + 1)
                pool.wait_ge(a_kr, m * 2)
                pool.tensor_tensor(u1[:, :], kv_s[:, c, 0, 0, :], aw.ck[:, :], ALU.mult).then_inc(a_u, 1)
                pool.tensor_tensor(u2[:, 0:hd], kv_s[:, c, 0, 0, hd:AD], aw.sk[:, 0:hd], ALU.mult).then_inc(a_u, 1)
                pool.tensor_tensor(u2[:, hd:AD], kv_s[:, c, 0, 0, 0:hd], aw.sk[:, hd:AD], ALU.mult).then_inc(a_u, 1)
                pool.wait_ge(a_u, m * 4 + 3)
                pool.tensor_tensor(u3[:, :], u1[:, :], u2[:, :], ALU.add).then_inc(a_u, 1)

            def pool_v(pool, g, m):
                pool.wait_ge(a_vhi, m + 1)
                pool.tensor_tensor(v_lo[:, g, :, :], kv_s[:, g % 2, :, 1, :], v_hi[:, g, :, :].bitcast(F32),
                                   ALU.subtract).then_inc(a_vlo, 1)

            def pool_roots(pool, g, m):
                pool_wait(pool, a_ss, m + 1, turn.get("ss"))
                pool.tensor_scalar(sse[:, :], ss[:, :], 1.0, AD * RMS_EPS, ALU.mult, ALU.add).then_inc(a_sse, 1)
                pool.wait_ge(a_sse, m + 1)
                pool.tensor_tensor(rs[:, g, :], sse[:, :], mh[:, :], ALU.pow).then_inc(a_rs, 1)

            def pool_q(pool, g, m):
                pool.wait_ge(a_t, m * 3 + 3)
                pool.wait_ge(a_qt, m)
                pool.tensor_tensor(q_r[:, :, :], t1[:, g % 2, :, :], t2[:, g % 2, :, :], ALU.add).then_inc(a_qr, 1)

            def pool_step(pool, b, g, first, last):
                n = b * KVH + g
                if g == 0 and not last:
                    pool_wait(pool, a_xt, b + 1, turn.get("xt"))
                    pool.tensor_copy(x_cur[:, None, :], x_tok[:, bass.ds(b + 1, 1), :]).then_inc(a_xcur, 1)
                if not (last and g >= 2):
                    pool_kv(pool, (g + 2) % KVH, n + 2)
                    pool_q(pool, (g + 2) % KVH, n + 2)
                    pool_roots(pool, (g + 2) % KVH, n + 2)
                    pool_v(pool, (g + 2) % KVH, n + 2)
                pool_wait(pool, a_rec, n + 1, turn.get("rec"))
                for h in range(AREP):
                    pool.tensor_scalar(prob[:, g % 2, h, :], prob[:, g % 2, h, :], rec[:, h:h + 1], 1.0, ALU.mult,
                                       ALU.mult).then_inc(a_prob, 1)
                if first:
                    pool.wait_ge(w_ohi, g + 1)
                    pool.tensor_tensor(wo_lo[:, g * AREP:(g + 1) * AREP, :], wo_raw[:, :, :],
                                       wo_hi[:, g * AREP:(g + 1) * AREP, :].bitcast(F32),
                                       ALU.subtract).then_inc(w_olo, 1)
                if g == 1 and not first:
                    pool_wait(pool, a_mv, b, turn.get("mv"))
                    pool.tensor_scalar(ve[:, :], mv[:, 1:2], 1.0, LN_EPS, ALU.mult, ALU.add).then_inc(a_ve, 1)
                    pool.wait_ge(a_ve, b)
                    pool.tensor_tensor(r1[:, :], ve[:, :], mh[:, 0:1], ALU.pow).then_inc(a_r1, 1)

            def over_batches(eng, step, tail):
                for g in range(KVH):
                    step(eng, 0, g, True, False)
                with eng.Fori(1, BATCH - 1) as b:
                    for g in range(KVH):
                        step(eng, b, g, False, False)
                step(eng, BATCH - 1, 0, False, True)
                tail(eng)

            N1, N2, N3 = NS - 3, NS - 2, NS - 1
            LAST = BATCH - 1

            def pe_tail(pe):
                pe_turn_qk(pe, N2)
                pe_scores(pe, 1, N1)
                pe_out(pe, LAST - 1, 3, N1 - 2)
                pe_turn_p(pe, 0, N1 - 1, None)
                pe_scores(pe, 2, N2)
                pe_values(pe, 0, N1 - 1)
                pe_turn_qk(pe, N3)
                pe_turn_p(pe, 1, N1, None)
                pe_out(pe, LAST, 0, N1 - 1)
                pe_scores(pe, 3, N3)
                pe_values(pe, 1, N1)
                pe_turn_p(pe, 2, N2, None)
                pe_out(pe, LAST, 1, N1)
                pe_values(pe, 2, N2)
                pe_turn_p(pe, 3, N3, None)
                pe_out(pe, LAST, 2, N2)
                pe_values(pe, 3, N3)
                pe_out(pe, LAST, 3, N3)

            def act_tail(act):
                act_o(act, N1 - 2)
                act_qk(act, 2, N2)
                act_exp(act, 1, N1)
                act_p(act, N1 - 1)
                act_exp(act, 2, N2)
                act_o(act, N1 - 1)
                act_qk(act, 3, N3)
                act_p(act, N1)
                act_exp(act, 3, N3)
                act_o(act, N1)
                act_p(act, N2)
                act_o(act, N2)
                act_p(act, N3)
                act_o(act, N3)

            def dve_tails(dve):
                dve_rotate(dve, 3, N3)
                dve_o(dve, N1 - 2)
                dve_max(dve, 1, N1)
                dve_qk(dve, 2, N2)
                dve_v(dve, 3, N3)
                dve_squares(dve, 3, N3)
                dve_rec(dve, N1)
                dve_p(dve, N1 - 1)
                dve_k(dve, 3, N3)
                dve_max(dve, 2, N2)
                dve_tail(dve, LAST - 1)
                dve_rec(dve, N2)
                dve_o(dve, N1 - 1)
                dve_qk(dve, 3, N3)
                dve_p(dve, N1)
                dve_max(dve, 3, N3)
                dve_tail2(dve, LAST - 1)
                dve_o(dve, N1)
                dve_rec(dve, N3)
                dve_p(dve, N2)
                dve_o(dve, N2)
                dve_p(dve, N3)
                dve_o(dve, N3)
                dve_tail(dve, LAST)
                dve_tail2(dve, LAST)

            def pool_tail(pool):
                for g in range(1, KVH):
                    pool_step(pool, LAST, g, False, True)

            with nc.Block() as block:
                @block.sync
                def _(sp):
                    def context(b):
                        sp.wait_ge(a_xt, b)
                        sp.dma_start(c_cur[:, None, :], a["ctx"][bass.ds(b, 1)].rearrange("b s d -> s b d")
                                     ).then_inc(a_ctx, 16)

                    def out_weights(g):
                        sp.dma_start(wo_raw[:, :, :], a["wo"].rearrange("(h p) n -> p h n", p=P)
                                     [:, g * AREP:(g + 1) * AREP, :]).then_inc(w_o, 16)

                    out_weights(0)
                    context(1)
                    for g in range(1, KVH):
                        sp.wait_ge(w_olo, g)
                        out_weights(g)
                    with sp.Fori(2, BATCH) as b:
                        context(b)

                @block.tensor
                def _(pe):
                    pe_x(pe, 0, None)
                    pe_project(pe, 0, 0, 0)
                    pe_project(pe, 0, 1, 1)
                    pe_project(pe, 0, 2, 2)
                    pe_turn_qk(pe, 0)
                    over_batches(pe, pe_step, pe_tail)

                @block.scalar
                def _(act):
                    act_x(act, 0, 0)
                    act_copies(act, 0, 0)
                    act_copies(act, 1, 1)
                    act_copies(act, 2, 2)
                    act_qk(act, 0, 0)
                    over_batches(act, act_step, act_tail)

                @block.vector
                def _(dve):
                    dve_x(dve, 0)
                    for m in range(2):
                        dve_rotate(dve, m, m)
                        dve_squares(dve, m, m)
                        dve_v(dve, m, m)
                    dve_k(dve, 0, 0)
                    dve_qk(dve, 0, 0)
                    dve_k(dve, 1, 1)
                    over_batches(dve, dve_step, dve_tails)

                @block.gpsimd
                def _(pool):
                    pool.memset(mh[:, :], -0.5).then_inc(a_const, 1)
                    pool.wait_ge(a_const, 1)
                    for name, first in (("ss", KVH + 3), ("rec", KVH + 1), ("xt", 2), ("mv", 1)):
                        turn[name] = counter(pool, f"attn_{name}_turn", first)
                    for m in range(2):
                        pool_kv(pool, m, m)
                        pool_q(pool, m, m)
                        pool_roots(pool, m, m)
                        pool_v(pool, m, m)
                    over_batches(pool, pool_step, pool_tail)
                    pool.wait_ge(a_mv, BATCH)
                    pool.tensor_scalar(ve[:, :], mv[:, 1:2], 1.0, LN_EPS, ALU.mult, ALU.add).then_inc(a_ve, 1)
                    pool.wait_ge(a_ve, BATCH)
                    pool.tensor_tensor(r1[:, :], ve[:, :], mh[:, 0:1], ALU.pow).then_inc(a_r1, 1)


def experts(nc, a, scope, ident, x_tok, wr, rank, s_router, out):
    NT = TOK // HALF
    with ExitStack() as layer:
        sb, ps, sem = scope(layer)
        x_hi = sb("x_hi", [P, KT, TOK], F32R)
        x_lo = sb("x_lo", [P, KT, TOK], F32R)
        comb = sb("comb", [P, BATCH, NE])
        gu_raw = [sb(f"gu_raw{i}", [P, 2, KT, FI]) for i in range(2)]
        dn_raw = [sb(f"dn_raw{i}", [P, IT, DM]) for i in range(2)]
        gu_hi = [sb(f"gu_hi{i}", [P, 2, KT, FI], F32R) for i in range(2)]
        gu_lo = [sb(f"gu_lo{i}", [P, 2, KT, FI], F32R) for i in range(2)]
        dn_hi = [sb(f"dn_hi{i}", [P, IT, DM], F32R) for i in range(2)]
        dn_lo = [sb(f"dn_lo{i}", [P, IT, DM], F32R) for i in range(2)]
        e_gu = [sem(f"e_gu{i}") for i in range(2)]
        e_dn = [sem(f"e_dn{i}") for i in range(2)]

        with ExitStack() as part:
            sb, ps, sem = scope(part)
            x_f = sb("x_f", [P, KT, TOK])
            logit = sb("logit", [P, BATCH, E])
            eneg = sb("eneg", [P, BATCH, E])
            e1 = sb("e1", [P, BATCH, E])
            sc = sb("sc", [P, BATCH, E])
            m1 = sb("m1", [P, BATCH])
            q1 = sb("q1", [P, BATCH, E])
            k1 = sb("k1", [P, BATCH])
            sel1 = sb("sel1", [P, BATCH, E])
            sc2 = sb("sc2", [P, BATCH, E])
            m2 = sb("m2", [P, BATCH])
            q2 = sb("q2", [P, BATCH, E])
            k2 = sb("k2", [P, BATCH])
            sel2 = sb("sel2", [P, BATCH, E])
            sel = sb("sel", [P, BATCH, E])
            tot = sb("tot", [P, BATCH])
            inv = sb("inv", [P, BATCH])
            picked = sb("picked", [P, BATCH, E])
            eq1 = sb("eq1", [P, BATCH, E])
            eq2 = sb("eq2", [P, BATCH, E])
            names = ("r_gh", "r_gl", "r_t", "r_f", "r_hi", "r_lo", "r_l", "r_c", "r_e", "r_v")
            r_gh, r_gl, r_t, r_f, r_hi, r_lo, r_l, r_c, r_e, r_v = [sem(n) for n in names]
            accm = sb("accm", [P, BATCH, DM])
            sg = sb("sg", [P, 2, HALF])
            hf = sb("hf", [P, 2, HALF])
            h_hi = sb("eh_hi", [P, NT, IT, HALF], F32R)
            h_lo = sb("eh_lo", [P, NT, IT, HALF], F32R)
            stats = sb("fstats", [P, BATCH, 6])
            mv = sb("fmv", [P, BATCH, 2])
            ve = sb("fve", [P, BATCH])
            rstd = sb("frstd", [P, BATCH])
            mh = sb("fmh", [P, BATCH])
            y = sb("y", [P, BATCH, DM])
            bg = [ps(f"bg{i}", [P, 512]) for i in range(2)]
            bu = [ps(f"bu{i}", [P, 512]) for i in range(2)]
            bd = [ps(f"bd{i}", [P, 512]) for i in range(4)]
            w_gh = [sem(f"w_gh{i}") for i in range(2)]
            w_gl = [sem(f"w_gl{i}") for i in range(2)]
            w_dh = [sem(f"w_dh{i}") for i in range(2)]
            w_dl = [sem(f"w_dl{i}") for i in range(2)]
            names = ("f_mh", "f_g", "f_sg", "f_h", "f_hhi", "f_hlo", "f_d", "f_acc", "f_st", "f_mv",
                     "f_ve", "f_r", "f_y", "f_out")
            (f_mh, f_g, f_sg, f_h, f_hhi, f_hlo, f_d, f_acc, f_st, f_mv, f_ve, f_r, f_y, f_out) = [
                sem(n) for n in names]
            GU, DN = NT * IT, BATCH

            with nc.Block() as block:
                @block.sync
                def _(sp):
                    for i in range(2):
                        sp.dma_start(gu_raw[i][:, :, :, :], a["gu"][i].rearrange("s (k p) n -> p s k n", p=P)
                                     ).then_inc(e_gu[i], 16)
                        sp.dma_start(dn_raw[i][:, :, :], a["dn"][i].rearrange("(i p) n -> p i n", p=P)
                                     ).then_inc(e_dn[i], 16)
                    with sp.Fori(1, NE // 2) as r:
                        for c in range(2):
                            sp.wait_ge(w_gl[c], r)
                            sp.dma_start(gu_raw[c][:, :, :, :].rearrange("p s k n -> p (s k) n"),
                                         a["gu"][bass.ds(r * 2 + c, 1)].rearrange("e s (k p) n -> p (e s k) n", p=P)
                                         ).then_inc(e_gu[c], 16)
                            sp.wait_ge(w_dl[c], r)
                            sp.dma_start(dn_raw[c][:, :, :],
                                         a["dn"][bass.ds(r * 2 + c, 1)].rearrange("e (i p) n -> p (e i) n", p=P)
                                         ).then_inc(e_dn[c], 16)
                    for b in range(BATCH):
                        sp.wait_ge(f_y, b + 1)
                        sp.dma_start(out[b], y[:, b, :]).then_inc(f_out, 16)
                    sp.wait_ge(f_out, 16 * BATCH)

                @block.gpsimd
                def _(pool):
                    pool.memset(mh[:, :], -0.5).then_inc(f_mh, 1)
                    def split(r, c):
                        pool.wait_ge(f_acc, (r * 2 + c) * DN)
                        split_gu(r, c)
                        split_dn(r, c)

                    def split_gu(r, c):
                        pool_wait(pool, e_gu[c], r * 16 + 16, gu_turn[c], 16)
                        gr, gh, gl = (t[:, :, :, :].rearrange("p s k n -> p (s k n)") for t in
                                      (gu_raw[c], gu_hi[c], gu_lo[c]))
                        pool.tensor_scalar(gh, gr, 1.0, 0.0, ALU.mult, ALU.add).then_inc(w_gh[c], 1)
                        pool.wait_ge(w_gh[c], r + c)
                        pool.tensor_tensor(gl, gr, gh.bitcast(F32), ALU.subtract).then_inc(w_gl[c], 1)

                    def split_dn(r, c):
                        pool_wait(pool, e_dn[c], r * 16 + 16, dn_turn[c], 16)
                        dr, dh, dl = (t[:, :, :].rearrange("p i n -> p (i n)") for t in
                                      (dn_raw[c], dn_hi[c], dn_lo[c]))
                        pool.tensor_scalar(dh, dr, 1.0, 0.0, ALU.mult, ALU.add).then_inc(w_dh[c], 1)
                        pool.wait_ge(w_dh[c], r + 1)
                        pool.tensor_tensor(dl, dr, dh.bitcast(F32), ALU.subtract).then_inc(w_dl[c], 1)

                    gu_turn = [counter(pool, f"gu_turn{c}", 32) for c in range(2)]
                    dn_turn = [counter(pool, f"dn_turn{c}", 32) for c in range(2)]
                    for q in range(4):
                        s = slice(q * 256, (q + 1) * 256)
                        pool.wait_ge(r_hi, q + 1)
                        pool.tensor_tensor(x_lo[:, :, s], x_f[:, :, s], x_hi[:, :, s].bitcast(F32),
                                           ALU.subtract).then_inc(r_lo, 1)
                    split_dn(0, 0)
                    split(0, 1)
                    with pool.Fori(1, NE // 2) as r:
                        for c in range(2):
                            split(r, c)
                    pool.wait_ge(f_mh, 1)
                    for th in range(2):
                        bs = slice(th * 4, th * 4 + 4)
                        pool.wait_ge(f_mv, th * 4 + 4)
                        pool.tensor_scalar(ve[:, bs], mv[:, bs, 1], 1.0, LN_EPS, ALU.mult, ALU.add).then_inc(f_ve, 1)
                        pool.wait_ge(f_ve, th + 1)
                        pool.tensor_tensor(rstd[:, bs], ve[:, bs], mh[:, bs], ALU.pow).then_inc(f_r, 1)

                @block.tensor
                def _(pe):
                    def gate_up(e, c, th, i):
                        step, slot = e * GU + (th * IT + i), (th * IT + i) % 2
                        s, w = slice(th * HALF, (th + 1) * HALF), slice(i * P, (i + 1) * P)
                        if not (isinstance(step, int) and step < 2):
                            pe.wait_ge(f_h, step - 1)
                        for dst, u in ((bg[slot], 0), (bu[slot], 1)):
                            for k in range(KT):
                                mm = products(pe, dst[:, :], (gu_hi[c][:, u, k, w], gu_lo[c][:, u, k, w]),
                                              (x_hi[:, k, s], x_lo[:, k, s]), k == 0, k == KT - 1)
                        mm.then_inc(f_g, 1)

                    def down(e, r, c, th):
                        if isinstance(e, int) and e == 0:
                            pe.wait_ge(r_c, 1)
                        pe.wait_ge(w_dl[c], r + 1)
                        pe.wait_ge(f_hlo, e * GU + (th + 1) * IT)
                        for t in range(4):
                            ts = slice(t * P, (t + 1) * P)
                            pe.wait_ge(f_acc, e * DN + (DN + 4 * (th - 1) + t + 1))
                            for i in range(IT):
                                mm = products(pe, bd[t][:, 0:DM], (h_hi[:, th, i, ts], h_lo[:, th, i, ts]),
                                              (dn_hi[c][:, i, :], dn_lo[c][:, i, :]), i == 0, i == IT - 1)
                            mm.then_inc(f_d, 1)

                    def pair(r, first):
                        for c in range(2):
                            e = r * 2 + c
                            for th in range(NT):
                                if th == 0:
                                    pe.wait_ge(w_gl[c], r + 1)
                                if first and c == 0:
                                    pe.wait_ge(r_lo, th * 2 + 2)
                                gate_up(e, c, th, 0)
                                gate_up(e, c, th, 1)
                                if th:
                                    down(e, r, c, 0)
                                elif c:
                                    down(e - 1, r, 0, 1)
                                elif not first:
                                    down(e - 1, r - 1, 1, 1)
                                for i in range(2, IT):
                                    gate_up(e, c, th, i)

                    for q in range(4):
                        for k in range(KT):
                            for b in range(2):
                                mm = pe.transpose(bd[q][:, k * 256 + b * P:k * 256 + (b + 1) * P],
                                                  x_tok[:, 2 * q + b, k * P:(k + 1) * P], ident[:, :])
                        mm.then_inc(r_t, 1)
                    pe.wait_ge(s_router, 32)
                    for b in range(BATCH):
                        pe.wait_ge(r_f, b // 2 + 1)
                        for k in range(KT):
                            mm = pe.matmul(bd[0][:, b * E:(b + 1) * E], x_f[:, k, b * P:(b + 1) * P], wr[:, k, :],
                                           start=(k == 0), stop=(k == KT - 1))
                    mm.then_inc(r_l, 1)
                    pair(0, True)
                    with pe.Fori(1, NE // 2) as r:
                        pair(r, False)
                    down(NE - 1, NE // 2 - 1, 1, 1)

                @block.scalar
                def _(act):
                    def expert(e, first):
                        for n in range(GU):
                            if not first or n >= 2:
                                act.wait_ge(f_h, e * GU + (n - 1))
                            act.wait_ge(f_g, e * GU + (n + 1))
                            act.activation(sg[:, n % 2, :], bg[n % 2][:, :], ACT.Silu).then_inc(f_sg, 1)
                            act.wait_ge(f_h, e * GU + (n + 1))
                            if not first:
                                act.wait_ge(f_d, e * DN - (4 if n < IT else 0))
                            act.activation(h_hi[:, n // IT, n % IT, :], hf[:, n % 2, :], ACT.Copy).then_inc(f_hhi, 1)

                    for q in range(4):
                        act.wait_ge(r_t, q + 1)
                        act.activation(x_f[:, :, q * 256:(q + 1) * 256], bd[q][:, :].rearrange("p (k t) -> p k t", k=KT),
                                       ACT.Copy).then_inc(r_f, 1)
                    act.wait_ge(e_gu[0], 16)
                    for u in range(2):
                        act.activation(gu_hi[0][:, u, :, :], gu_raw[0][:, u, :, :], ACT.Copy).then_inc(r_gh, 1)
                    act.wait_ge(r_c, 1)
                    act.activation(eneg[:, :, :], logit[:, :, :], ACT.Exp, scale=-1.0).then_inc(r_e, 1)
                    expert(0, True)
                    with act.Fori(1, NE) as e:
                        expert(e, False)

                @block.vector
                def _(dve):
                    def gated(e, n, first):
                        dve.wait_ge(f_sg, e * GU + (n + 1))
                        if not first or n >= 2:
                            dve.wait_ge(f_hlo, e * GU + (n - 1))
                        dve.tensor_tensor(hf[:, n % 2, :], sg[:, n % 2, :], bu[n % 2][:, :],
                                          ALU.mult).then_inc(f_h, 1)
                        dve.wait_ge(f_hhi, e * GU + (n + 1))
                        dve.tensor_tensor(h_lo[:, n // IT, n % IT, :], hf[:, n % 2, :],
                                          h_hi[:, n // IT, n % IT, :].bitcast(F32), ALU.subtract).then_inc(f_hlo, 1)

                    def add(e, th):
                        for t in range(4):
                            b = th * 4 + t
                            dve.wait_ge(f_d, e * DN + (b + 1))
                            dve.wait_ge(f_acc, e * DN + (b + 1))
                            dve.scalar_tensor_tensor(accm[:, b, :], bd[t][:, 0:DM], comb[:, b, bass.ds(e, 1)],
                                                     accm[:, b, :], ALU.mult, ALU.add).then_inc(f_acc, 1)

                    def expert(e, first):
                        for th in range(NT):
                            for i in range(IT):
                                if i == 2 and th:
                                    add(e, 0)
                                elif i == 2 and not first:
                                    add(e - 1, 1)
                                gated(e, th * IT + i, first)
                                if first and th == 0 and i == 1:
                                    best()
                                if first and th == 0 and i == 2:
                                    second()
                                if first and th == 0 and i == 3:
                                    shares()

                    count = [0]

                    def step(ins):
                        count[0] += 1
                        ins.then_inc(r_v, 1)
                        dve.wait_ge(r_v, count[0])

                    per_tok = lambda t: t[:, :, None].broadcast_to([P, BATCH, E])
                    ranks = rank[:, None, :].broadcast_to([P, BATCH, E])

                    def best():
                        dve.wait_ge(r_e, 1)
                        step(dve.tensor_scalar(e1[:, :, :], eneg[:, :, :], 1.0, None, ALU.add))
                        step(dve.reciprocal(sc[:, :, :], e1[:, :, :]))
                        step(dve.tensor_reduce(m1[:, :], sc[:, :, :], AX_X, ALU.max))
                        step(dve.tensor_tensor(eq1[:, :, :], sc[:, :, :], per_tok(m1), ALU.is_equal))
                        step(dve.tensor_tensor(q1[:, :, :], eq1[:, :, :], ranks, ALU.mult))
                        step(dve.tensor_reduce(k1[:, :], q1[:, :, :], AX_X, ALU.max))
                        step(dve.tensor_tensor(sel1[:, :, :], q1[:, :, :], per_tok(k1), ALU.is_equal))

                    def second():
                        step(dve.scalar_tensor_tensor(sc2[:, :, :], sel1[:, :, :], -2.0, sc[:, :, :], ALU.mult, ALU.add))
                        step(dve.tensor_reduce(m2[:, :], sc2[:, :, :], AX_X, ALU.max))
                        step(dve.tensor_tensor(eq2[:, :, :], sc2[:, :, :], per_tok(m2), ALU.is_equal))
                        step(dve.tensor_tensor(q2[:, :, :], eq2[:, :, :], ranks, ALU.mult))
                        step(dve.tensor_reduce(k2[:, :], q2[:, :, :], AX_X, ALU.max))
                        step(dve.tensor_tensor(sel2[:, :, :], q2[:, :, :], per_tok(k2), ALU.is_equal))

                    def shares():
                        step(dve.tensor_tensor(sel[:, :, :], sel1[:, :, :], sel2[:, :, :], ALU.add))
                        step(dve.tensor_tensor(tot[:, :], m1[:, :], m2[:, :], ALU.add))
                        step(dve.reciprocal(inv[:, :], tot[:, :]))
                        step(dve.tensor_tensor(picked[:, :, :], sel[:, :, :], sc[:, :, :], ALU.mult))
                        step(dve.tensor_tensor(comb[:, :, 0:E], picked[:, :, :], per_tok(inv), ALU.mult))
                        step(dve.memset(comb[:, :, E:NE], 1.0))

                    def norm_stats(b):
                        dve.wait_ge(f_acc, NE * DN + b + 1)
                        dve.bn_stats(stats[:, b, :], accm[:, b, :]).then_inc(f_st, 1)
                        dve.wait_ge(f_st, b + 1)
                        dve.bn_aggr(mv[:, b, :], stats[:, b, :]).then_inc(f_mv, 1)

                    def norm(th):
                        dve.wait_ge(f_r, th + 1)
                        for b in range(th * 4, th * 4 + 4):
                            dve.tensor_scalar(y[:, b, :], accm[:, b, :], mv[:, b, 0:1], rstd[:, b:b + 1],
                                              ALU.subtract, ALU.mult).then_inc(f_y, 1)

                    for q in range(4):
                        s = slice(q * 256, (q + 1) * 256)
                        dve.wait_ge(r_f, q + 1)
                        dve.tensor_copy(x_hi[:, :, s], x_f[:, :, s]).then_inc(r_hi, 1)
                    for u in range(2):
                        dve.wait_ge(r_gh, u + 1)
                        dve.tensor_tensor(gu_lo[0][:, u, :, :], gu_raw[0][:, u, :, :],
                                          gu_hi[0][:, u, :, :].bitcast(F32),
                                          ALU.subtract).then_inc(w_gl[0] if u else r_gl, 1)
                    dve.wait_ge(s_router, 32)
                    dve.wait_ge(r_l, 1)
                    dve.tensor_scalar(logit[:, :, :], bd[0][:, 0:BATCH * E].rearrange("p (b e) -> p b e", e=E), -87.0,
                                      None, ALU.max).then_inc(r_c, 1)
                    for b in range(BATCH):
                        dve.tensor_copy(accm[:, b, :], x_tok[:, b, :]).then_inc(f_acc, 1)
                    expert(0, True)
                    with dve.Fori(1, NE) as e:
                        expert(e, False)
                    for b in range(4):
                        norm_stats(b)
                    norm(0)
                    add(NE - 1, 1)
                    for b in range(4, BATCH):
                        norm_stats(b)
                    norm(1)



def _host_arrays(inputs):
    f = lambda name: np.asarray(inputs[name])
    at, xa, ff = "L0_attn_", "L0_xattn_", "L0_ffn_"
    col = lambda v, n: np.ascontiguousarray(v.reshape(n, P).T)
    w = f(at + "in_proj_w")
    z, xr, bm, cm, dtr = (w[s:e] for s, e in ((0, 512), (512, 640), (640, 768), (768, 1280), (1280, 1288)))
    twice = lambda m: np.concatenate([m[0:HD], m[0:HD], m[HD:P], m[HD:P]])
    win = np.concatenate([z, cm, twice(bm), twice(xr), dtr, z[0:P - NH]])
    rows = lambda v: np.broadcast_to(v, (P,) + v.shape)
    kw, qw = f(xa + "k_norm_w"), f(xa + "q_norm_w")
    turned = lambda v: np.concatenate([v[AD // 2:], v[:AD // 2]])
    inv_freq = np.float32(1) / np.float32(10000.0) ** (np.arange(0, AD, 2, dtype=np.float32) / np.float32(AD))
    emb = np.outer(np.arange(SEQ, dtype=np.float32), np.concatenate([inv_freq, inv_freq]))
    sign = np.concatenate([-np.ones(AD // 2), np.ones(AD // 2)]).astype(np.float32)
    mask = np.zeros((P, MT * P), np.float32)
    mask[:, P:] = np.where(np.arange(P)[None, :] > np.arange(P)[:, None], np.float32(-2.0 ** 100), np.float32(0))
    kv = lambda k, v: np.concatenate([f(xa + k).reshape(DM, KVH, AD), f(xa + v).reshape(DM, KVH, AD)],
                                     axis=2).reshape(DM, KVH * 2 * AD)
    return {
        "x": f("x"), "ctx": f("ctx_2048"),
        "ident": np.eye(P, dtype=np.float32),
        "upper": np.triu(np.ones((P, P), np.float32)),
        "lower": np.tril(np.ones((P, P), np.float32), -1),
        "ln_w": col(f(at + "ln_w"), KT), "ln_b": col(f(at + "ln_b"), KT),
        "fc1_b": col(f(at + "fc1_b"), IT1), "fc2_b": rows(f(at + "fc2_b")),
        "dt_bias": f(at + "dt_bias").reshape(NH, 1),
        "A_log": np.broadcast_to(f(at + "A_log"), (P, BATCH, NH)),
        "Dp": col(np.repeat(f(at + "Dp"), HD), PAIRS), "norm_w": col(f(at + "norm_w"), PAIRS),
        "winT": win.T, "fc1T": f(at + "fc1_w").T, "fc2T": f(at + "fc2_w").T, "woutT": f(at + "out_proj_w").T,
        "wq": f(xa + "wq"), "wkv": np.stack([kv("wk", "wv"), kv("wk_ctx", "wv_ctx")]), "wo": f(xa + "wo"),
        "cos": np.cos(emb), "sin": np.sin(emb) * sign,
        "qw": rows(qw), "qwr": rows(turned(qw)), "kw": rows(kw), "kwr": rows(turned(kw)), "mask": mask,
        "w_router": f(ff + "w_router").T,
        "rank": rows(np.arange(E, 0, -1).astype(np.float32)),
        "gu": np.stack([np.concatenate([f(ff + "wg"), f(ff + "sg")]).transpose(0, 2, 1),
                        np.concatenate([f(ff + "wu"), f(ff + "su")]).transpose(0, 2, 1)], axis=1),
        "dn": np.concatenate([f(ff + "wd"), f(ff + "sd")]).transpose(0, 2, 1),
    }


def kernel(**inputs):
    import concourse.bacc as bacc
    from concourse.bass_utils import run_bass_kernel_spmd

    nc = bacc.Bacc("TRN2", target_bir_lowering=False, num_devices=1)
    arrays, args = {}, {}
    for name, v in _host_arrays(inputs).items():
        v = np.ascontiguousarray(v)
        arrays[f"in_{name}"] = v
        args[name] = nc.dram_tensor(f"in_{name}", v.shape, mybir.dt.from_np(v.dtype), kind="ExternalInput").ap()
    out = nc.dram_tensor("out_y", (BATCH, SEQ, DM), F32, kind="ExternalOutput").ap()
    decoder_layer(nc, args, out)
    r = run_bass_kernel_spmd(nc, [arrays], core_ids=[0])
    return r.results[0]["out_y"]
```
